# Optimizing a Trainium2 kernel written in Bass

```python
import numpy as np
import jax
import jax.numpy as jnp

def _softmax(x, axis=-1):
    return jax.nn.softmax(x, axis=axis)

def _gelu(x):
    return jax.nn.gelu(x, approximate=True)

def _silu(x):
    return jax.nn.silu(x)

def _sigmoid(x):
    return jax.nn.sigmoid(x)

def _layernorm(x, axis=-1, eps=1e-05):
    m = jnp.mean(x, axis=axis, keepdims=True)
    v = jnp.var(x, axis=axis, keepdims=True)
    return (x - m) / jnp.sqrt(v + eps)

def _scatter_add(tgt, idx, src, axis=0):
    return tgt.at[idx].add(src)

def _segment_sum(src, seg, n):
    return jax.ops.segment_sum(src, seg, n)
kernel_name = 'mk_adaln_attn_ffn_d1_seqx_r4_381826'

def setup_inputs(seed: int=0):
    np.random.seed(seed)
    _w = jnp.asarray

    def _rec_inputs():
        import jax
        import jax.numpy as jnp
        _rk = jax.random.key(seed)
        x = 7.22e-05 + 1 * jax.random.normal(jax.random.fold_in(_rk, 1), (2, 1024, 256), jnp.float32)
        _lenS = 1024 - jax.random.randint(jax.random.fold_in(_rk, 7), (2,), 0, max(1, 1024 // 4) + 1, jnp.int32)
        _lenS2 = 1024 - jax.random.randint(jax.random.fold_in(_rk, 8), (2,), 0, max(1, 1024 // 4) + 1, jnp.int32)
        cond_64 = -0.104238 + 1.01173 * jax.random.normal(jax.random.fold_in(_rk, 11), (2, 64), jnp.float32)
        _validS = jnp.arange(1024)[None, :] < _lenS[:, None]
        _validS2 = jnp.arange(1024)[None, :] < _lenS2[:, None]
        _causal = jnp.tril(jnp.ones((1024, 1024), dtype=bool))
        mask_BxS_bf1 = jnp.ones((2, 1024), dtype=bool)
        return (x, cond_64, mask_BxS_bf1)
    x, cond_64, mask_BxS_bf1 = _rec_inputs()

    def _L0_cond_setup():
        import jax, jax.numpy as jnp
        import numpy as np
        B, S, H = (4, 512, 256)
        E = 8
        M = 128
        K = 2
        N_SHARED = 2
        SM = M * N_SHARED
        G = 64
        GE_TEMP = 1.0
        ALPHA = 0.001
        SEQ_AUX = True
        NORM_TOPK = True
        COS_TEMP = 0.78
        CONS_ALPHA = 0.01
        LEAKY_SLOPE = 0.01
        EPS_COS = 1e-08

        def _leaky(x):
            return jnp.where(x >= 0, x, LEAKY_SLOPE * x)

        def _moe_forward(hidden_states, g, wt, wg, w_gate, w_up, w_down, sw_gate, sw_up, sw_down):
            b, s, h = hidden_states.shape
            x = hidden_states.reshape(-1, h)
            T = x.shape[0]
            logits_h = x @ wt.T
            logits_g = g @ wg.T
            logits_g = jnp.repeat(logits_g, s, axis=0)
            logits = (logits_h + logits_g / GE_TEMP) / (1.0 + 1.0 / GE_TEMP)
            scores = jax.nn.softmax(logits, axis=-1)
            topk_w, topk_idx = jax.lax.top_k(scores, K)
            if K > 1 and NORM_TOPK:
                topk_w = topk_w / (topk_w.sum(-1, keepdims=True) + 1e-20)
            onehot = jax.nn.one_hot(topk_idx.reshape(b, s * K), E, dtype=jnp.float32)
            ce = onehot.sum(1) / (s * K / E)
            aux_loss = (ce * scores.reshape(b, s, E).mean(1)).sum(1).mean() * ALPHA
            gp = _leaky(jnp.einsum('th,ehm->etm', x, w_gate))
            up = jnp.einsum('th,ehm->etm', x, w_up)
            y_all = jnp.einsum('etm,emh->eth', gp * up, w_down)
            y_sel = y_all[topk_idx, jnp.arange(T)[:, None], :]
            y = (y_sel * topk_w[..., None]).sum(1).reshape(b, s, h)
            p = _leaky(hidden_states @ sw_gate) * (hidden_states @ sw_up) @ sw_down
            y = y + p
            num = jnp.sum(y * p, -1)
            den = jnp.maximum(jnp.linalg.norm(y, axis=-1), EPS_COS) * jnp.maximum(jnp.linalg.norm(p, axis=-1), EPS_COS)
            closs = CONS_ALPHA * jnp.mean(num / den / (1.0 + COS_TEMP))
            return (y, aux_loss + closs)
        key = jax.random.key(seed)
        ks = jax.random.split(key, 12)
        sh = 1.0 / np.sqrt(H)
        sm = 1.0 / np.sqrt(M)
        ssm = 1.0 / np.sqrt(SM)
        sg = 1.0 / np.sqrt(G)
        return {'hidden_states': jax.random.normal(ks[0], (B, S, H), jnp.float32), 'g': jax.random.normal(ks[1], (B, G), jnp.float32), 'wt': jax.random.uniform(ks[2], (E, H), jnp.float32, -sh, sh), 'wg': jax.random.uniform(ks[3], (E, G), jnp.float32, -sg, sg), 'w_gate': jax.random.uniform(ks[4], (E, H, M), jnp.float32, -sh, sh), 'w_up': jax.random.uniform(ks[5], (E, H, M), jnp.float32, -sh, sh), 'w_down': jax.random.uniform(ks[6], (E, M, H), jnp.float32, -sm, sm), 'sw_gate': jax.random.uniform(ks[7], (H, SM), jnp.float32, -sh, sh), 'sw_up': jax.random.uniform(ks[8], (H, SM), jnp.float32, -sh, sh), 'sw_down': jax.random.uniform(ks[9], (SM, H), jnp.float32, -ssm, ssm)}
    _L0_cond_all = _L0_cond_setup()
    _L0_cond_in = {k: v for k, v in _L0_cond_all.items() if k in ('wt', 'wg', 'w_gate', 'w_up', 'w_down', 'sw_gate', 'sw_up', 'sw_down')}
    del _L0_cond_all

    def _L0_attn_setup():
        import jax, jax.numpy as jnp
        import numpy as np
        D_MODEL = 256
        N_HEADS = 16
        HEAD_DIM = D_MODEL // N_HEADS
        MAX_LEN = 512
        BATCH = 2
        SEQ = 512
        key = jax.random.key(seed)
        ks = jax.random.split(key, 10)
        s = 1.0 / np.sqrt(D_MODEL)
        inp = {'x': jax.random.normal(ks[0], (BATCH, SEQ, D_MODEL), dtype=jnp.float32), 'Wq': jax.random.uniform(ks[1], (D_MODEL, D_MODEL), jnp.float32, -s, s), 'bq': jax.random.uniform(ks[2], (D_MODEL,), jnp.float32, -s, s), 'Wk': jax.random.uniform(ks[3], (D_MODEL, D_MODEL), jnp.float32, -s, s), 'bk': jax.random.uniform(ks[4], (D_MODEL,), jnp.float32, -s, s), 'Wv': jax.random.uniform(ks[5], (D_MODEL, D_MODEL), jnp.float32, -s, s), 'bv': jax.random.uniform(ks[6], (D_MODEL,), jnp.float32, -s, s), 'Wo': jax.random.uniform(ks[7], (D_MODEL, D_MODEL), jnp.float32, -s, s), 'bo': jax.random.uniform(ks[8], (D_MODEL,), jnp.float32, -s, s), 'rel_emb': jax.random.normal(ks[9], (MAX_LEN * 2 - 1, HEAD_DIM), dtype=jnp.float32)}
        return inp
    _L0_attn_all = _L0_attn_setup()
    _L0_attn_in = {k: v for k, v in _L0_attn_all.items() if k in ('Wq', 'bq', 'Wk', 'bk', 'Wv', 'bv', 'Wo', 'bo', 'rel_emb')}
    del _L0_attn_all

    def _L0_cond2_setup():
        import jax, jax.numpy as jnp
        import numpy as np
        DIM = 256
        HEADS = 16
        DIM_HEAD = 64
        SCALE = 8.0

        def ln(x, g, eps=1e-05):
            mean = x.mean(axis=-1, keepdims=True)
            var = ((x - mean) ** 2).mean(axis=-1, keepdims=True)
            return (x - mean) * jax.lax.rsqrt(var + eps) * g

        def l2norm(t):
            n = jnp.maximum(jnp.linalg.norm(t, axis=-1, keepdims=True), 1e-12)
            return t / n

        def rel_pos_bias(n, w0, b0, g0, w1, b1, g1, w2, b2, dtype):
            pos = jnp.arange(-n + 1, n, dtype=dtype)[:, None]
            h = jax.nn.silu(ln(pos @ w0 + b0, g0))
            h = jax.nn.silu(ln(h @ w1 + b1, g1))
            h = h @ w2 + b2
            i = jnp.arange(n)
            idx = i[:, None] - i[None, :] + n - 1
            bias = h[idx]
            return jnp.transpose(bias, (2, 0, 1))
        key = jax.random.key(seed)
        ks = jax.random.split(key, 16)
        b, n = (2, 512)
        inner = HEADS * DIM_HEAD
        s = 0.02
        return {'x': jax.random.normal(ks[0], (b, n, DIM), jnp.float32), 'mask': jnp.ones((b, n), dtype=bool), 'g_norm': jnp.ones((DIM,), jnp.float32), 'Wq': jax.random.normal(ks[1], (DIM, inner), jnp.float32) * s, 'Wkv': jax.random.normal(ks[2], (DIM, 2 * DIM_HEAD), jnp.float32) * s, 'q_scale': jnp.ones((DIM_HEAD,), jnp.float32), 'k_scale': jnp.ones((DIM_HEAD,), jnp.float32), 'null_kv': jax.random.normal(ks[3], (2, DIM_HEAD), jnp.float32), 'null_attn_bias': jax.random.normal(ks[4], (HEADS,), jnp.float32), 'w0': jax.random.normal(ks[5], (1, DIM), jnp.float32) * s, 'b0': jnp.zeros((DIM,), jnp.float32), 'g0': jnp.ones((DIM,), jnp.float32), 'w1': jax.random.normal(ks[6], (DIM, DIM), jnp.float32) * s, 'b1': jnp.zeros((DIM,), jnp.float32), 'g1': jnp.ones((DIM,), jnp.float32), 'w2': jax.random.normal(ks[7], (DIM, HEADS), jnp.float32) * s, 'b2': jnp.zeros((HEADS,), jnp.float32), 'Wout': jax.random.normal(ks[8], (inner, DIM), jnp.float32) * s, 'g_out': jnp.ones((DIM,), jnp.float32)}
    _L0_cond2_all = _L0_cond2_setup()
    _L0_cond2_in = {k: v for k, v in _L0_cond2_all.items() if k in ('g_norm', 'Wq', 'Wkv', 'q_scale', 'k_scale', 'null_attn_bias', 'w0', 'b0', 'g0', 'w1', 'b1', 'g1', 'w2', 'b2', 'Wout', 'g_out')}
    del _L0_cond2_all

    def _L0_ffn_setup():
        import jax, jax.numpy as jnp
        import numpy as np
        E = 8
        TOP_K = 2
        LN_EPS = 1e-05

        def _layernorm(x, g, b):
            mu = jnp.mean(x, axis=-1, keepdims=True)
            var = jnp.var(x, axis=-1, keepdims=True)
            return (x - mu) * jax.lax.rsqrt(var + LN_EPS) * g + b
        key = jax.random.key(seed)
        ks = jax.random.split(key, 4)
        B, T, H, HF = (4, 512, 256, 512)
        s_in = 1.0 / np.sqrt(H)
        s_hid = 1.0 / np.sqrt(HF)
        return {'x': jax.random.normal(ks[0], (B, T, H), dtype=jnp.float32), 'ln_g': jnp.ones((H,), dtype=jnp.float32), 'ln_b': jnp.zeros((H,), dtype=jnp.float32), 'rW': jax.random.normal(ks[1], (H, E), dtype=jnp.float32) * s_in, 'rb': jnp.zeros((E,), dtype=jnp.float32), 'W1': jax.random.normal(ks[2], (E, H, HF), dtype=jnp.float32) * s_in, 'b1': jnp.zeros((E, HF), dtype=jnp.float32), 'W2': jax.random.normal(ks[3], (E, HF, H), dtype=jnp.float32) * s_hid, 'b2': jnp.zeros((E, H), dtype=jnp.float32)}
    _L0_ffn_all = _L0_ffn_setup()
    _L0_ffn_in = {k: v for k, v in _L0_ffn_all.items() if k in ('ln_g', 'ln_b', 'rW', 'rb', 'W1', 'b1', 'W2', 'b2')}
    del _L0_ffn_all
    return {'x': x, 'cond_64': cond_64, 'mask_BxS_bf1': mask_BxS_bf1, 'L0_cond_wt': _L0_cond_in['wt'], 'L0_cond_wg': _L0_cond_in['wg'], 'L0_cond_w_gate': _L0_cond_in['w_gate'], 'L0_cond_w_up': _L0_cond_in['w_up'], 'L0_cond_w_down': _L0_cond_in['w_down'], 'L0_cond_sw_gate': _L0_cond_in['sw_gate'], 'L0_cond_sw_up': _L0_cond_in['sw_up'], 'L0_cond_sw_down': _L0_cond_in['sw_down'], 'L0_attn_Wq': _L0_attn_in['Wq'], 'L0_attn_bq': _L0_attn_in['bq'], 'L0_attn_Wk': _L0_attn_in['Wk'], 'L0_attn_bk': _L0_attn_in['bk'], 'L0_attn_Wv': _L0_attn_in['Wv'], 'L0_attn_bv': _L0_attn_in['bv'], 'L0_attn_Wo': _L0_attn_in['Wo'], 'L0_attn_bo': _L0_attn_in['bo'], 'L0_attn_rel_emb': _L0_attn_in['rel_emb'], 'L0_cond2_g_norm': _L0_cond2_in['g_norm'], 'L0_cond2_Wq': _L0_cond2_in['Wq'], 'L0_cond2_Wkv': _L0_cond2_in['Wkv'], 'L0_cond2_q_scale': _L0_cond2_in['q_scale'], 'L0_cond2_k_scale': _L0_cond2_in['k_scale'], 'L0_cond2_null_attn_bias': _L0_cond2_in['null_attn_bias'], 'L0_cond2_w0': _L0_cond2_in['w0'], 'L0_cond2_b0': _L0_cond2_in['b0'], 'L0_cond2_g0': _L0_cond2_in['g0'], 'L0_cond2_w1': _L0_cond2_in['w1'], 'L0_cond2_b1': _L0_cond2_in['b1'], 'L0_cond2_g1': _L0_cond2_in['g1'], 'L0_cond2_w2': _L0_cond2_in['w2'], 'L0_cond2_b2': _L0_cond2_in['b2'], 'L0_cond2_Wout': _L0_cond2_in['Wout'], 'L0_cond2_g_out': _L0_cond2_in['g_out'], 'L0_ffn_ln_g': _L0_ffn_in['ln_g'], 'L0_ffn_ln_b': _L0_ffn_in['ln_b'], 'L0_ffn_rW': _L0_ffn_in['rW'], 'L0_ffn_rb': _L0_ffn_in['rb'], 'L0_ffn_W1': _L0_ffn_in['W1'], 'L0_ffn_b1': _L0_ffn_in['b1'], 'L0_ffn_W2': _L0_ffn_in['W2'], 'L0_ffn_b2': _L0_ffn_in['b2']}

def reference(x, cond_64, mask_BxS_bf1, L0_cond_wt, L0_cond_wg, L0_cond_w_gate, L0_cond_w_up, L0_cond_w_down, L0_cond_sw_gate, L0_cond_sw_up, L0_cond_sw_down, L0_attn_Wq, L0_attn_bq, L0_attn_Wk, L0_attn_bk, L0_attn_Wv, L0_attn_bv, L0_attn_Wo, L0_attn_bo, L0_attn_rel_emb, L0_cond2_g_norm, L0_cond2_Wq, L0_cond2_Wkv, L0_cond2_q_scale, L0_cond2_k_scale, L0_cond2_null_attn_bias, L0_cond2_w0, L0_cond2_b0, L0_cond2_g0, L0_cond2_w1, L0_cond2_b1, L0_cond2_g1, L0_cond2_w2, L0_cond2_b2, L0_cond2_Wout, L0_cond2_g_out, L0_ffn_ln_g, L0_ffn_ln_b, L0_ffn_rW, L0_ffn_rb, L0_ffn_W1, L0_ffn_b1, L0_ffn_W2, L0_ffn_b2):
    import jax
    import jax.numpy as jnp

    def _L0_cond_ref(hidden_states, g, wt, wg, w_gate, w_up, w_down, sw_gate, sw_up, sw_down):
        import jax, jax.numpy as jnp
        import numpy as np
        B, S, H = (4, 512, 256)
        E = 8
        M = 128
        K = 2
        N_SHARED = 2
        SM = M * N_SHARED
        G = 64
        GE_TEMP = 1.0
        ALPHA = 0.001
        SEQ_AUX = True
        NORM_TOPK = True
        COS_TEMP = 0.78
        CONS_ALPHA = 0.01
        LEAKY_SLOPE = 0.01
        EPS_COS = 1e-08

        def _leaky(x):
            return jnp.where(x >= 0, x, LEAKY_SLOPE * x)

        def _moe_forward(hidden_states, g, wt, wg, w_gate, w_up, w_down, sw_gate, sw_up, sw_down):
            b, s, h = hidden_states.shape
            x = hidden_states.reshape(-1, h)
            T = x.shape[0]
            logits_h = x @ wt.T
            logits_g = g @ wg.T
            logits_g = jnp.repeat(logits_g, s, axis=0)
            logits = (logits_h + logits_g / GE_TEMP) / (1.0 + 1.0 / GE_TEMP)
            scores = jax.nn.softmax(logits, axis=-1)
            topk_w, topk_idx = jax.lax.top_k(scores, K)
            if K > 1 and NORM_TOPK:
                topk_w = topk_w / (topk_w.sum(-1, keepdims=True) + 1e-20)
            onehot = jax.nn.one_hot(topk_idx.reshape(b, s * K), E, dtype=jnp.float32)
            ce = onehot.sum(1) / (s * K / E)
            aux_loss = (ce * scores.reshape(b, s, E).mean(1)).sum(1).mean() * ALPHA
            gp = _leaky(jnp.einsum('th,ehm->etm', x, w_gate))
            up = jnp.einsum('th,ehm->etm', x, w_up)
            y_all = jnp.einsum('etm,emh->eth', gp * up, w_down)
            y_sel = y_all[topk_idx, jnp.arange(T)[:, None], :]
            y = (y_sel * topk_w[..., None]).sum(1).reshape(b, s, h)
            p = _leaky(hidden_states @ sw_gate) * (hidden_states @ sw_up) @ sw_down
            y = y + p
            num = jnp.sum(y * p, -1)
            den = jnp.maximum(jnp.linalg.norm(y, axis=-1), EPS_COS) * jnp.maximum(jnp.linalg.norm(p, axis=-1), EPS_COS)
            closs = CONS_ALPHA * jnp.mean(num / den / (1.0 + COS_TEMP))
            return (y, aux_loss + closs)
        y, _ = _moe_forward(hidden_states, g, wt, wg, w_gate, w_up, w_down, sw_gate, sw_up, sw_down)
        return y

    def _L0_attn_ref(x, Wq, bq, Wk, bk, Wv, bv, Wo, bo, rel_emb):
        import jax, jax.numpy as jnp
        import numpy as np
        D_MODEL = 256
        N_HEADS = 16
        HEAD_DIM = D_MODEL // N_HEADS
        MAX_LEN = 512
        BATCH = 2
        SEQ = 512
        B, L, _ = x.shape

        def lin(x, W, b):
            return jnp.einsum('bld,ed->ble', x, W) + b

        def split_heads(t):
            return t.reshape(B, L, N_HEADS, HEAD_DIM).transpose(0, 2, 1, 3)
        q = split_heads(lin(x, Wq, bq))
        k = split_heads(lin(x, Wk, bk))
        v = split_heads(lin(x, Wv, bv))
        r = jnp.arange(L)
        idx = r[None, :] - r[:, None] + (MAX_LEN - 1)
        rel = rel_emb[idx]
        qk = jnp.einsum('bhld,bhrd->bhlr', q, k) / np.sqrt(HEAD_DIM)
        qk = qk + jnp.einsum('bhld,lrd->bhlr', q, rel)
        att = jax.nn.softmax(qk, axis=-1)
        out = jnp.einsum('bhlr,bhrd->bhld', att, v)
        out = out.transpose(0, 2, 1, 3).reshape(B, L, D_MODEL)
        return lin(out, Wo, bo)

    def _L0_cond2_ref(x, mask, g_norm, Wq, Wkv, q_scale, k_scale, null_kv, null_attn_bias, w0, b0, g0, w1, b1, g1, w2, b2, Wout, g_out):
        import jax, jax.numpy as jnp
        import numpy as np
        DIM = 256
        HEADS = 16
        DIM_HEAD = 64
        SCALE = 8.0

        def ln(x, g, eps=1e-05):
            mean = x.mean(axis=-1, keepdims=True)
            var = ((x - mean) ** 2).mean(axis=-1, keepdims=True)
            return (x - mean) * jax.lax.rsqrt(var + eps) * g

        def l2norm(t):
            n = jnp.maximum(jnp.linalg.norm(t, axis=-1, keepdims=True), 1e-12)
            return t / n

        def rel_pos_bias(n, w0, b0, g0, w1, b1, g1, w2, b2, dtype):
            pos = jnp.arange(-n + 1, n, dtype=dtype)[:, None]
            h = jax.nn.silu(ln(pos @ w0 + b0, g0))
            h = jax.nn.silu(ln(h @ w1 + b1, g1))
            h = h @ w2 + b2
            i = jnp.arange(n)
            idx = i[:, None] - i[None, :] + n - 1
            bias = h[idx]
            return jnp.transpose(bias, (2, 0, 1))
        b, n, _ = x.shape
        xn = ln(x, g_norm)
        q = (xn @ Wq).reshape(b, n, HEADS, DIM_HEAD).transpose(0, 2, 1, 3)
        kv = xn @ Wkv
        k, v = (kv[..., :DIM_HEAD], kv[..., DIM_HEAD:])
        nk = jnp.broadcast_to(null_kv[0], (b, 1, DIM_HEAD))
        nv = jnp.broadcast_to(null_kv[1], (b, 1, DIM_HEAD))
        k = jnp.concatenate([nk, k], axis=1)
        v = jnp.concatenate([nv, v], axis=1)
        q = l2norm(q) * q_scale
        k = l2norm(k) * k_scale
        sim = jnp.einsum('bhid,bjd->bhij', q, k) * SCALE
        bias = rel_pos_bias(n, w0, b0, g0, w1, b1, g1, w2, b2, q.dtype)
        null_bias = jnp.broadcast_to(null_attn_bias[:, None, None], (HEADS, n, 1))
        attn_bias = jnp.concatenate([null_bias, bias], axis=-1)
        sim = sim + attn_bias
        neg = -jnp.finfo(sim.dtype).max
        causal = jnp.triu(jnp.ones((n, n + 1), dtype=bool), k=2)
        sim = jnp.where(causal, neg, sim)
        m = jnp.pad(mask, ((0, 0), (1, 0)), constant_values=True)[:, None, None, :]
        sim = jnp.where(m, sim, neg)
        attn = jax.nn.softmax(sim, axis=-1)
        out = jnp.einsum('bhij,bjd->bhid', attn, v)
        out = out.transpose(0, 2, 1, 3).reshape(b, n, HEADS * DIM_HEAD)
        return ln(out @ Wout, g_out)

    def _L0_ffn_ref(x, ln_g, ln_b, rW, rb, W1, b1, W2, b2):
        import jax, jax.numpy as jnp
        import numpy as np
        E = 8
        TOP_K = 2
        LN_EPS = 1e-05

        def _layernorm(x, g, b):
            mu = jnp.mean(x, axis=-1, keepdims=True)
            var = jnp.var(x, axis=-1, keepdims=True)
            return (x - mu) * jax.lax.rsqrt(var + LN_EPS) * g + b
        z = _layernorm(x, ln_g, ln_b)
        logits = jnp.einsum('bth,he->bte', z, rW) + rb
        probs = jax.nn.softmax(logits, axis=-1)
        topv, topi = jax.lax.top_k(probs, TOP_K)
        mask = jnp.sum(jax.nn.one_hot(topi, E, dtype=probs.dtype) * topv[..., None], axis=-2)
        denom = jnp.maximum(jnp.sum(mask, axis=-1, keepdims=True), 1e-08)
        w = mask / denom
        hid = jax.nn.gelu(jnp.einsum('bth,ehf->btef', z, W1) + b1, approximate=False)
        outs = jnp.einsum('btef,efh->bteh', hid, W2) + b2
        mixed = jnp.sum(outs * w[..., None], axis=2)
        return x + mixed
    x = x + _L0_attn_ref(_L0_cond_ref(x, cond_64, L0_cond_wt, L0_cond_wg, L0_cond_w_gate, L0_cond_w_up, L0_cond_w_down, L0_cond_sw_gate, L0_cond_sw_up, L0_cond_sw_down), L0_attn_Wq, L0_attn_bq, L0_attn_Wk, L0_attn_bk, L0_attn_Wv, L0_attn_bv, L0_attn_Wo, L0_attn_bo, L0_attn_rel_emb)
    x = x + _L0_ffn_ref(_L0_cond2_ref(x, mask_BxS_bf1, L0_cond2_g_norm, L0_cond2_Wq, L0_cond2_Wkv, L0_cond2_q_scale, L0_cond2_k_scale, cond_64, L0_cond2_null_attn_bias, L0_cond2_w0, L0_cond2_b0, L0_cond2_g0, L0_cond2_w1, L0_cond2_b1, L0_cond2_g1, L0_cond2_w2, L0_cond2_b2, L0_cond2_Wout, L0_cond2_g_out), L0_ffn_ln_g, L0_ffn_ln_b, L0_ffn_rW, L0_ffn_rb, L0_ffn_W1, L0_ffn_b1, L0_ffn_W2, L0_ffn_b2)
    return x

_drawn_inputs = setup_inputs


def setup_inputs(seed=0):
    import zlib

    import numpy as np

    out = dict(_drawn_inputs(seed))
    spreads = {'L0_cond2_g_norm': (1.0, 0.2),
     'L0_cond2_q_scale': (1.0, 0.2),
     'L0_cond2_k_scale': (1.0, 0.2),
     'L0_cond2_b0': (0.0, 0.1),
     'L0_cond2_g0': (1.0, 0.6),
     'L0_cond2_b1': (0.0, 0.269),
     'L0_cond2_g1': (1.0, 0.6),
     'L0_cond2_b2': (0.0, 0.1),
     'L0_cond2_g_out': (1.0, 0.2),
     'L0_ffn_ln_g': (1.0, 0.2),
     'L0_ffn_ln_b': (0.0, 0.1),
     'L0_ffn_rb': (0.0, 0.1),
     'L0_ffn_b1': (0.0, 0.1),
     'L0_ffn_b2': (0.0, 0.1)}
    factors = {'L0_cond_wt': 3.896,
     'L0_attn_Wq': 7.603,
     'L0_attn_bq': 8.0,
     'L0_attn_Wk': 8.0,
     'L0_attn_bk': 8.0,
     'L0_attn_rel_emb': 6.126}
    for name, (base, spread) in spreads.items():
        noise = np.random.default_rng([zlib.crc32(name.encode()), seed]).standard_normal(out[name].shape)
        drawn = base * np.exp(spread * noise) if base else spread * noise
        out[name] = jnp.asarray(drawn.astype(out[name].dtype))
    for name, factor in factors.items():
        out[name] = (out[name] * factor).astype(out[name].dtype)
    return out
```

```python
from contextlib import ExitStack

import concourse.bass as bass
from concourse import mybir

F32 = mybir.dt.float32
F16 = mybir.dt.float16
U32 = mybir.dt.uint32
U8 = mybir.dt.uint8
ALU = mybir.AluOpType
ACT = mybir.ActivationFunctionType
X = mybir.AxisListType.X

P = 128
B, S, H = 2, 1024, 256
T = B * S
TT = T // P
KC = H // P
E = 8
M = 128
NS = 2
GE = E + NS
F = 512
FC = F // P
TC = T // 512
HI, LO = 0, 1
PRODUCTS = ((HI, HI), (HI, LO), (LO, HI))


class Scope:

    def __init__(self, nc, stack, prefix=""):
        self.nc, self.stack, self.prefix = nc, stack, prefix

    def sb(self, name, shape, dt):
        return self.stack.enter_context(self.nc.sbuf_tensor(self.prefix + name, shape, dt))

    def banks(self, name, n, dt=F32):
        return self.stack.enter_context(self.nc.psum_tensor(self.prefix + name, [P, n, 2048 // (4 if dt == F32 else 2)], dt))

    def sem(self, name):
        sem = self.nc.alloc_semaphore(self.prefix + name)
        SEMAPHORES.append(sem)
        return sem


SEMAPHORES = []


def end_of_part(nc):
    nc.clear_and_free_semaphores(list(SEMAPHORES))
    SEMAPHORES.clear()
    nc.all_engine_barrier()


class Chain:

    def __init__(self, eng, sem):
        self.eng, self.sem, self.base, self.n = eng, sem, 0, 0

    def __call__(self, ins):
        self.n += 1
        ins.then_inc(self.sem, 1)
        self.eng.wait_ge(self.sem, self.base + self.n)


def part(i):
    return slice(i, i + 1)


def constants(nc, k):
    with ExitStack() as stack:
        s = Scope(nc, stack)
        blank = s.sem("blank")
        made = s.sem("constants_made")
        with nc.Block() as block:
            @block.gpsimd
            def _(pool):
                pool.memset(k.ident32[:], 0.0).then_inc(blank, 1)
                pool.memset(k.ones[:], 1.0).then_inc(made, 1)
                pool.iota(k.iota[:], [[1, E]], 0, 0, True).then_inc(made, 1)
                pool.wait_ge(blank, 1)
                pool.affine_select(out=k.ident32[:], in_=k.ident32[:], compare_op=ALU.not_equal, fill=1.0,
                                   base=0, pattern=[[-1, P]], channel_multiplier=1).then_inc(blank, 1)
                pool.wait_ge(blank, 2)
                pool.tensor_copy(k.ident16[:], k.ident32[:]).then_inc(made, 1)
                pool.wait_ge(made, 3)


def transpose_split(nc, k, src, name, tiles=TT):
    with ExitStack() as stack:
        s = Scope(nc, stack)
        ps = s.banks(name + "_ps", 2)
        turned = s.sem(name + "_turned")
        hi_done = s.sem(name + "_hi_done")
        lo_done = s.sem(name + "_lo_done")
        G = tiles // 2
        with nc.Block() as block:
            @block.tensor
            def _(pe):
                for g in range(G):
                    if g >= 2:
                        pe.wait_ge(lo_done, g - 1)
                    for kc in range(KC):
                        for a in range(2):
                            last = nc.tensor.transpose(ps[:, g % 2, (kc * 2 + a) * P:(kc * 2 + a + 1) * P],
                                                       src[:, 2 * g + a, kc * P:(kc + 1) * P], k.ident32[:])
                    last.then_inc(turned, 1)

            @block.scalar
            def _(act):
                for g in range(G):
                    act.wait_ge(turned, g + 1)
                    nc.scalar.copy(k.zT[:, HI, :, g * 2 * P:(g + 1) * 2 * P],
                                   ps[:, g % 2, :].rearrange("p (c t) -> p c t", c=KC)).then_inc(hi_done, 1)

            @block.vector
            def _(dve):
                for g in range(G):
                    dve.wait_ge(hi_done, g + 1)
                    nc.vector.tensor_tensor(k.zT[:, LO, :, g * 2 * P:(g + 1) * 2 * P],
                                            ps[:, g % 2, :].rearrange("p (c t) -> p c t", c=KC),
                                            k.zT[:, HI, :, g * 2 * P:(g + 1) * 2 * P],
                                            ALU.subtract).then_inc(lo_done, 1)


def split_weights(nc, jobs, name, width=4096):
    with ExitStack() as stack:
        s = Scope(nc, stack)
        stage = s.sb(name + "_stage", [P, 2, width], F32)
        loaded = [s.sem(f"{name}_loaded{i}") for i in range(2)]
        hi_done = s.sem(name + "_hi_done")
        lo_done = s.sem(name + "_lo_done")

        def staged(n):
            shape = jobs[n][1].shape
            p, rest = shape[0], shape[1:]
            size = 1
            for x in rest:
                size *= x
            flat = stage[0:p, n % 2, 0:size]
            if len(rest) == 2:
                flat = flat.rearrange("p (a b) -> p a b", a=rest[0])
            return flat

        with nc.Block() as block:
            @block.sync
            def _(sp):
                for n, (src, _, _) in enumerate(jobs):
                    if n >= 2:
                        sp.wait_ge(lo_done, n - 1)
                    sp.dma_start(staged(n), src).then_inc(loaded[n % 2], 16)

            @block.scalar
            def _(act):
                for n, (_, hi, _) in enumerate(jobs):
                    act.wait_ge(loaded[n % 2], 16 * (n // 2 + 1))
                    nc.scalar.copy(hi, staged(n)).then_inc(hi_done, 1)

            @block.vector
            def _(dve):
                for n, (_, hi, lo) in enumerate(jobs):
                    dve.wait_ge(loaded[n % 2], 16 * (n // 2 + 1))
                    dve.wait_ge(hi_done, n + 1)
                    nc.vector.tensor_tensor(lo, staged(n), hi, ALU.subtract).then_inc(lo_done, 1)


def routing(nc, k, name, wr, gate, rb, scale, finish, W):
    with ExitStack() as stack:
        s = Scope(nc, stack)
        ps = s.banks(name + "_ps", 2)
        L = s.sb(name + "_L", [P, TT, E], F32)
        pm = s.sb(name + "_pm", [P, TT, E], F32)
        mask2 = s.sb(name + "_mask2", [P, TT, E], F32)
        best = s.sb(name + "_best", [P, TT, 8], F32)
        idx = s.sb(name + "_idx", [P, TT, 8], U32)
        idxf = s.sb(name + "_idxf", [P, TT, 8], F32)
        col = s.sb(name + "_col", [P, 4, TT], F32)
        gsb = s.sb(name + "_g", [B, 64], F32)
        wsb = s.sb(name + "_w", [E, 64], F32)
        gT = s.sb(name + "_gT", [64, B, P], F32)
        wT = s.sb(name + "_wT", [64, E], F32)
        rbr = s.sb(name + "_rb", [1, E], F32)
        ones32 = s.sb(name + "_ones", [1, P], F32)
        loaded = s.sem(name + "_loaded")
        turned = s.sem(name + "_turned")
        ready = s.sem(name + "_rows_ready")
        logits = s.sem(name + "_logits")
        centred = s.sem(name + "_centred")
        exps = s.sem(name + "_exps")
        steps = s.sem(name + "_steps")
        with nc.Block() as block:
            @block.sync
            def _(sp):
                if gate:
                    sp.dma_start(gsb[:], gate[0]).then_inc(loaded, 16)
                    sp.dma_start(wsb[:], gate[1]).then_inc(loaded, 16)
                else:
                    sp.dma_start(rbr[:], rb.rearrange("(a e) -> a e", a=1)).then_inc(loaded, 16)
                    sp.wait_ge(loaded, 16)

            @block.tensor
            def _(pe):
                if gate:
                    pe.wait_ge(loaded, 32)
                    nc.tensor.transpose(ps[0:64, 1, 0:B], gsb[:], k.ident32[0:B, 0:B])
                    nc.tensor.transpose(ps[0:64, 1, 16:16 + E], wsb[:], k.ident32[0:E, 0:E]).then_inc(turned, 1)
                else:
                    pe.wait_ge(loaded, 16)
                pe.wait_ge(ready, 1)
                for tt in range(TT):
                    out = ps[:, 0, tt * E:(tt + 1) * E]
                    n = 0
                    for a, b in PRODUCTS:
                        for kc in range(KC):
                            nc.tensor.matmul(out, k.zT[:, a, kc, tt * P:(tt + 1) * P], wr[:, b, kc, :],
                                             start=(n == 0), stop=False)
                            n += 1
                    if gate:
                        last = nc.tensor.matmul(out, gT[:, tt * P // S, :], wT[:], start=False, stop=True)
                    else:
                        last = nc.tensor.matmul(out, ones32[:], rbr[:], start=False, stop=True)
                last.then_inc(logits, 1)

            @block.scalar
            def _(act):
                act.wait_ge(centred, 1)
                nc.scalar.activation(L[:], L[:], ACT.Exp).then_inc(exps, 1)

            @block.vector
            def _(dve):
                link = Chain(dve, steps)
                if gate:
                    dve.wait_ge(turned, 1)
                    link(nc.vector.tensor_copy(gT[:], ps[0:64, 1, 0:B].unsqueeze(2).broadcast_to([64, B, P])))
                    nc.vector.tensor_copy(wT[:], ps[0:64, 1, 16:16 + E]).then_inc(ready, 1)
                else:
                    nc.vector.memset(ones32[:], 1.0).then_inc(ready, 1)
                wide = lambda c: col[:, c, :].unsqueeze(2).broadcast_to([P, TT, E])
                dve.wait_ge(logits, 1)
                link(nc.vector.tensor_scalar(L[:], ps[:, 0, 0:TT * E].rearrange("p (t e) -> p t e", e=E),
                                             scale, None, ALU.mult))
                link(nc.vector.tensor_reduce(col[:, 0, :], L[:], X, ALU.max))
                nc.vector.tensor_tensor(L[:], L[:], wide(0), ALU.subtract).then_inc(centred, 1)
                dve.wait_ge(exps, 1)
                link(nc.vector.tensor_reduce(col[:, 1, :], L[:], X, ALU.add))
                link(nc.vector.reciprocal(col[:, 2, :], col[:, 1, :]))
                link(nc.vector.tensor_tensor(L[:], L[:], wide(2), ALU.mult))
                for tt in range(TT):
                    nc.vector.max(best[:, tt, :], L[:, tt, :]).then_inc(steps, 1)
                link.n += TT
                dve.wait_ge(steps, link.n)
                for tt in range(TT):
                    nc.vector.max_index(idx[:, tt, :], best[:, tt, :], L[:, tt, :]).then_inc(steps, 1)
                link.n += TT
                dve.wait_ge(steps, link.n)
                link(nc.vector.tensor_copy(idxf[:], idx[:]))
                lane = k.iota[:].unsqueeze(1).broadcast_to([P, TT, E])
                link(nc.vector.tensor_tensor(pm[:], lane, idxf[:, :, 0:1].broadcast_to([P, TT, E]), ALU.is_equal))
                link(nc.vector.tensor_tensor(mask2[:], lane, idxf[:, :, 1:2].broadcast_to([P, TT, E]), ALU.is_equal))
                link(nc.vector.tensor_tensor(pm[:], pm[:], mask2[:], ALU.add))
                link(nc.vector.tensor_tensor(pm[:], pm[:], L[:], ALU.mult))
                link(nc.vector.tensor_reduce(col[:, 3, :], pm[:], X, ALU.add))
                link(nc.vector.tensor_scalar(col[:, 3, :], col[:, 3, :], finish[0], None, finish[1]))
                link(nc.vector.reciprocal(col[:, 2, :], col[:, 3, :]))
                link(nc.vector.tensor_tensor(W[:, 0:E, :].rearrange("p e t -> p t e"), pm[:], wide(2), ALU.mult))


def block_col(w, e, width):
    if isinstance(e, int):
        return w[:, e, :]
    return w.rearrange("p e n -> p (e n)")[:, bass.ds(e * width, width)]


def expert_weight(W, e, t):
    if isinstance(e, int):
        return W[:, e, t:t + 1]
    return W[:].rearrange("p e t -> p (e t)")[:, bass.ds(e * TT + t, 1)]


def load_rows(nc, src, rows, name):
    with ExitStack() as stack:
        loaded = Scope(nc, stack).sem(name + "_loaded")
        with nc.Block() as block:
            @block.sync
            def _(sp):
                sp.dma_start(rows[:], src.rearrange("b (t p) h -> p (b t) h", p=P)).then_inc(loaded, 16)
                sp.wait_ge(loaded, 16)


def store_rows(nc, rows, out):
    with ExitStack() as stack:
        stored = Scope(nc, stack).sem("rows_stored")
        with nc.Block() as block:
            @block.sync
            def _(sp):
                sp.dma_start(out.rearrange("b (t p) h -> p (b t) h", p=P), rows[:]).then_inc(stored, 16)
                sp.wait_ge(stored, 16)


def gated_router_weights(nc, k, wt, wr, W):
    with ExitStack() as stack:
        s = Scope(nc, stack)
        ps = s.banks("wt_ps", 1)
        rows = s.sb("wt_rows", [E, H], F32)
        loaded = s.sem("wt_loaded")
        turned = s.sem("wt_turned")
        hi_done = s.sem("wt_hi_done")
        with nc.Block() as block:
            @block.sync
            def _(sp):
                sp.dma_start(rows[:], wt).then_inc(loaded, 16)

            @block.tensor
            def _(pe):
                pe.wait_ge(loaded, 16)
                for kc in range(KC):
                    last = nc.tensor.transpose(ps[:, 0, kc * E:(kc + 1) * E], rows[:, kc * P:(kc + 1) * P],
                                               k.ident32[0:E, 0:E])
                last.then_inc(turned, 1)

            @block.vector
            def _(dve):
                nc.vector.memset(W[:, E:GE, :], 1.0)
                turned_w = ps[:, 0, 0:KC * E].rearrange("p (c e) -> p c e", c=KC)
                dve.wait_ge(turned, 1)
                nc.vector.tensor_copy(wr[:, HI, :, :], turned_w).then_inc(hi_done, 1)
                dve.wait_ge(hi_done, 1)
                nc.vector.tensor_tensor(wr[:, LO, :, :], turned_w, wr[:, HI, :, :], ALU.subtract)


def gated_experts(nc, k, wg, wu, wd, W, acc):
    with ExitStack() as stack:
        s = Scope(nc, stack)
        pg = s.banks("gate_ps", 2)
        pu = s.banks("up_ps", 2)
        py = s.banks("down_ps", 4)
        small = s.sb("gate_small", [P, 2, 512], F32)
        leaky = s.sb("gate_leaky", [P, 2, 512], F32)
        prod = s.sb("gate_prod", [P, 2, 512], F32)
        parts = s.sb("gate_parts", [P, 2, 2, 512], F16)
        hid_ready = s.sem("hid_ready")
        small_ready = s.sem("small_ready")
        leaky_ready = s.sem("leaky_ready")
        prod_ready = s.sem("prod_ready")
        hi_ready = s.sem("prod_hi_ready")
        lo_ready = s.sem("prod_lo_ready")
        down_ready = s.sem("down_ready")
        down_free = s.sem("down_banks_free")
        cleared = s.sem("acc_cleared")
        with nc.Block() as block:
            @block.tensor
            def _(pe):
                pe.sem_inc(down_ready, 8)

                def hidden(e, c):
                    n = TC * e + c
                    pe.wait_ge(prod_ready, n + 1)
                    for bank, w in ((pg, wg), (pu, wu)):
                        i = 0
                        for a, b in PRODUCTS:
                            for kc in range(KC):
                                last = nc.tensor.matmul(bank[:, c % 2, :], block_col(w[:, a, kc], e, M),
                                                        k.zT[:, b, kc, c * 512:(c + 1) * 512],
                                                        start=(i == 0), stop=(i == 5))
                                i += 1
                    last.then_inc(hid_ready, 1)

                def down(e, c):
                    n = TC * e + c
                    pe.wait_ge(hi_ready, n + 1)
                    pe.wait_ge(lo_ready, n + 3)
                    for j in range(4):
                        pe.wait_ge(down_free, 4 * n + j + 1)
                        for i, (a, b) in enumerate(PRODUCTS):
                            last = nc.tensor.matmul(py[:, j, 0:H], parts[:, c % 2, a, j * P:(j + 1) * P],
                                                    block_col(wd[:, b], e, H), start=(i == 0), stop=(i == 2))
                        last.then_inc(down_ready, 1)

                def block_of(e, following):
                    for c in range(TC):
                        if c + 1 < TC:
                            hidden(e, c + 1)
                        elif following is not None:
                            hidden(following, 0)
                        down(e, c)

                hidden(0, 0)
                with pe.Fori(0, GE - 1) as e:
                    block_of(e, e + 1)
                block_of(GE - 1, None)

            @block.scalar
            def _(act):
                with act.Fori(0, GE) as e:
                    for c in range(TC):
                        n = TC * e + c
                        act.wait_ge(hid_ready, n + 1)
                        act.wait_ge(prod_ready, n + 1)
                        nc.scalar.mul(small[:, c % 2, :], pg[:, c % 2, :], 0.01).then_inc(small_ready, 1)
                        act.wait_ge(prod_ready, n + 3)
                        act.wait_ge(down_ready, 4 * n + 4)
                        nc.scalar.copy(parts[:, c % 2, HI, :], prod[:, c % 2, :]).then_inc(hi_ready, 1)

            @block.gpsimd
            def _(pool):
                pool.sem_inc(lo_ready, 2)
                with pool.Fori(0, GE) as e:
                    for c in range(TC):
                        n = TC * e + c
                        pool.wait_ge(hi_ready, n + 1)
                        nc.gpsimd.tensor_tensor(parts[:, c % 2, LO, :], prod[:, c % 2, :],
                                                parts[:, c % 2, HI, :], ALU.subtract).then_inc(lo_ready, 1)

            @block.vector
            def _(dve):
                dve.sem_inc(prod_ready, 2)
                dve.sem_inc(down_free, 4)
                nc.vector.memset(acc[:], 0.0).then_inc(cleared, 1)
                dve.wait_ge(cleared, 1)

                def product(e, c):
                    n = TC * e + c
                    dve.wait_ge(small_ready, n + 1)
                    nc.vector.tensor_tensor(leaky[:, c % 2, :], pg[:, c % 2, :], small[:, c % 2, :],
                                            ALU.max).then_inc(leaky_ready, 1)
                    dve.wait_ge(leaky_ready, n + 1)
                    dve.wait_ge(lo_ready, n + 1)
                    nc.vector.tensor_tensor(prod[:, c % 2, :], pu[:, c % 2, :], leaky[:, c % 2, :],
                                            ALU.mult).then_inc(prod_ready, 1)

                def weigh(e, c):
                    n = TC * e + c
                    for j in range(4):
                        t = 4 * c + j
                        dve.wait_ge(down_ready, 8 + 4 * n + j + 1)
                        nc.vector.scalar_tensor_tensor(out=acc[:, t, :], in0=py[:, j, 0:H],
                                                       scalar=expert_weight(W, e, t), in1=acc[:, t, :],
                                                       op0=ALU.mult, op1=ALU.add).then_inc(down_free, 1)

                def block_of(e, following):
                    for c in range(TC):
                        if c + 1 < TC:
                            product(e, c + 1)
                        elif following is not None:
                            product(following, 0)
                        weigh(e, c)

                product(0, 0)
                with dve.Fori(0, GE - 1) as e:
                    block_of(e, e + 1)
                block_of(GE - 1, None)


NH = 16
D = H // NH
RT = S // P
LB = 32
QT = P // LB
REL = 1023
RK = 2 * 3 * D
AHEAD = 3
LP = S + AHEAD * LB
WIN = S + LB - 2
RW = 2 * S + AHEAD * LB
QPARTS = (HI, HI, LO)
FOUR = (0, 1, 3, 4)
KPARTS = (HI, LO, HI)


def turned_weights(nc, k, jobs, name):
    with ExitStack() as stack:
        s = Scope(nc, stack)
        ps = s.banks(name + "_wturn_ps", len(jobs))
        rows = s.sb(name + "_wturn_rows", [P, len(jobs), KC, H], F32)
        loaded = s.sem(name + "_wturn_loaded")
        turned = s.sem(name + "_wturn_turned")
        hi_done = s.sem(name + "_wturn_hi_done")
        with nc.Block() as block:
            @block.sync
            def _(sp):
                for n, (src, _) in enumerate(jobs):
                    sp.dma_start(rows[:, n], src.rearrange("(c p) d -> p c d", p=P)).then_inc(loaded, 16)

            @block.tensor
            def _(pe):
                pe.wait_ge(loaded, 16 * len(jobs))
                for n in range(len(jobs)):
                    for dc in range(KC):
                        for ec in range(KC):
                            last = nc.tensor.transpose(ps[:, n, dc * H + ec * P:dc * H + (ec + 1) * P],
                                                       rows[:, n, ec, dc * P:(dc + 1) * P], k.ident32[:])
                    last.then_inc(turned, 1)

            @block.scalar
            def _(act):
                for n, (_, w) in enumerate(jobs):
                    act.wait_ge(turned, n + 1)
                    nc.scalar.copy(w[:, HI], ps[:, n, :].rearrange("p (c e) -> p c e", c=KC)).then_inc(hi_done, 1)

            @block.vector
            def _(dve):
                for n, (_, w) in enumerate(jobs):
                    dve.wait_ge(hi_done, n + 1)
                    nc.vector.tensor_tensor(w[:, LO], ps[:, n, :].rearrange("p (c e) -> p c e", c=KC),
                                            w[:, HI], ALU.subtract)


def queries_keys(nc, k, jobs):
    with ExitStack() as stack:
        s = Scope(nc, stack)
        ps = s.banks("proj_ps", 4)
        bias = s.sb("proj_bias", [P, 2, KC], F32)
        full = s.sb("proj_full", [P, 4, 512], F32)
        parts = s.sb("proj_parts", [P, 2, 2, KC, T], F16)
        loaded = s.sem("proj_loaded")
        scaled = s.sem("proj_bias_scaled")
        ready = s.sem("proj_ready")
        full_ready = s.sem("proj_full_ready")
        hi_done = s.sem("proj_hi_done")
        lo_done = s.sem("proj_lo_done")
        stored = s.sem("proj_stored")
        steps = [(j, ec, c) for j in range(2) for ec in range(KC) for c in range(TC)]
        with nc.Block() as block:
            @block.sync
            def _(sp):
                for j, (_, b, _, _) in enumerate(jobs):
                    sp.dma_start(bias[:, j, :], b.rearrange("(c p) -> p c", p=P),
                                 allow_slow_non_contiguous=True).then_inc(loaded, 16)
                for j, (_, _, _, dst) in enumerate(jobs):
                    sp.wait_ge(lo_done, 8 * (j + 1))
                    sp.wait_ge(hi_done, 8 * (j + 1))
                    for hl in range(2):
                        sp.dma_start(dst[hl].rearrange("(c p) t -> p c t", p=P), parts[:, j, hl]).then_inc(stored, 16)
                sp.wait_ge(stored, 64)

            @block.tensor
            def _(pe):
                for n, (j, ec, c) in enumerate(steps):
                    if n >= 4:
                        pe.wait_ge(full_ready, n - 3)
                    i = 0
                    for a, b in PRODUCTS:
                        for kc in range(KC):
                            last = nc.tensor.matmul(ps[:, n % 4, :], jobs[j][0][:, a, kc, ec * P:(ec + 1) * P],
                                                    k.zT[:, b, kc, c * 512:(c + 1) * 512],
                                                    start=(i == 0), stop=(i == 5))
                            i += 1
                    last.then_inc(ready, 1)

            @block.scalar
            def _(act):
                act.wait_ge(scaled, 2)
                for n, (j, ec, c) in enumerate(steps):
                    act.wait_ge(ready, n + 1)
                    if n >= 4:
                        act.wait_ge(lo_done, n - 3)
                    nc.scalar.activation(full[:, n % 4, :], ps[:, n % 4, :], ACT.Identity,
                                         bias=bias[:, j, ec:ec + 1], scale=jobs[j][2]).then_inc(full_ready, 1)

            @block.vector
            def _(dve):
                dve.wait_ge(loaded, 32)
                for j in range(2):
                    nc.vector.tensor_scalar(bias[:, j, :], bias[:, j, :], jobs[j][2], None, ALU.mult).then_inc(scaled, 1)
                for n, (j, ec, c) in enumerate(steps):
                    dve.wait_ge(full_ready, n + 1)
                    cols = slice(c * 512, (c + 1) * 512)
                    nc.vector.tensor_copy(parts[:, j, HI, ec, cols], full[:, n % 4, :]).then_inc(hi_done, 1)
                    dve.wait_ge(hi_done, n + 1)
                    nc.vector.tensor_tensor(parts[:, j, LO, ec, cols], full[:, n % 4, :],
                                            parts[:, j, HI, ec, cols], ALU.subtract).then_inc(lo_done, 1)


def values(nc, k, wv, bv, V):
    with ExitStack() as stack:
        s = Scope(nc, stack)
        ps = s.banks("v_ps", 4)
        bias = s.sb("v_bias", [P, H], F32)
        full = s.sb("v_full", [P, 4, H], F32)
        loaded = s.sem("v_loaded")
        ready = s.sem("v_ready")
        full_ready = s.sem("v_full_ready")
        hi_done = s.sem("v_hi_done")
        lo_done = s.sem("v_lo_done")
        heads = lambda t: t.rearrange("p (h d) -> p h d", d=D)
        with nc.Block() as block:
            @block.sync
            def _(sp):
                sp.dma_start(bias[:], bv.rearrange("(a d) -> a d", a=1).broadcast_to([P, H])).then_inc(loaded, 16)

            @block.gpsimd
            def _(pool):
                pool.memset(V[:, :, :, 2 * D:2 * D + 1], 1.0)

            @block.tensor
            def _(pe):
                for t in range(TT):
                    if t >= 4:
                        pe.wait_ge(full_ready, t - 3)
                    i = 0
                    for a, b in PRODUCTS:
                        for kc in range(KC):
                            last = nc.tensor.matmul(ps[:, t % 4, 0:H], k.zT[:, a, kc, t * P:(t + 1) * P],
                                                    wv[:, b, kc, :], start=(i == 0), stop=(i == 5))
                            i += 1
                    last.then_inc(ready, 1)

            @block.scalar
            def _(act):
                for t in range(TT):
                    act.wait_ge(full_ready, t + 1)
                    nc.scalar.copy(V[:, t, :, 0:D], heads(full[:, t % 4, :])).then_inc(hi_done, 1)

            @block.vector
            def _(dve):
                dve.wait_ge(loaded, 16)
                for t in range(TT):
                    dve.wait_ge(ready, t + 1)
                    if t >= 4:
                        dve.wait_ge(lo_done, t - 3)
                    nc.vector.tensor_tensor(full[:, t % 4, :], ps[:, t % 4, 0:H], bias[:], ALU.add).then_inc(full_ready, 1)
                    dve.wait_ge(hi_done, t + 1)
                    dve.wait_ge(full_ready, t + 1)
                    nc.vector.tensor_tensor(V[:, t, :, D:2 * D], heads(full[:, t % 4, :]), V[:, t, :, 0:D],
                                            ALU.subtract).then_inc(lo_done, 1)


def relative_rows(nc, k, rel, RS, half, quarter):
    with ExitStack() as stack:
        s = Scope(nc, stack)
        ps = s.banks("rel_ps", 2)
        rows = s.sb("rel_rows", [P, 8, D], F32)
        full = s.sb("rel_full", [D, 1536], F32)
        parts = s.sb("rel_parts", [D, 2, 1536], F16)
        loaded = s.sem("rel_loaded")
        turned = s.sem("rel_turned")
        cleared = s.sem("rel_cleared")
        steps = s.sem("rel_steps")
        placed = s.sem("rel_placed")
        masks = s.sem("rel_masks")
        WRAP = 512
        with nc.Block() as block:
            @block.sync
            def _(sp):
                sp.dma_start(rows[:, 0:7, :], rel[0:7 * P, :].rearrange("(c p) d -> p c d", p=P)).then_inc(loaded, 16)
                sp.dma_start(rows[0:P - 1, 7, :], rel[7 * P:REL, :]).then_inc(loaded, 16)
                sp.wait_ge(steps, 4)
                sp.wait_ge(cleared, 2)
                for l in range(2):
                    for i, hl in enumerate(KPARTS):
                        r = (3 * l + i) * D
                        x = AHEAD * LB + 1 + l
                        sp.dma_start(RS[r:r + D, 0, x:x + WRAP], parts[:, hl, REL - WRAP:REL]).then_inc(placed, 16)
                        sp.dma_start(RS[r:r + D, 0, x + WRAP:RW], parts[:, hl, 0:2 * S - 1 - l - WRAP])\
                            .then_inc(placed, 16)
                for l, group in enumerate(FOUR):
                    r = group * D
                    x = AHEAD * LB + 1 + l
                    sp.dma_start(RS[r:r + D, 1, x:x + WRAP], parts[:, HI, REL - WRAP:REL]).then_inc(placed, 16)
                    sp.dma_start(RS[r:r + D, 1, x + WRAP:RW], parts[:, HI, 0:2 * S - 1 - l - WRAP]).then_inc(placed, 16)
                sp.wait_ge(placed, 20 * 16)

            @block.gpsimd
            def _(pool):
                pool.memset(RS[:], 0.0).then_inc(cleared, 1)
                pool.wait_ge(cleared, 1)
                pool.memset(RS[RK:RK + 1, 0, :], 1.0).then_inc(cleared, 1)
                pool.memset(quarter[:], 1.0).then_inc(masks, 1)
                pool.wait_ge(masks, 1)
                for l, group in enumerate(FOUR):
                    rows = quarter[:, l:l + 1]
                    pool.affine_select(out=rows, in_=rows, compare_op=ALU.is_ge, fill=0.0,
                                       base=-group * D, pattern=[[0, 1]], channel_multiplier=1).then_inc(masks, 1)
                    pool.wait_ge(masks, 2 * l + 2)
                    pool.affine_select(out=rows, in_=rows, compare_op=ALU.is_ge, fill=0.0,
                                       base=group * D + D - 1, pattern=[[0, 1]], channel_multiplier=-1).then_inc(masks, 1)
                    pool.wait_ge(masks, 2 * l + 3)
                pool.memset(half[:], 1.0).then_inc(masks, 1)
                pool.wait_ge(masks, 10)
                pool.affine_select(out=half[:, 0:1], in_=half[:, 0:1], compare_op=ALU.is_ge, fill=0.0,
                                   base=3 * D - 1, pattern=[[0, 1]], channel_multiplier=-1).then_inc(masks, 1)
                pool.affine_select(out=half[:, 1:2], in_=half[:, 1:2], compare_op=ALU.is_ge, fill=0.0,
                                   base=-3 * D, pattern=[[0, 1]], channel_multiplier=1).then_inc(masks, 1)

            @block.tensor
            def _(pe):
                pe.wait_ge(loaded, 32)
                for c in range(8):
                    n = P if c < 7 else P - 1
                    last = nc.tensor.transpose(ps[0:D, c // 4, (c % 4) * P:(c % 4) * P + n], rows[0:n, c, :],
                                               k.ident32[0:n, 0:n])
                last.then_inc(turned, 1)

            @block.vector
            def _(dve):
                link = Chain(dve, steps)
                dve.wait_ge(turned, 1)
                link(nc.vector.tensor_copy(full[:, 0:REL], ps[0:D].rearrange("p a b -> p (a b)")[:, 0:REL]))
                link(nc.vector.tensor_copy(full[:, REL:1536], full[:, REL - 1:REL].broadcast_to([D, 1536 - REL])))
                link(nc.vector.tensor_copy(parts[:, HI, :], full[:]))
                link(nc.vector.tensor_tensor(parts[:, LO, :], full[:], parts[:, HI, :], ALU.subtract))


def relative_operands(nc, b, qd, kd, Q, KT):
    with ExitStack() as stack:
        s = Scope(nc, stack, f"b{b}_")
        loaded = s.sem("ops_loaded")
        cleared = s.sem("ops_cleared")
        tok = slice(b * S, (b + 1) * S)
        with nc.Block() as block:
            @block.sync
            def _(sp):
                for half in range(2):
                    for i in range(3):
                        r = (3 * half + i) * D
                        sp.dma_start(Q[r:r + D, :, 0:S], qd[QPARTS[i], :, tok].rearrange("(h d) t -> d h t", d=D))\
                            .then_inc(loaded, 16)
                        sp.dma_start(KT[r:r + D, :, :], kd[KPARTS[i], :, tok].rearrange(
                            "(g two d) t -> two d g t", two=2, d=D)[half]).then_inc(loaded, 16)
                sp.wait_ge(loaded, 12 * 16)

            @block.gpsimd
            def _(pool):
                pool.memset(Q[:, :, S:LP], 0.0).then_inc(cleared, 1)
                pool.wait_ge(cleared, 1)


def relative_attention(nc, k, b, Q, KT, RS, half, quarter, V, o):
    with ExitStack() as stack:
        s = Scope(nc, stack, f"b{b}_")
        pm = s.banks("max_ps", 2)
        pz = s.banks("score_ps", 2)
        pv = s.banks("pv_ps", 2)
        pt = s.banks("turn_ps", 1)
        top = s.sb("top", [P, 2, 512], F32)
        peak = s.sb("peak", [P, QT], F32)
        negpeak = s.sb("negpeak", [P, QT], F16)
        full = s.sb("prob_full", [P, 4, 512], F32)
        probs = s.sb("probs", [P, 2, RT, NH, P], F16)
        inv = s.sb("inv", [P, 2, 8], F32)
        low = s.sb("low", [P, 2, 8, D], F32)
        mid = s.sb("mid", [P, 2, 8, D], F32)
        win = s.sb("table_windows", [RK + 1, QT, 2, WIN + 2], F16)
        qr = s.sb("step_q_rel", [RK + 1, QT, NH, LB], F16)
        q4 = s.sb("step_q_rel4", [RK, QT, NH, LB], F16)
        qk = s.sb("step_q_key", [RK, QT, NH, LB], F16)
        laid = s.sem("step_laid")
        win_loaded = [s.sem(f"window_loaded{u}") for u in range(QT)]
        raw_ready = s.sem("raw_ready")
        raw_free = s.sem("raw_taken")
        turned = s.sem("top_turned")
        peak_done = s.sem("peak_done")
        neg_ready = s.sem("negpeak_ready")
        row_made = s.sem("row_made")
        row_ready = s.sem("row_ready")
        score_ready = s.sem("score_ready")
        full_ready = s.sem("full_ready")
        cast_ready = s.sem("hi_cast_ready")
        lo_ready = s.sem("prob_lo_ready")
        pv_ready = s.sem("pv_ready")
        out_done = s.sem("out_done")
        nsteps = s.sem("norm_steps")
        CAST = (1, 3, 5)

        with nc.Block() as block:
            def windows(engine, n, u):
                x = (S + 2 + (AHEAD - 1) * LB) - LB * n
                engine.dma_start(win[:, u, :, 0:WIN], RS[:, :, bass.ds(x, WIN)]).then_inc(win_loaded[u], 16)

            @block.sync
            def _(sp):
                for u in range(QT):
                    sp.wait_ge(win_loaded[u], 16 * (RT + (u < AHEAD)))

            @block.tensor
            def _(pe):
                def keys(bank, u, rt):
                    for g in range(NH // 2):
                        nc.tensor.matmul(bank[:, 2 * g * LB:2 * (g + 1) * LB], KT[0:RK, g, rt * P:(rt + 1) * P],
                                         qk[0:RK, u, 2 * g:2 * g + 2, :], start=(g == 0), stop=False)

                def table(bank, u, rt, form, moving, rows, together):
                    cols = bank.rearrange("p (h l) -> p h l", l=LB)
                    for j in range(0, LB, together):
                        x = rt * P + LB - 2 - j
                        last = nc.tensor.matmul(cols[:, :, j:j + together], win[0:rows, u, form, x:x + P],
                                                moving[0:rows, u, :, j:j + together],
                                                start=False, stop=(j == LB - together))
                    return last

                def raw(t, n, u, rt):
                    if rt == 0:
                        pe.wait_ge(laid, n + 1)
                        pe.wait_ge(win_loaded[u], 16 * t + 16)
                    pe.wait_ge(raw_free, RT * n + rt + 1)
                    keys(pm[:, rt % 2, :], u, rt)
                    table(pm[:, rt % 2, :], u, rt, 1, q4, RK, 4).then_inc(raw_ready, 1)

                def score(n, u, rt):
                    if rt == 0:
                        pe.wait_ge(row_ready, n + 2)
                    pe.wait_ge(full_ready, RT * n + rt + 1)
                    keys(pz[:, rt % 2, :], u, rt)
                    table(pz[:, rt % 2, :], u, rt, 0, qr, RK + 1, 2).then_inc(score_ready, 1)

                def turn(n, u):
                    pe.wait_ge(raw_free, RT * n + RT + 2)
                    pe.wait_ge(row_ready, n + 1)
                    for c in range(QT):
                        last = nc.tensor.transpose(pt[:, 0, c * P:(c + 1) * P], top[:, u % 2, c * P:(c + 1) * P],
                                                   k.ident32[:])
                    last.then_inc(turned, 1)

                def row(n):
                    pe.wait_ge(neg_ready, n + 1)
                    for c in range(QT):
                        last = nc.tensor.matmul(pt[RK:RK + 1, 0, c * P:(c + 1) * P], negpeak[:, c:c + 1],
                                                k.ident16[:], start=True, stop=True)
                    last.then_inc(row_made, 1)

                def ahead(t, n, u, i):
                    m = 1 if i < 4 else 2
                    raw(t + (u + m) // QT, n + m, (u + m) % QT, (i + 4) % RT)

                def pv_tile(t, n, rt):
                    if rt == 0:
                        pe.wait_ge(out_done, t + 1)
                    if rt in CAST:
                        pe.wait_ge(cast_ready, len(CAST) * n + CAST.index(rt) + 1)
                    else:
                        pe.wait_ge(full_ready, 2 + RT * n + rt + 1)
                    for hl in range(2):
                        if hl == LO:
                            pe.wait_ge(lo_ready, 4 + RT * n + rt + 1)
                        for h in range(NH):
                            last = nc.tensor.matmul(pv[:, h // 8, (h % 8) * 33:(h % 8 + 1) * 33],
                                                    probs[:, hl, rt, h, :], V[:, b * RT + rt, h, :],
                                                    start=(rt == 0 and hl == HI and h % 8 == 0),
                                                    stop=(rt == RT - 1 and hl == LO and h % 8 == 7))
                    last.then_inc(pv_ready, 1)

                def step(t, u):
                    n = QT * t + u
                    for i in range(4):
                        ahead(t, n, u, i)
                        score(n, u, i)
                    if u < QT - 1:
                        order = ("a4", "s4", "a5", "s5", "turn", "a6", "s6", "row", "a7", "s7")
                    else:
                        order = ("p0", "a4", "s4", "p1", "a5", "s5", "turn", "p2", "a6", "s6", "row", "p3", "a7", "s7",
                                 "p4", "p5", "p6", "p7")
                    for what in order:
                        if what == "turn":
                            turn(n + 1, (u + 1) % QT)
                        elif what == "row":
                            row(n + 1)
                        elif what[0] == "a":
                            ahead(t, n, u, int(what[1]))
                        elif what[0] == "p":
                            pv_tile(t, n, int(what[1]))
                        else:
                            score(n, u, int(what[1]))

                pe.sem_inc(pv_ready, RT)
                pe.sem_inc(score_ready, QT * RT)
                for rt in range(RT):
                    raw(0, 0, 0, rt)
                raw(0, 1, 1, 0)
                raw(0, 1, 1, 1)
                turn(0, 0)
                raw(0, 1, 1, 2)
                row(0)
                raw(0, 1, 1, 3)
                with pe.Fori(0, RT) as t:
                    for u in range(QT):
                        step(t, u)

            @block.scalar
            def _(act):
                def copy_row(n, u):
                    act.wait_ge(row_made, n + 1)
                    nc.scalar.copy(qr[RK:RK + 1, u, :, :],
                                   pt[RK:RK + 1, 0, :].rearrange("p (h l) -> p h l", l=LB)).then_inc(row_ready, 1)

                act.sem_inc(full_ready, 2)
                act.sem_inc(row_ready, 1)
                for n in range(AHEAD):
                    windows(act, n, n)
                copy_row(0, 0)
                with act.Fori(0, RT) as t:
                    for q in range(QT):
                        n = QT * t + q
                        for rt in range(RT):
                            act.wait_ge(score_ready, QT * RT + RT * n + rt + 1)
                            if q == 0:
                                act.wait_ge(pv_ready, RT * t + rt + 1)
                            if rt not in CAST:
                                nc.scalar.activation(probs[:, HI, rt, :, q * LB:(q + 1) * LB],
                                                     pz[:, rt % 2, :].rearrange("p (h l) -> p h l", l=LB), ACT.Exp)
                            act.wait_ge(lo_ready, RT * n + rt + 1)
                            nc.scalar.activation(full[:, rt % 4, :], pz[:, rt % 2, :], ACT.Exp).then_inc(full_ready, 1)
                            if rt == 2:
                                windows(act, n + AHEAD, (q + AHEAD) % QT)
                            if rt == 6:
                                copy_row(n + 1, (q + 1) % QT)

            @block.gpsimd
            def _(pool):
                pool.sem_inc(lo_ready, 4)
                with pool.Fori(0, RT) as t:
                    for q in range(QT):
                        n = QT * t + q
                        for rt in range(RT):
                            if rt in CAST:
                                pool.wait_ge(cast_ready, len(CAST) * n + CAST.index(rt) + 1)
                            else:
                                pool.wait_ge(full_ready, 2 + RT * n + rt + 1)
                            nc.gpsimd.tensor_tensor(probs[:, LO, rt, :, q * LB:(q + 1) * LB],
                                                    full[:, rt % 4, :].rearrange("p (h l) -> p h l", l=LB),
                                                    probs[:, HI, rt, :, q * LB:(q + 1) * LB],
                                                    ALU.subtract).then_inc(lo_ready, 1)

            @block.vector
            def _(dve):
                dve.sem_inc(raw_free, 2)
                dve.sem_inc(out_done, 1)

                def lay(n, u, i):
                    if i == 0:
                        dve.wait_ge(score_ready, RT * n + RT)
                    q_in = Q[:, :, bass.ds(LB * n, LB)]
                    if i == 0:
                        pairs = lambda x: x.rearrange("p (g two) l -> p g two l", two=2)
                        nc.vector.tensor_tensor(pairs(qk[:, u]), pairs(q_in),
                                                half[:].unsqueeze(1).unsqueeze(3).broadcast_to([RK, NH // 2, 2, LB]),
                                                ALU.mult)
                        return
                    dst, mask, m = ((qr[0:RK, u], half, 2), (q4[:, u], quarter, 4))[i - 1]
                    groups = lambda x: x.rearrange("p h (l m) -> p h l m", m=m)
                    last = nc.vector.tensor_tensor(
                        groups(dst), groups(q_in),
                        mask[:].unsqueeze(1).unsqueeze(2).broadcast_to([RK, NH, LB // m, m]), ALU.mult)
                    if i == 2:
                        last.then_inc(laid, 1)

                def take(n, u, rt):
                    dve.wait_ge(raw_ready, RT * n + rt + 1)
                    if rt == 0:
                        nc.vector.tensor_copy(top[:, u % 2, :], pm[:, 0, :]).then_inc(raw_free, 1)
                    else:
                        dve.wait_ge(raw_free, RT * n + rt + 2)
                        nc.vector.tensor_tensor(top[:, u % 2, :], pm[:, rt % 2, :], top[:, u % 2, :],
                                                ALU.max).then_inc(raw_free, 1)

                def peaks(n):
                    dve.wait_ge(turned, n + 1)
                    nc.vector.tensor_reduce(peak[:], pt[:, 0, :].rearrange("p (c r) -> p c r", r=P), X, ALU.max)\
                        .then_inc(peak_done, 1)
                    dve.wait_ge(peak_done, n + 1)
                    nc.vector.tensor_scalar(negpeak[:], peak[:], -1.0, None, ALU.mult).then_inc(neg_ready, 1)

                def cast(n, q, rt):
                    dve.wait_ge(full_ready, 2 + RT * n + rt + 1)
                    nc.vector.tensor_copy(probs[:, HI, rt, :, q * LB:(q + 1) * LB],
                                          full[:, rt % 4, :].rearrange("p (h l) -> p h l", l=LB)).then_inc(cast_ready, 1)

                def norm(t, chain):
                    link = Chain(dve, nsteps)
                    link.base = chain
                    heads = pv[:, :, 0:8 * 33].rearrange("p a (h c) -> p a h c", c=33)
                    dve.wait_ge(pv_ready, RT * (t + 2))
                    nc.vector.reciprocal(inv[:], heads[:, :, :, 32]).then_inc(nsteps, 1)
                    link.n = 1
                    link(nc.vector.tensor_copy(low[:], heads[:, :, :, D:2 * D]))
                    link(nc.vector.tensor_tensor(mid[:], heads[:, :, :, 0:D], low[:], ALU.add))
                    place = slice((b * RT + t) * H, (b * RT + t + 1) * H) if isinstance(t, int) else \
                        bass.ds((b * RT + t) * H, H)
                    nc.vector.tensor_tensor(o[:, place].rearrange("p (a h d) -> p a h d", a=2, d=D),
                                            mid[:], inv[:].unsqueeze(3).broadcast_to([P, 2, 8, D]),
                                            ALU.mult).then_inc(out_done, 1)

                def step(t, u, before=None):
                    n = QT * t + u
                    for i in range(RT):
                        m = 1 if i < 4 else 2
                        take(n + m, (u + m) % QT, (i + 4) % RT)
                        if i < 3:
                            lay(n + 2, (u + 2) % QT, i)
                        if i == 3 and before is not None:
                            norm(before, 3 * before)
                        if i - 1 in CAST:
                            cast(n, u, i - 1)
                        if i == 5:
                            peaks(n + 1)

                for n in range(2):
                    for i in range(3):
                        lay(n, n, i)
                for rt in range(RT):
                    take(0, 0, rt)
                take(1, 1, 0)
                take(1, 1, 1)
                peaks(0)
                take(1, 1, 2)
                take(1, 1, 3)
                for u in range(QT):
                    step(0, u)
                with dve.Fori(1, RT) as t:
                    for u in range(QT):
                        step(t, u, t - 1 if u == 0 else None)
                norm(RT - 1, 3 * (RT - 1))


def output_rows(nc, k, w, bias, dst, name, tiles=TT, add=True):
    with ExitStack() as stack:
        s = Scope(nc, stack)
        ps = s.banks(name + "_ps", 4)
        row = s.sb(name + "_bias", [P, H], F32)
        loaded = s.sem(name + "_loaded")
        ready = s.sem(name + "_ready")
        biased = s.sem(name + "_biased")
        added = s.sem(name + "_added")
        with nc.Block() as block:
            @block.sync
            def _(sp):
                sp.dma_start(row[:], bias.rearrange("(a d) -> a d", a=1).broadcast_to([P, H])).then_inc(loaded, 16)

            @block.tensor
            def _(pe):
                for t in range(tiles):
                    if t >= 4:
                        pe.wait_ge(added, t - 3)
                    i = 0
                    for a, b in PRODUCTS:
                        for kc in range(KC):
                            last = nc.tensor.matmul(ps[:, t % 4, 0:H], k.zT[:, a, kc, t * P:(t + 1) * P],
                                                    w[:, b, kc, :], start=(i == 0), stop=(i == 5))
                            i += 1
                    last.then_inc(ready, 1)

            @block.vector
            def _(dve):
                dve.wait_ge(loaded, 16)
                if add:
                    for t in range(tiles):
                        nc.vector.tensor_tensor(dst[:, t, :], dst[:, t, :], row[:], ALU.add).then_inc(biased, 1)
                for t in range(tiles):
                    dve.wait_ge(ready, t + 1)
                    if add:
                        dve.wait_ge(biased, t + 1)
                    nc.vector.tensor_tensor(dst[:, t, :], ps[:, t % 4, 0:H], dst[:, t, :] if add else row[:],
                                            ALU.add).then_inc(added, 1)


QH, QD = 16, 64
QI = QH * QD
RAISE = 10.5
FAR = -1e30
PAD = P
TL = PAD + S
VW = 2 * QD + 1


def row_of(v):
    return v.rearrange("(a d) -> a d", a=1)


def layer_norm(nc, src, dst, n, gain, shift, name, silu=False):
    with ExitStack() as stack:
        s = Scope(nc, stack, name + "_")
        rows = s.sb("rows", [P, 2, H], F32)
        stats = s.sb("stats", [P, n, 6], F32)
        mv = s.sb("mean_var", [P, n, 2], F32)
        std = s.sb("std", [P, n], F32)
        inv = s.sb("inv", [P, n], F32)
        loaded = s.sem("loaded")
        steps = s.sem("steps")
        with_eps = s.sem("with_eps")
        rooted = s.sem("rooted")
        scaled = s.sem("scaled")
        acted = s.sem("acted")
        params = [x for x in (gain, shift) if x is not None]
        with nc.Block() as block:
            @block.sync
            def _(sp):
                for i, x in enumerate(params):
                    sp.dma_start(rows[:, i, :], row_of(x).broadcast_to([P, H])).then_inc(loaded, 16)

            @block.scalar
            def _(act):
                act.wait_ge(with_eps, 1)
                nc.scalar.activation(std[:], std[:], ACT.Sqrt).then_inc(rooted, 1)
                if silu:
                    for t in range(n):
                        act.wait_ge(scaled, t + 1)
                        nc.scalar.activation(dst[:, t, :], dst[:, t, :], ACT.Silu).then_inc(acted, 1)

            @block.vector
            def _(dve):
                for t in range(n):
                    nc.vector.bn_stats(stats[:, t, :], src[:, t, :]).then_inc(steps, 1)
                for t in range(n):
                    dve.wait_ge(steps, t + 1)
                    nc.vector.bn_aggr(mv[:, t, :], stats[:, t, :]).then_inc(steps, 1)
                dve.wait_ge(steps, 2 * n)
                nc.vector.tensor_scalar(std[:], mv[:, :, 1], 1e-5, None, ALU.add).then_inc(with_eps, 1)
                dve.wait_ge(rooted, 1)
                nc.vector.reciprocal(inv[:], std[:]).then_inc(steps, 1)
                dve.wait_ge(steps, 2 * n + 1)
                dve.wait_ge(loaded, 16 * len(params))
                for t in range(n):
                    nc.vector.tensor_scalar(dst[:, t, :], src[:, t, :], mv[:, t, 0:1], inv[:, t:t + 1],
                                            ALU.subtract, ALU.mult).then_inc(steps, 1)
                for t in range(n):
                    dve.wait_ge(steps, 2 * n + 2 + t)
                    last = nc.vector.tensor_tensor(dst[:, t, :], dst[:, t, :], rows[:, 0, :], ALU.mult)
                    if shift is not None:
                        last.then_inc(steps, 1)
                    else:
                        last.then_inc(scaled, 1)
                if shift is not None:
                    for t in range(n):
                        dve.wait_ge(steps, 3 * n + 2 + t)
                        nc.vector.tensor_tensor(dst[:, t, :], dst[:, t, :], rows[:, 1, :], ALU.add).then_inc(scaled, 1)


def position_rows(nc, w0, b0, dst):
    with ExitStack() as stack:
        s = Scope(nc, stack, "pos_")
        rows = s.sb("rows", [P, 2, H], F32)
        pos = s.sb("distance", [P, RT], F32)
        loaded = s.sem("loaded")
        counted = s.sem("counted")
        with nc.Block() as block:
            @block.sync
            def _(sp):
                sp.dma_start(rows[:, 0, :], w0.broadcast_to([P, H])).then_inc(loaded, 16)
                sp.dma_start(rows[:, 1, :], row_of(b0).broadcast_to([P, H])).then_inc(loaded, 16)

            @block.gpsimd
            def _(pool):
                pool.iota(pos[:], [[P, RT]], 0, 1, True).then_inc(counted, 1)

            @block.vector
            def _(dve):
                dve.wait_ge(loaded, 32)
                dve.wait_ge(counted, 1)
                for c in range(RT):
                    nc.vector.scalar_tensor_tensor(out=dst[:, c, :], in0=rows[:, 0, :], scalar=pos[:, c:c + 1],
                                                   in1=rows[:, 1, :], op0=ALU.mult, op1=ALU.add)


def bias_table(nc, k, w2, b2, q_scale, k_scale, null_bias, table, null_d):
    with ExitStack() as stack:
        s = Scope(nc, stack, "table_")
        ps = s.banks("ps", 2)
        col = s.sb("col", [QH, 8], F32)
        scales = s.sb("scales", [QH, 2, QD], F32)
        loaded = s.sem("loaded")
        rooted = s.sem("rooted")
        ready = s.sem("ready")
        steps = s.sem("steps")
        stored = s.sem("stored")
        with nc.Block() as block:
            @block.sync
            def _(sp):
                sp.dma_start(scales[:, 0, :], row_of(q_scale).broadcast_to([QH, QD])).then_inc(loaded, 16)
                sp.dma_start(scales[:, 1, :], row_of(k_scale).broadcast_to([QH, QD])).then_inc(loaded, 16)
                sp.dma_start(col[:, 0:1], b2.rearrange("(h a) -> h a", a=1)).then_inc(loaded, 16)
                sp.dma_start(col[:, 1:2], null_bias.rearrange("(h a) -> h a", a=1)).then_inc(loaded, 16)
                sp.wait_ge(steps, 9)
                sp.dma_start(null_d, col[:, 5:6]).then_inc(stored, 16)
                sp.wait_ge(stored, 16)

            @block.tensor
            def _(pe):
                for c in range(2):
                    i = 0
                    for a, b in PRODUCTS:
                        for kc in range(KC):
                            last = nc.tensor.matmul(ps[0:QH, c, :], w2[:, a, kc, :], k.zT[:, b, kc, c * 512:(c + 1) * 512],
                                                    start=(i == 0), stop=(i == 5))
                            i += 1
                last.then_inc(ready, 1)

            @block.vector
            def _(dve):
                link = Chain(dve, steps)
                dve.wait_ge(loaded, 64)
                link(nc.vector.tensor_tensor(scales[:, 0, :], scales[:, 0, :], scales[:, 1, :], ALU.mult))
                link(nc.vector.tensor_tensor(scales[:, 0, :], scales[:, 0, :], scales[:, 0, :], ALU.mult))
                link(nc.vector.tensor_reduce(col[:, 2:3], scales[:, 0, :], X, ALU.max))
                dve.wait_ge(ready, 1)
                link(nc.vector.tensor_scalar(table[:, PAD:TL], ps[0:QH].rearrange("p a b -> p (a b)"), col[:, 0:1],
                                             None, ALU.add))
                link(nc.vector.tensor_reduce(col[:, 3:4], table[:, PAD:TL], X, ALU.max))
                link(nc.vector.tensor_tensor(col[:, 3:4], col[:, 3:4], col[:, 1:2], ALU.max))
                dve.wait_ge(rooted, 1)
                link(nc.vector.scalar_tensor_tensor(out=col[:, 4:5], in0=col[:, 4:5], scalar=-RAISE, in1=col[:, 3:4],
                                                    op0=ALU.add, op1=ALU.add))
                link(nc.vector.tensor_scalar(table[:, PAD:TL], table[:, PAD:TL], col[:, 4:5], None, ALU.subtract))
                link(nc.vector.tensor_tensor(col[:, 5:6], col[:, 1:2], col[:, 4:5], ALU.subtract))
                link(nc.vector.memset(table[:, 0:PAD], FAR))

            @block.scalar
            def _(act):
                act.wait_ge(steps, 3)
                nc.scalar.activation(col[:, 4:5], col[:, 2:3], ACT.Sqrt, scale=64.0).then_inc(rooted, 1)


def causal_operands(nc, k, wq, wkv, a, table, table_d, q_d, KT, V, side, nullrow):
    with ExitStack() as stack:
        s = Scope(nc, stack, "causal_")
        pq = s.banks("q_ps", 2)
        pkv = s.banks("kv_ps", 1)
        ptq = s.banks("turn_ps", 2, F16)
        ptk = s.banks("turnk_ps", 1, F16)
        pn = s.banks("null_ps", 1)
        pmask = s.banks("mask_ps", 1)
        sq = s.sb("sq", [P, QI], F32)
        norm = s.sb("norm", [P, 3, QH + 1], F32)
        unit = s.sb("unit", [P, QI], F32)
        qn = s.sb("qn", [P, 2, QH, 2, QD], F16)
        QT = s.sb("QT", [P, 2, QH, P], F16)
        kraw = s.sb("kraw", [P, 2, QD], F32)
        kn = s.sb("kn", [P, 2, 2, 2, QD], F16)
        srow = s.sb("srow", [P, 3, QD], F32)
        nk = s.sb("nk", [1, 4, QD], F32)
        nkn = s.sb("nkn", [1, 2, 2, QD], F16)
        nkc = s.sb("nkc", [1, 4], F32)
        NK = s.sb("NK", [P, 2], F16)
        nb = s.sb("null_bias", [P, QH], F32)
        m8 = s.sb("mask8", [TT, P], U8)
        m32 = s.sb("mask32", [TT, P], F32)
        loaded = s.sem("loaded")
        copied = s.sem("table_copied")
        nsteps = s.sem("null_steps")
        null_sq = s.sem("null_squares")
        null_root = s.sem("null_root")
        null_turned = s.sem("null_turned")
        null_ready = s.sem("null_ready")
        null_scored = s.sem("null_scored")
        null_biased = s.sem("null_biased")
        mask_cast = s.sem("mask_cast")
        mask_turned = s.sem("mask_turned")
        q_ready = s.sem("q_ready")
        squared = s.sem("squared")
        summed = s.sem("summed")
        rooted = s.sem("rooted")
        steps = s.sem("steps")
        unit_ready = s.sem("unit_ready")
        hi_done = s.sem("hi_done")
        lo_done = s.sem("lo_done")
        k_done = s.sem("k_done")
        zeroed = s.sem("zeroed")
        turned = s.sem("turned")
        q_moved = s.sem("q_moved")
        k_moved = s.sem("k_moved")
        stored = [s.sem(f"stored{i}") for i in range(2)]
        with nc.Block() as block:
            @block.sync
            def _(sp):
                sp.dma_start(srow[:, 0, :], row_of(a["L0_cond2_q_scale"]).broadcast_to([P, QD])).then_inc(loaded, 16)
                sp.dma_start(srow[:, 1, :], row_of(a["L0_cond2_k_scale"]).broadcast_to([P, QD])).then_inc(loaded, 16)
                sp.dma_start(nk[:, 0, :], a["cond_64"][0:1, :]).then_inc(loaded, 16)
                sp.dma_start(nb[:], nullrow[1].rearrange("h a -> a h").broadcast_to([P, QH]),
                             allow_slow_non_contiguous=True).then_inc(loaded, 16)
                sp.dma_start(m8[:], a["mask_BxS_bf1"].rearrange("b (t p) -> (b t) p", p=P)).then_inc(loaded, 16)
                for h in range(QH):
                    sp.dma_start(table_d[h:h + 1], table[h:h + 1, :].unsqueeze(1).broadcast_to([1, P, TL])).then_inc(copied, 16)
                for t in range(TT):
                    sp.wait_ge(q_moved, 2 * (t + 1))
                    sp.dma_start(q_d[:, :, t * P:(t + 1) * P].rearrange("h p t -> p h t"), QT[:, t % 2]).then_inc(stored[t % 2], 16)
                for i in range(2):
                    sp.wait_ge(stored[i], 16 * (TT // 2))
                sp.wait_ge(copied, 16 * QH)

            @block.gpsimd
            def _(pool):
                pool.memset(kn[:], 0.0).then_inc(zeroed, 1)
                pool.memset(V[:, :, 2 * QD:VW], 1.0)
                for t in range(TT):
                    pool.wait_ge(hi_done, t + 1)
                    nc.gpsimd.tensor_tensor(qn[:, t % 2, :, LO, :], unit[:].rearrange("p (h d) -> p h d", d=QD),
                                            qn[:, t % 2, :, HI, :], ALU.subtract).then_inc(lo_done, 1)

            @block.tensor
            def _(pe):
                pe.wait_ge(mask_cast, 1)
                nc.tensor.transpose(pmask[:, 0, 0:TT], m32[:], k.ident32[0:TT, 0:TT]).then_inc(mask_turned, 1)
                pe.wait_ge(nsteps, 6)
                nc.tensor.transpose(ptk[:, 0, 0:2:2], nkn[:, 0].rearrange("p a d -> p (a d)"), k.ident16[0:1, 0:1])
                nc.tensor.transpose(ptk[:, 0, 2:4:2], nkn[:, 1].rearrange("p a d -> p (a d)"), k.ident16[0:1, 0:1])\
                    .then_inc(null_turned, 1)

                def project(t):
                    if t >= 1:
                        pe.wait_ge(unit_ready, t)
                        pe.wait_ge(k_done, t)
                    for c in range(2):
                        i = 0
                        for x, y in PRODUCTS:
                            for kc in range(KC):
                                nc.tensor.matmul(pq[:, c, :], k.zT[:, x, kc, t * P:(t + 1) * P],
                                                 wq[:, y, kc, c * 512:(c + 1) * 512], start=(i == 0), stop=(i == 5))
                                i += 1
                    i = 0
                    for x, y in PRODUCTS:
                        for kc in range(KC):
                            last = nc.tensor.matmul(pkv[:, 0, 0:2 * QD], k.zT[:, x, kc, t * P:(t + 1) * P],
                                                    wkv[:, y, kc, :], start=(i == 0), stop=(i == 5))
                            i += 1
                    last.then_inc(q_ready, 1)

                def turn(t):
                    pe.wait_ge(lo_done, t + 1)
                    pe.wait_ge(k_done, t + 1)
                    for c in range(2):
                        if t >= 1:
                            pe.wait_ge(q_moved, 2 * (t - 1) + c + 1)
                        for h in range(8):
                            last = nc.tensor.transpose(ptq[:, c, h * P:(h + 1) * P],
                                                       qn[:, t % 2, 8 * c + h].rearrange("p a d -> p (a d)"), k.ident16[:])
                        last.then_inc(turned, 1)
                    if t >= 1:
                        pe.wait_ge(k_moved, t)
                    for c in range(2):
                        last = nc.tensor.transpose(ptk[:, 0, c * P:(c + 1) * P],
                                                   kn[:, t % 2, c].rearrange("p a d -> p (a d)"), k.ident16[:])
                    last.then_inc(turned, 1)
                    pe.wait_ge(q_moved, 2 * (t + 1))
                    for h in range(QH):
                        for c in range(2):
                            last = nc.tensor.matmul(pn[:, 0, t * QH + h:t * QH + h + 1], QT[:, t % 2, h, :],
                                                    NK[:, c:c + 1], start=(c == 0), stop=(c == 1))
                    last.then_inc(null_scored, 1)

                project(0)
                pe.wait_ge(null_ready, 1)
                for t in range(TT):
                    if t + 1 < TT:
                        project(t + 1)
                    turn(t)

            @block.scalar
            def _(act):
                act.wait_ge(null_sq, 1)
                nc.scalar.activation(nkc[:, 1:2], nkc[:, 0:1], ACT.Sqrt).then_inc(null_root, 1)

                def squares(t):
                    act.wait_ge(q_ready, t + 1)
                    nc.scalar.activation(sq[:], pq[:].rearrange("p a b -> p (a b)"), ACT.Square).then_inc(squared, 1)

                def rest(t):
                    act.wait_ge(summed, t + 1)
                    nc.scalar.activation(norm[:, 1, :], norm[:, 0, :], ACT.Sqrt).then_inc(rooted, 1)
                    act.wait_ge(unit_ready, t + 1)
                    nc.scalar.copy(qn[:, t % 2, :, HI, :], unit[:].rearrange("p (h d) -> p h d", d=QD)).then_inc(hi_done, 1)
                    for c in range(2):
                        if t >= 2:
                            act.wait_ge(stored[t % 2], 16 * (t // 2))
                            act.wait_ge(null_scored, t - 1)
                        act.wait_ge(turned, 3 * t + c + 1)
                        nc.scalar.copy(QT[:, t % 2, 8 * c:8 * c + 8, :],
                                       ptq[:, c, :].rearrange("p (h t) -> p h t", t=P)).then_inc(q_moved, 1)

                for t in range(TT):
                    squares(t)
                    rest(t)
                act.wait_ge(null_biased, 1)
                nc.scalar.activation(nullrow[0][:], nullrow[0][:], ACT.Exp).then_inc(null_biased, 1)

            @block.vector
            def _(dve):
                link = Chain(dve, nsteps)
                dve.wait_ge(loaded, 16 * 5)
                link(nc.vector.tensor_tensor(srow[:, 2, :], srow[:, 0, :], srow[:, 1, :], ALU.mult))
                link(nc.vector.tensor_scalar(srow[:, 2, :], srow[:, 2, :], 8.0, None, ALU.mult))
                nc.vector.tensor_copy(m32[:], m8[:]).then_inc(mask_cast, 1)
                link(nc.vector.tensor_tensor(nk[:, 1, :], nk[:, 0, :], nk[:, 0, :], ALU.mult))
                nc.vector.tensor_reduce(nkc[:, 0:1], nk[:, 1, :], X, ALU.add).then_inc(null_sq, 1)
                dve.wait_ge(null_root, 1)
                nc.vector.tensor_scalar(nkc[:, 2:3], nkc[:, 1:2], 1e-12, None, ALU.max).then_inc(null_sq, 1)
                dve.wait_ge(null_sq, 2)
                nc.vector.reciprocal(nkc[:, 3:4], nkc[:, 2:3]).then_inc(null_sq, 1)
                dve.wait_ge(null_sq, 3)
                link(nc.vector.scalar_tensor_tensor(out=nk[:, 2, :], in0=nk[:, 0, :], scalar=nkc[:, 3:4],
                                                    in1=srow[0:1, 2, :], op0=ALU.mult, op1=ALU.mult))
                nc.vector.memset(nkn[:, 1, 1, :], 0.0)
                nc.vector.tensor_copy(nkn[:, 0, 1, :], nk[:, 2, :])
                link(nc.vector.tensor_copy(nkn[:, 0, 0, :], nk[:, 2, :]))
                link(nc.vector.tensor_tensor(nkn[:, 1, 0, :], nk[:, 2, :], nkn[:, 0, 0, :], ALU.subtract))
                dve.wait_ge(null_turned, 1)
                nc.vector.tensor_copy(NK[:], ptk[:, 0, 0:4:2]).then_inc(null_ready, 1)
                dve.wait_ge(mask_turned, 1)
                nc.vector.tensor_scalar(side[:], pmask[:, 0, 0:TT], 1.0, -FAR, ALU.subtract, ALU.mult)
                dve.wait_ge(zeroed, 1)
                chain = Chain(dve, steps)
                for t in range(TT):
                    dve.wait_ge(squared, t + 1)
                    chain(nc.vector.tensor_reduce(norm[:, 0, 0:QH], sq[:].rearrange("p (h d) -> p h d", d=QD), X, ALU.add))
                    chain(nc.vector.tensor_copy(kraw[:, 0, :], pkv[:, 0, 0:QD]))
                    chain(nc.vector.tensor_tensor(kraw[:, 1, :], kraw[:, 0, :], kraw[:, 0, :], ALU.mult))
                    nc.vector.tensor_reduce(norm[:, 0, QH:QH + 1], kraw[:, 1, :], X, ALU.add).then_inc(summed, 1)
                    dve.wait_ge(rooted, t + 1)
                    chain(nc.vector.tensor_scalar(norm[:, 2, :], norm[:, 1, :], 1e-12, None, ALU.max))
                    chain(nc.vector.reciprocal(norm[:, 2, :], norm[:, 2, :]))
                    if t >= 1:
                        dve.wait_ge(lo_done, t)
                    nc.vector.tensor_tensor(unit[:].rearrange("p (h d) -> p h d", d=QD),
                                            pq[:].rearrange("p a (h d) -> p (a h) d", d=QD),
                                            norm[:, 2, 0:QH].unsqueeze(2).broadcast_to([P, QH, QD]),
                                            ALU.mult).then_inc(unit_ready, 1)
                    chain(nc.vector.scalar_tensor_tensor(out=kraw[:, 1, :], in0=kraw[:, 0, :], scalar=norm[:, 2, QH:QH + 1],
                                                         in1=srow[:, 2, :], op0=ALU.mult, op1=ALU.mult))
                    if t >= 2:
                        dve.wait_ge(turned, 3 * (t - 1))
                    nc.vector.tensor_copy(kn[:, t % 2, 0, 1, :], kraw[:, 1, :])
                    chain(nc.vector.tensor_copy(kn[:, t % 2, 0, 0, :], kraw[:, 1, :]))
                    nc.vector.tensor_tensor(kn[:, t % 2, 1, 0, :], kraw[:, 1, :], kn[:, t % 2, 0, 0, :], ALU.subtract)
                    chain(nc.vector.tensor_copy(V[:, t, 0:QD], pkv[:, 0, QD:2 * QD]))
                    nc.vector.tensor_tensor(V[:, t, QD:2 * QD], pkv[:, 0, QD:2 * QD], V[:, t, 0:QD],
                                            ALU.subtract).then_inc(k_done, 1)
                    if t >= 1:
                        dve.wait_ge(turned, 3 * t)
                        nc.vector.tensor_copy(KT[:, :, (t - 1) * P:t * P],
                                              ptk[:, 0, 0:2 * P].rearrange("p (a t) -> p a t", a=2)).then_inc(k_moved, 1)
                dve.wait_ge(turned, 3 * TT)
                nc.vector.tensor_copy(KT[:, :, (TT - 1) * P:T],
                                      ptk[:, 0, 0:2 * P].rearrange("p (a t) -> p a t", a=2)).then_inc(k_moved, 1)
                dve.wait_ge(null_scored, TT)
                nc.vector.tensor_tensor(nullrow[0][:], pn[:, 0, 0:TT * QH].rearrange("p (t h) -> p t h", h=QH),
                                        nb[:].unsqueeze(1).broadcast_to([P, TT, QH]), ALU.add).then_inc(null_biased, 1)


def causal_pieces():
    out, at = [], 0
    for c in range(2):
        for j in range(4 * (c + 1)):
            first = max(512 * c, P * j)
            out.append((j, first, 512 * (c + 1) - first, at))
            at += 512 * (c + 1) - first
    return out, at


PIECES, PCOLS = causal_pieces()
NP = len(PIECES)


def causal_attention(nc, k, table_d, q_d, KT, V, side, null, nv, o):
    with ExitStack() as stack:
        s = Scope(nc, stack, "heads_")
        pz = s.banks("ps", 4)
        pv = s.banks("pv", 4)
        tile = s.sb("toeplitz", [P, 2, S], F32)
        q = s.sb("q", [P, 4, S], F16)
        sums = s.sb("biased", [P, 4, 512], F32)
        full = s.sb("prob_full", [P, 4, 512], F32)
        probs = s.sb("probs", [P, 2, 2, PCOLS], F16)
        nvrow = s.sb("null_value", [P, QD], F32)
        low = s.sb("low", [P, RT, QD], F32)
        mid = s.sb("mid", [P, RT, QD], F32)
        nulls = s.sb("nulls", [P, RT, QD], F32)
        inv = s.sb("inv", [P, 2, RT], F32)
        nv_loaded = s.sem("nv_loaded")
        tile_loaded = [s.sem(f"tile_loaded{i}") for i in range(2)]
        q_loaded = [s.sem(f"q_loaded{i}") for i in range(4)]
        score_ready = s.sem("score_ready")
        sum_ready = s.sem("sum_ready")
        full_ready = s.sem("full_ready")
        hi_ready = s.sem("hi_ready")
        lo_ready = s.sem("lo_ready")
        pv_ready = s.sem("pv_ready")
        out_done = s.sem("out_done")
        steps = s.sem("steps")
        HP = QH // 2
        with nc.Block() as block:
            @block.sync
            def _(sp):
                sp.dma_start(nvrow[:], nv.broadcast_to([P, QD])).then_inc(nv_loaded, 16)
                sp.wait_ge(nv_loaded, 16)
                with sp.Fori(0, HP) as g:
                    for u in range(2):
                        n0 = 4 * g + 2 * u
                        sp.wait_ge(sum_ready, NP * (n0 - 2) + 2 * NP + 4)
                        src = bass.AP(tensor=table_d.tensor, offset=(2 * g + u) * (P * TL) + PAD,
                                      ap=[[TL - 1, P], [1, S]])
                        sp.dma_start(tile[:, u, :], src).then_inc(tile_loaded[u], 16)
                        for b in range(B):
                            sp.dma_start(q[:, 2 * u + b, :], q_rows(q_d, 2 * g + u, b)).then_inc(q_loaded[2 * u + b], 16)

            @block.tensor
            def _(pe):
                def score(n, g, v):
                    b = v % 2
                    pe.wait_ge(q_loaded[v], 16 * g + 16)
                    for i, (j, first, w, _) in enumerate(PIECES):
                        pe.wait_ge(sum_ready, NP * n + i + 1)
                        at = b * S + j * P
                        nc.tensor.matmul(pz[:, i % 4, 0:w], KT[:, 0, at:at + P], q[:, v, first:first + w],
                                         start=True, stop=False)
                        nc.tensor.matmul(pz[:, i % 4, 0:w], KT[:, 1, at:at + P], q[:, v, first:first + w],
                                         start=False, stop=True).then_inc(score_ready, 1)

                def mix(n, v):
                    b = v % 2
                    pe.wait_ge(hi_ready, 4 + NP * (n + 1))
                    pe.wait_ge(lo_ready, 4 + NP * (n + 1))
                    pe.wait_ge(out_done, n + 1)
                    for t in range(RT):
                        mine = [(j, at + t * P - first) for j, first, w, at in PIECES
                                if first <= t * P < first + w and j <= t]
                        for i, (j, at) in enumerate(mine):
                            for hl in range(2):
                                last = nc.tensor.matmul(pv[:, t // 2, (t % 2) * VW:(t % 2 + 1) * VW],
                                                        probs[:, n_par(v), hl, at:at + P], V[:, b * RT + j, :],
                                                        start=(i == 0 and hl == 0), stop=(i == t and hl == 1))
                    last.then_inc(pv_ready, 1)

                pe.sem_inc(pv_ready, 2)
                score(0, 0, 0)
                with pe.Fori(0, HP - 1) as g:
                    for v in range(4):
                        score(4 * g + v + 1, g + (v + 1) // 4, (v + 1) % 4)
                        mix(4 * g + v, v)
                g = HP - 1
                for v in range(4):
                    if v < 3:
                        score(4 * g + v + 1, g, v + 1)
                    mix(4 * g + v, v)

            @block.scalar
            def _(act):
                act.sem_inc(hi_ready, 4)
                with act.Fori(0, HP) as g:
                    for v in range(4):
                        n = 4 * g + v
                        act.wait_ge(pv_ready, n + 1)
                        for i, (j, first, w, at) in enumerate(PIECES):
                            key = v % 2 * RT + j
                            act.wait_ge(sum_ready, 4 + NP * n + i + 1)
                            act.wait_ge(lo_ready, NP * n + i + 1)
                            nc.scalar.activation(full[:, i % 4, 0:w], sums[:, i % 4, 0:w], ACT.Exp,
                                                 bias=side[:, key:key + 1]).then_inc(full_ready, 1)
                            nc.scalar.activation(probs[:, n_par(v), HI, at:at + w], sums[:, i % 4, 0:w], ACT.Exp,
                                                 bias=side[:, key:key + 1]).then_inc(hi_ready, 1)

            @block.gpsimd
            def _(pool):
                pool.sem_inc(lo_ready, 4)
                with pool.Fori(0, HP) as g:
                    for v in range(4):
                        n = 4 * g + v
                        for i, (j, first, w, at) in enumerate(PIECES):
                            pool.wait_ge(full_ready, NP * n + i + 1)
                            pool.wait_ge(hi_ready, 4 + NP * n + i + 1)
                            nc.gpsimd.tensor_tensor(probs[:, n_par(v), LO, at:at + w], full[:, i % 4, 0:w],
                                                    probs[:, n_par(v), HI, at:at + w], ALU.subtract).then_inc(lo_ready, 1)

            @block.vector
            def _(dve):
                dve.sem_inc(sum_ready, 4)
                dve.sem_inc(out_done, 1)

                def bias(n, g, v):
                    dve.wait_ge(tile_loaded[v // 2], 16 * g + 16)
                    for i, (j, first, w, _) in enumerate(PIECES):
                        dve.wait_ge(score_ready, NP * n + i + 1)
                        dve.wait_ge(hi_ready, NP * n + i + 1)
                        nc.vector.tensor_tensor(sums[:, i % 4, 0:w], pz[:, i % 4, 0:w],
                                                tile[:, v // 2, first - j * P:first - j * P + w],
                                                ALU.add).then_inc(sum_ready, 1)

                def norm(n, g, v):
                    b = v % 2
                    head = 2 * g + v // 2
                    link = Chain(dve, steps)
                    link.base = 5 * n
                    pn = null_of(null, b, head)
                    acc = pv[:, :, 0:2 * VW].rearrange("p a (t c) -> p a t c", c=VW)
                    pair = lambda x: x.rearrange("p (a t) d -> p a t d", t=2)
                    dve.wait_ge(pv_ready, n + 3)
                    nc.vector.tensor_tensor(nulls[:], pn.unsqueeze(2).broadcast_to([P, RT, QD]),
                                            nvrow[:].unsqueeze(1).broadcast_to([P, RT, QD]), ALU.mult).then_inc(steps, 1)
                    nc.vector.tensor_tensor(inv[:, 0, :].rearrange("p (a t) -> p a t", t=2), acc[:, :, :, 2 * QD],
                                            pn.rearrange("p (a t) -> p a t", t=2), ALU.add).then_inc(steps, 1)
                    link.n = 2
                    dve.wait_ge(steps, link.base + 2)
                    link(nc.vector.tensor_tensor(pair(low[:]), acc[:, :, :, QD:2 * QD], pair(nulls[:]), ALU.add))
                    nc.vector.reciprocal(inv[:, 1, :], inv[:, 0, :]).then_inc(steps, 1)
                    nc.vector.tensor_tensor(pair(mid[:]), acc[:, :, :, 0:QD], pair(low[:]), ALU.add).then_inc(steps, 1)
                    dve.wait_ge(steps, link.base + 5)
                    nc.vector.tensor_tensor(out_of(o, b, head), mid[:],
                                            inv[:, 1, :].unsqueeze(2).broadcast_to([P, RT, QD]),
                                            ALU.mult).then_inc(out_done, 1)

                bias(0, 0, 0)
                with dve.Fori(0, HP - 1) as g:
                    for v in range(4):
                        bias(4 * g + v + 1, g + (v + 1) // 4, (v + 1) % 4)
                        norm(4 * g + v, g, v)
                g = HP - 1
                for v in range(4):
                    if v < 3:
                        bias(4 * g + v + 1, g, v + 1)
                    norm(4 * g + v, g, v)


def n_par(v):
    return v % 2


def q_rows(q_d, head, b):
    return bass.AP(tensor=q_d.tensor, offset=head * (P * T) + b * S, ap=[[T, P], [1, S]])


def null_of(null, b, head):
    return null[:].rearrange("p h t -> p (h t)")[:, bass.ds(head * TT + b * RT, RT)]


def out_of(o, b, head):
    return o[:, b * RT:(b + 1) * RT, bass.ds(head * QD, QD)]


def causal_output(nc, k, o, w, dst):
    with ExitStack() as stack:
        s = Scope(nc, stack, "causal_out_")
        pt = s.banks("turn_ps", 4)
        ps = s.banks("ps", 2)
        oT = s.sb("oT", [P, 2, 2, 8, P], F16)
        turned = s.sem("turned")
        hi_done = s.sem("hi_done")
        lo_done = s.sem("lo_done")
        ready = s.sem("ready")
        copied = s.sem("copied")
        with nc.Block() as block:
            @block.tensor
            def _(pe):
                def turn(t):
                    for c in range(2):
                        n = 2 * t + c
                        if n >= 4:
                            pe.wait_ge(lo_done, n - 3)
                        for i in range(4):
                            x = (4 * c + i) * P
                            last = nc.tensor.transpose(pt[:, n % 4, i * P:(i + 1) * P], o[:, t, x:x + P], k.ident32[:])
                        last.then_inc(turned, 1)

                turn(0)
                for t in range(TT):
                    if t + 1 < TT:
                        turn(t + 1)
                    pe.wait_ge(lo_done, 2 * (t + 1))
                    if t >= 2:
                        pe.wait_ge(copied, t - 1)
                    i = 0
                    for x, y in PRODUCTS:
                        for c in range(8):
                            last = nc.tensor.matmul(ps[:, t % 2, 0:H], oT[:, t % 2, x, c, :], w[:, y, c, :],
                                                    start=(i == 0), stop=(i == 23))
                            i += 1
                    last.then_inc(ready, 1)

            @block.scalar
            def _(act):
                for n in range(2 * TT):
                    t, c = n // 2, n % 2
                    act.wait_ge(turned, n + 1)
                    if t >= 2:
                        act.wait_ge(ready, t - 1)
                    nc.scalar.copy(oT[:, t % 2, HI, 4 * c:4 * c + 4, :],
                                   pt[:, n % 4, :].rearrange("p (c t) -> p c t", t=P)).then_inc(hi_done, 1)

            @block.vector
            def _(dve):
                for t in range(TT):
                    for c in range(2):
                        n = 2 * t + c
                        dve.wait_ge(hi_done, n + 1)
                        nc.vector.tensor_tensor(oT[:, t % 2, LO, 4 * c:4 * c + 4, :],
                                                pt[:, n % 4, :].rearrange("p (c t) -> p c t", t=P),
                                                oT[:, t % 2, HI, 4 * c:4 * c + 4, :], ALU.subtract).then_inc(lo_done, 1)
                    if t >= 1:
                        dve.wait_ge(ready, t)
                        nc.vector.tensor_copy(dst[:, t - 1, :], ps[:, (t - 1) % 2, 0:H]).then_inc(copied, 1)
                dve.wait_ge(ready, TT)
                nc.vector.tensor_copy(dst[:, TT - 1, :], ps[:, (TT - 1) % 2, 0:H]).then_inc(copied, 1)


def gelu_operands(nc, k, b1, b2, W, b1T, x):
    with ExitStack() as stack:
        s = Scope(nc, stack, "gelu_pre_")
        pt = s.banks("ps", 4)
        pb = s.banks("bias_ps", 2)
        rows = s.sb("b1_rows", [E * FC, P], F32)
        b2r = s.sb("b2_rows", [E, H], F32)
        WT = s.sb("WT", [E, T], F32)
        loaded = s.sem("loaded")
        b1_turned = s.sem("b1_turned")
        b1_done = s.sem("b1_done")
        w_turned = s.sem("w_turned")
        w_done = s.sem("w_done")
        ready = s.sem("ready")
        added = s.sem("added")
        with nc.Block() as block:
            @block.sync
            def _(sp):
                sp.dma_start(rows[:], b1.rearrange("e (c p) -> (e c) p", p=P)).then_inc(loaded, 16)
                sp.dma_start(b2r[:], b2).then_inc(loaded, 16)

            @block.tensor
            def _(pe):
                for t in range(TT):
                    last = nc.tensor.transpose(pt[0:E, t // 4, (t % 4) * P:(t % 4 + 1) * P], W[:, 0:E, t], k.ident32[:])
                last.then_inc(w_turned, 1)
                pe.wait_ge(loaded, 32)
                nc.tensor.transpose(pb[:, 0, 0:E * FC], rows[:], k.ident32[0:E * FC, 0:E * FC]).then_inc(b1_turned, 1)
                pe.wait_ge(w_done, 1)
                pe.wait_ge(b1_done, 1)
                for t in range(TT):
                    if t >= 2:
                        pe.wait_ge(added, t - 1)
                    nc.tensor.matmul(pb[:, t % 2, 0:H], WT[:, t * P:(t + 1) * P], b2r[:], start=True, stop=True)\
                        .then_inc(ready, 1)

            @block.vector
            def _(dve):
                dve.wait_ge(w_turned, 1)
                nc.vector.tensor_copy(WT[:], pt[0:E].rearrange("p a b -> p (a b)")).then_inc(w_done, 1)
                dve.wait_ge(b1_turned, 1)
                nc.vector.tensor_copy(b1T[:], pb[:, 0, 0:E * FC]).then_inc(b1_done, 1)
                for t in range(TT):
                    dve.wait_ge(ready, t + 1)
                    nc.vector.tensor_tensor(x[:, t, :], pb[:, t % 2, 0:H], x[:, t, :], ALU.add).then_inc(added, 1)


def gelu_experts(nc, k, w1, w2, b1T, W, acc):
    with ExitStack() as stack:
        s = Scope(nc, stack, "gelu_")
        ph = s.banks("hid_ps", FC)
        py = s.banks("down_ps", 4)
        full = s.sb("full", [P, 2, FC, 512], F32)
        parts = s.sb("parts", [P, 2, 2, FC, 512], F16)
        hid_ready = s.sem("hid_ready")
        full_ready = s.sem("full_ready")
        hi_ready = s.sem("hi_ready")
        lo_ready = s.sem("lo_ready")
        down_ready = s.sem("down_ready")
        down_free = s.sem("down_free")
        b1 = s.sb("b1_of_expert", [P, FC], F32)
        b1_ready = s.sem("b1_ready")
        with nc.Block() as block:
            @block.tensor
            def _(pe):
                pe.sem_inc(down_ready, 8)

                def hidden(e, c):
                    n = TC * e + c
                    for f in range(FC):
                        pe.wait_ge(full_ready, FC * n + f + 1)
                        i = 0
                        for a, b in PRODUCTS:
                            for kc in range(KC):
                                last = nc.tensor.matmul(ph[:, f, :], part_of(w1[:, a, kc], e, F, f * P, P),
                                                        k.zT[:, b, kc, c * 512:(c + 1) * 512],
                                                        start=(i == 0), stop=(i == 5))
                                i += 1
                        last.then_inc(hid_ready, 1)

                def down(e, c):
                    n = TC * e + c
                    pe.wait_ge(hi_ready, FC * (n + 1))
                    pe.wait_ge(lo_ready, 8 + FC * (n + 1))
                    for j in range(4):
                        pe.wait_ge(down_free, 4 * n + j + 1)
                        i = 0
                        for f in range(FC):
                            for a, b in PRODUCTS:
                                last = nc.tensor.matmul(py[:, j, 0:H], parts[:, c % 2, a, f, j * P:(j + 1) * P],
                                                        part_of(w2[:, b].rearrange("p (e f) h -> p e (f h)", f=FC),
                                                                e, FC * H, f * H, H),
                                                        start=(i == 0), stop=(i == 3 * FC - 1))
                                i += 1
                        last.then_inc(down_ready, 1)

                def expert(e, following):
                    for c in range(TC):
                        if c + 1 < TC:
                            hidden(e, c + 1)
                        elif following is not None:
                            hidden(following, 0)
                        down(e, c)

                hidden(0, 0)
                with pe.Fori(0, E - 1) as e:
                    expert(e, e + 1)
                expert(E - 1, None)

            @block.scalar
            def _(act):
                act.sem_inc(full_ready, 4)
                with act.Fori(0, E) as e:
                    act.wait_ge(b1_ready, e + 1)
                    for c in range(TC):
                        for f in range(FC):
                            m = FC * (TC * e + c) + f
                            act.wait_ge(hid_ready, m + 1)
                            act.wait_ge(lo_ready, m + 1)
                            nc.scalar.activation(full[:, c % 2, f, :], ph[:, f, :], ACT.Gelu,
                                                 bias=b1[:, f:f + 1]).then_inc(full_ready, 1)

            @block.gpsimd
            def _(pool):
                pool.sem_inc(lo_ready, 8)
                with pool.Fori(0, E) as e:
                    for c in range(TC):
                        for f in range(FC):
                            m = FC * (TC * e + c) + f
                            pool.wait_ge(hi_ready, m + 1)
                            nc.gpsimd.tensor_tensor(parts[:, c % 2, LO, f, :], full[:, c % 2, f, :],
                                                    parts[:, c % 2, HI, f, :], ALU.subtract).then_inc(lo_ready, 1)

            @block.vector
            def _(dve):
                dve.sem_inc(down_free, 4)

                def bias(e):
                    cols = slice(0, FC) if isinstance(e, int) and e == 0 else bass.ds(FC * e, FC)
                    nc.vector.tensor_copy(b1[:], b1T[:, cols]).then_inc(b1_ready, 1)

                def halves(e, c):
                    n = TC * e + c
                    dve.wait_ge(down_ready, 4 * n + 4)
                    for f in range(FC):
                        dve.wait_ge(full_ready, 4 + FC * n + f + 1)
                        nc.vector.tensor_copy(parts[:, c % 2, HI, f, :], full[:, c % 2, f, :]).then_inc(hi_ready, 1)

                def weigh(e, c):
                    n = TC * e + c
                    for j in range(4):
                        t = 4 * c + j
                        dve.wait_ge(down_ready, 8 + 4 * n + j + 1)
                        nc.vector.scalar_tensor_tensor(out=acc[:, t, :], in0=py[:, j, 0:H],
                                                       scalar=expert_weight(W, e, t), in1=acc[:, t, :],
                                                       op0=ALU.mult, op1=ALU.add).then_inc(down_free, 1)

                def expert(e, following):
                    for c in range(TC):
                        if c + 1 < TC:
                            halves(e, c + 1)
                            if c + 2 == TC and following is not None:
                                bias(following)
                        elif following is not None:
                            halves(following, 0)
                        weigh(e, c)

                bias(0)
                halves(0, 0)
                with dve.Fori(0, E - 1) as e:
                    expert(e, e + 1)
                expert(E - 1, None)


def part_of(w, e, stride, at, width):
    if isinstance(e, int):
        return w[:, e, at:at + width]
    return w.rearrange("p e n -> p (e n)")[:, bass.ds(e * stride + at, width)]


def add_rows(nc, src, dst):
    with nc.Block() as block:
        @block.vector
        def _(dve):
            for t in range(TT):
                nc.vector.tensor_tensor(dst[:, t, :], dst[:, t, :], src[:, t, :], ALU.add)


def build(nc, a, out):
    with ExitStack() as stack:
        s = Scope(nc, stack)

        SEMAPHORES.clear()

        class Kept:
            ident32 = s.sb("ident32", [P, P], F32)
            ident16 = s.sb("ident16", [P, P], F16)
            ones = s.sb("ones", [P, P], F16)
            iota = s.sb("iota", [P, E], F32)
            acc = s.sb("acc_rows", [P, TT, H], F32)

        k = Kept
        constants(nc, k)
        with ExitStack() as inner:
            g = Scope(nc, inner)
            k.zT = g.sb("xT", [P, 2, KC, T], F16)
            with ExitStack() as first:
                x = Scope(nc, first).sb("x_rows", [P, TT, H], F32)
                load_rows(nc, a["x"], x, "x")
                transpose_split(nc, k, x, "x")
            wg = g.sb("wg", [P, 2, KC, GE, M], F16)
            wu = g.sb("wu", [P, 2, KC, GE, M], F16)
            wd = g.sb("wd", [P, 2, GE, H], F16)
            wr = g.sb("wr", [P, 2, KC, E], F16)
            W = g.sb("W", [P, GE, TT], F32)
            jobs = []
            for w, name, shared in ((wg, "L0_cond_w_gate", "L0_cond_sw_gate"), (wu, "L0_cond_w_up", "L0_cond_sw_up")):
                for kc in range(KC):
                    jobs.append((a[name][:, kc * P:(kc + 1) * P, :].rearrange("e p m -> p e m"),
                                 w[:, HI, kc, 0:E, :], w[:, LO, kc, 0:E, :]))
                    jobs.append((a[shared][kc * P:(kc + 1) * P, :].rearrange("p (e m) -> p e m", e=NS),
                                 w[:, HI, kc, E:GE, :], w[:, LO, kc, E:GE, :]))
            jobs.append((a["L0_cond_w_down"].rearrange("e m h -> m e h"), wd[:, HI, 0:E, :], wd[:, LO, 0:E, :]))
            jobs.append((a["L0_cond_sw_down"].rearrange("(e m) h -> m e h", e=NS), wd[:, HI, E:GE, :], wd[:, LO, E:GE, :]))
            split_weights(nc, jobs, "gated_w", 2048)
            gated_router_weights(nc, k, a["L0_cond_wt"], wr, W)
            routing(nc, k, "gated_router", wr, (a["cond_64"], a["L0_cond_wg"]), None, 0.5, (1e-20, ALU.add), W)
            gated_experts(nc, k, wg, wu, wd, W, k.acc)
        end_of_part(nc)
        with ExitStack() as inner:
            g = Scope(nc, inner)
            qd = nc.dram_tensor("query_parts", (2, H, T), F16, kind="Internal").ap()
            kd = nc.dram_tensor("key_parts", (2, H, T), F16, kind="Internal").ap()
            V = g.sb("V", [P, TT, NH, 2 * D + 1], F16)
            with ExitStack() as first:
                f = Scope(nc, first)
                k.zT = f.sb("yT", [P, 2, KC, T], F16)
                transpose_split(nc, k, k.acc, "y")
                wq, wk, wv = (f.sb(n, [P, 2, KC, H], F16) for n in ("wq", "wk", "wv"))
                turned_weights(nc, k, [(a["L0_attn_Wq"], wq), (a["L0_attn_Wk"], wk), (a["L0_attn_Wv"], wv)], "qkv")
                queries_keys(nc, k, [(wq, a["L0_attn_bq"], 1.0, qd), (wk, a["L0_attn_bk"], D ** -0.5, kd)])
                values(nc, k, wv, a["L0_attn_bv"], V)
            with ExitStack() as main:
                f = Scope(nc, main)
                RS = f.sb("RS", [RK + 1, 2, RW], F16)
                quarter = f.sb("quarter", [RK, 4], F16)
                half = f.sb("half", [RK, 2], F16)
                Q = f.sb("Q", [RK, NH, LP], F16)
                KT = f.sb("KT", [RK, NH // 2, S], F16)
                relative_rows(nc, k, a["L0_attn_rel_emb"], RS, half, quarter)
                for b in range(B):
                    relative_operands(nc, b, qd, kd, Q, KT)
                    relative_attention(nc, k, b, Q, KT, RS, half, quarter, V, k.acc[:].rearrange("p t h -> p (t h)"))
        k.x = s.sb("x_rows_again", [P, TT, H], F32)
        load_rows(nc, a["x"], k.x, "x_again")
        with ExitStack() as inner:
            g = Scope(nc, inner)
            wo = g.sb("wo", [P, 2, KC, H], F16)
            k.zT = g.sb("oT", [P, 2, KC, T], F16)
            turned_weights(nc, k, [(a["L0_attn_Wo"], wo)], "wo")
            transpose_split(nc, k, k.acc, "o")
            output_rows(nc, k, wo, a["L0_attn_bo"], k.x, "attn_out")
        end_of_part(nc)
        with ExitStack() as inner:
            g = Scope(nc, inner)
            q_d = nc.dram_tensor("unit_queries", (QH, P, T), F16, kind="Internal").ap()
            table_d = nc.dram_tensor("bias_tables", (QH, P, TL), F32, kind="Internal").ap()
            null_d = nc.dram_tensor("null_bias_less_bound", (QH, 1), F32, kind="Internal").ap()
            KT = g.sb("causal_KT", [P, 2, T], F16)
            V = g.sb("causal_V", [P, TT, VW], F16)
            side = g.sb("key_mask", [P, TT], F32)
            null = g.sb("null_probs", [P, QH, TT], F32)
            wout = g.sb("wout", [P, 2, 8, H], F16)
            with ExitStack() as first:
                f = Scope(nc, first)
                wq = f.sb("c_wq", [P, 2, KC, QI], F16)
                wkv = f.sb("c_wkv", [P, 2, KC, 2 * QD], F16)
                w1 = f.sb("c_w1", [P, 2, KC, H], F16)
                w2 = f.sb("c_w2", [P, 2, KC, QH], F16)
                table = f.sb("bias_table", [QH, TL], F32)
                hp = f.sb("pos_hidden", [P, RT, H], F32)
                k.zT = f.sb("c_zT", [P, 2, KC, T], F16)
                chunked = lambda name, c: a[name].rearrange("(c p) n -> p c n", p=P)
                split_weights(nc, [(chunked(n, 0), w[:, HI], w[:, LO]) for n, w in (
                    ("L0_cond2_w1", w1), ("L0_cond2_w2", w2), ("L0_cond2_Wq", wq), ("L0_cond2_Wkv", wkv),
                    ("L0_cond2_Wout", wout))], "causal_w", 2048)
                position_rows(nc, a["L0_cond2_w0"], a["L0_cond2_b0"], hp)
                layer_norm(nc, hp, hp, RT, a["L0_cond2_g0"], None, "pos_ln0", silu=True)
                transpose_split(nc, k, hp, "pos0", RT)
                output_rows(nc, k, w1, a["L0_cond2_b1"], hp, "pos1", RT, add=False)
                layer_norm(nc, hp, hp, RT, a["L0_cond2_g1"], None, "pos_ln1", silu=True)
                transpose_split(nc, k, hp, "pos2", RT)
                bias_table(nc, k, w2, a["L0_cond2_b2"], a["L0_cond2_q_scale"], a["L0_cond2_k_scale"],
                           a["L0_cond2_null_attn_bias"], table, null_d)
                layer_norm(nc, k.x, k.acc, TT, a["L0_cond2_g_norm"], None, "ln_in")
                transpose_split(nc, k, k.acc, "xn")
                causal_operands(nc, k, wq, wkv, a, table, table_d, q_d, KT, V, side,
                                (null[:].rearrange("p h t -> p t h"), null_d))
            with ExitStack() as main:
                f = Scope(nc, main)
                o = f.sb("causal_o", [P, TT, QI], F32)
                causal_attention(nc, k, table_d, q_d, KT, V, side, null, a["cond_64"][1:2, :], o)
                causal_output(nc, k, o, wout, k.acc)
            layer_norm(nc, k.acc, k.acc, TT, a["L0_cond2_g_out"], None, "ln_out")
        end_of_part(nc)
        with ExitStack() as inner:
            g = Scope(nc, inner)
            w1 = g.sb("f_w1", [P, 2, KC, E, F], F16)
            w2 = g.sb("f_w2", [P, 2, E * FC, H], F16)
            wr = g.sb("f_wr", [P, 2, KC, E], F16)
            b1T = g.sb("f_b1T", [P, E * FC], F32)
            W = g.sb("f_W", [P, E, TT], F32)
            k.zT = g.sb("f_zT", [P, 2, KC, T], F16)
            jobs = []
            for kc in range(KC):
                for h in range(2):
                    es = slice(4 * h, 4 * h + 4)
                    jobs.append((a["L0_ffn_W1"][es, kc * P:(kc + 1) * P, :].rearrange("e p f -> p e f"),
                                 w1[:, HI, kc, es, :], w1[:, LO, kc, es, :]))
            for h in range(4):
                es = slice(8 * h, 8 * h + 8)
                jobs.append((a["L0_ffn_W2"].rearrange("e (c p) h -> p (e c) h", p=P)[:, es, :],
                             w2[:, HI, es, :], w2[:, LO, es, :]))
            jobs.append((a["L0_ffn_rW"].rearrange("(c p) e -> p c e", p=P), wr[:, HI], wr[:, LO]))
            split_weights(nc, jobs, "ffn_w", 2048)
            add_rows(nc, k.acc, k.x)
            layer_norm(nc, k.acc, k.acc, TT, a["L0_ffn_ln_g"], a["L0_ffn_ln_b"], "ln_ffn")
            transpose_split(nc, k, k.acc, "z")
            routing(nc, k, "gelu_router", wr, None, a["L0_ffn_rb"], 1.0, (1e-8, ALU.max), W)
            gelu_operands(nc, k, a["L0_ffn_b1"], a["L0_ffn_b2"], W, b1T, k.x)
            gelu_experts(nc, k, w1, w2, b1T, W, k.x)
        store_rows(nc, k.x, out)


def kernel(**inputs):
    import numpy as _np
    import concourse.bacc as _bacc
    from concourse import mybir as _mybir
    from concourse.bass_utils import run_bass_kernel_spmd as _run

    nc = _bacc.Bacc("TRN2", target_bir_lowering=False, num_devices=1)
    arrays, args = {}, {}
    for name, value in inputs.items():
        v = _np.ascontiguousarray(value)
        if v.dtype == _np.bool_:
            v = v.view(_np.uint8)
        arrays["in_" + name] = v
        args[name] = nc.dram_tensor("in_" + name, v.shape, _mybir.dt.from_np(v.dtype), kind="ExternalInput").ap()
    out = nc.dram_tensor("out", (B, S, H), F32, kind="ExternalOutput").ap()
    build(nc, args, out)
    r = _run(nc, [arrays], core_ids=[0])
    return r.results[0]["out"]
```

```python
from contextlib import ExitStack

import concourse.bass as bass
from concourse import mybir

F32 = mybir.dt.float32
F16 = mybir.dt.float16
U32 = mybir.dt.uint32
U8 = mybir.dt.uint8
ALU = mybir.AluOpType
ACT = mybir.ActivationFunctionType
X = mybir.AxisListType.X

P = 128
B, S, H = 2, 1024, 256
T = B * S
TT = T // P
KC = H // P
E = 8
M = 128
NS = 2
GE = E + NS
F = 512
FC = F // P
TC = T // 512
HI, LO = 0, 1
PRODUCTS = ((HI, HI), (HI, LO), (LO, HI))


class Scope:

    def __init__(self, nc, stack, prefix=""):
        self.nc, self.stack, self.prefix = nc, stack, prefix

    def sb(self, name, shape, dt):
        return self.stack.enter_context(self.nc.sbuf_tensor(self.prefix + name, shape, dt))

    def banks(self, name, n, dt=F32):
        return self.stack.enter_context(self.nc.psum_tensor(self.prefix + name, [P, n, 2048 // (4 if dt == F32 else 2)], dt))

    def sem(self, name):
        sem = self.nc.alloc_semaphore(self.prefix + name)
        SEMAPHORES.append(sem)
        return sem


SEMAPHORES = []


def end_of_part(nc):
    nc.clear_and_free_semaphores(list(SEMAPHORES))
    SEMAPHORES.clear()
    nc.all_engine_barrier()


class Chain:

    def __init__(self, eng, sem):
        self.eng, self.sem, self.base, self.n = eng, sem, 0, 0

    def __call__(self, ins):
        self.n += 1
        ins.then_inc(self.sem, 1)
        self.eng.wait_ge(self.sem, self.base + self.n)


def part(i):
    return slice(i, i + 1)


def constants(nc, k):
    with ExitStack() as stack:
        s = Scope(nc, stack)
        blank = s.sem("blank")
        made = s.sem("constants_made")
        with nc.Block() as block:
            @block.gpsimd
            def _(pool):
                pool.memset(k.ident32[:], 0.0).then_inc(blank, 1)
                pool.memset(k.ones[:], 1.0).then_inc(made, 1)
                pool.iota(k.iota[:], [[1, E]], 0, 0, True).then_inc(made, 1)
                pool.wait_ge(blank, 1)
                pool.affine_select(out=k.ident32[:], in_=k.ident32[:], compare_op=ALU.not_equal, fill=1.0,
                                   base=0, pattern=[[-1, P]], channel_multiplier=1).then_inc(blank, 1)
                pool.wait_ge(blank, 2)
                pool.tensor_copy(k.ident16[:], k.ident32[:]).then_inc(made, 1)
                pool.wait_ge(made, 3)


def transpose_split(nc, k, src, name, tiles=TT):
    with ExitStack() as stack:
        s = Scope(nc, stack)
        ps = s.banks(name + "_ps", 4)
        turned = s.sem(name + "_turned")
        hi_done = s.sem(name + "_hi_done")
        lo_done = s.sem(name + "_lo_done")
        G = tiles // 2
        with nc.Block() as block:
            @block.tensor
            def _(pe):
                for g in range(G):
                    if g >= 4:
                        pe.wait_ge(lo_done, g - 3)
                    for kc in range(KC):
                        for a in range(2):
                            last = nc.tensor.transpose(ps[:, g % 4, (kc * 2 + a) * P:(kc * 2 + a + 1) * P],
                                                       src[:, 2 * g + a, kc * P:(kc + 1) * P], k.ident32[:])
                    last.then_inc(turned, 1)

            @block.scalar
            def _(act):
                for g in range(G):
                    act.wait_ge(turned, g + 1)
                    nc.scalar.copy(k.zT[:, HI, :, g * 2 * P:(g + 1) * 2 * P],
                                   ps[:, g % 4, :].rearrange("p (c t) -> p c t", c=KC)).then_inc(hi_done, 1)

            @block.vector
            def _(dve):
                for g in range(G):
                    dve.wait_ge(hi_done, g + 1)
                    nc.vector.tensor_tensor(k.zT[:, LO, :, g * 2 * P:(g + 1) * 2 * P],
                                            ps[:, g % 4, :].rearrange("p (c t) -> p c t", c=KC),
                                            k.zT[:, HI, :, g * 2 * P:(g + 1) * 2 * P],
                                            ALU.subtract).then_inc(lo_done, 1)


class WeightJobs:

    def __init__(self, nc, s, jobs, buffers=2):
        self.nc, self.jobs, self.begun, self.n = nc, jobs, 0, buffers
        if jobs:
            self.stage = s.sb("weight_stage", [P, buffers, 2048], F32)
            self.loaded = [s.sem(f"weights_loaded{i}") for i in range(buffers)]
            self.hi_done = s.sem("weights_hi_done")
            self.lo_done = [s.sem(f"weights_lo_done{i}") for i in range(2)]

    def staged(self, n):
        p, *rest = self.jobs[n][1].shape
        size = rest[0] * (rest[1] if len(rest) == 2 else 1)
        flat = self.stage[0:p, n % self.n, 0:size]
        return flat.rearrange("p (a b) -> p a b", a=rest[0]) if len(rest) == 2 else flat

    def load(self, sp):
        for n, (src, _, _) in enumerate(self.jobs):
            if n >= self.n:
                sp.wait_ge(self.lo_done[n % 2], (n - self.n) // 2 + 1)
            sp.dma_start(self.staged(n), src).then_inc(self.loaded[n % self.n], 16)

    def hi(self, act, last=None):
        end = len(self.jobs) if last is None else min(last + 1, len(self.jobs))
        for n in range(self.begun, end):
            act.wait_ge(self.loaded[n % self.n], 16 * (n // self.n + 1))
            self.nc.scalar.copy(self.jobs[n][1], self.staged(n)).then_inc(self.hi_done, 1)
        self.begun = max(self.begun, end)

    def lo_even(self, pool):
        for n, (_, hi, lo) in list(enumerate(self.jobs))[0::2]:
            pool.wait_ge(self.hi_done, n + 1)
            self.nc.gpsimd.tensor_tensor(lo, self.staged(n), hi, ALU.subtract).then_inc(self.lo_done[0], 1)

    def lo_odd(self, dve):
        for n, (_, hi, lo) in list(enumerate(self.jobs))[1::2]:
            dve.wait_ge(self.hi_done, n + 1)
            self.nc.vector.tensor_tensor(lo, self.staged(n), hi, ALU.subtract).then_inc(self.lo_done[1], 1)


def split_weights(nc, jobs, name, width=4096):
    with ExitStack() as stack:
        s = Scope(nc, stack)
        stage = s.sb(name + "_stage", [P, 2, width], F32)
        loaded = [s.sem(f"{name}_loaded{i}") for i in range(2)]
        hi_done = s.sem(name + "_hi_done")
        lo_done = s.sem(name + "_lo_done")

        def staged(n):
            shape = jobs[n][1].shape
            p, rest = shape[0], shape[1:]
            size = 1
            for x in rest:
                size *= x
            flat = stage[0:p, n % 2, 0:size]
            if len(rest) == 2:
                flat = flat.rearrange("p (a b) -> p a b", a=rest[0])
            return flat

        with nc.Block() as block:
            @block.sync
            def _(sp):
                for n, (src, _, _) in enumerate(jobs):
                    if n >= 2:
                        sp.wait_ge(lo_done, n - 1)
                    sp.dma_start(staged(n), src).then_inc(loaded[n % 2], 16)

            @block.scalar
            def _(act):
                for n, (_, hi, _) in enumerate(jobs):
                    act.wait_ge(loaded[n % 2], 16 * (n // 2 + 1))
                    nc.scalar.copy(hi, staged(n)).then_inc(hi_done, 1)

            @block.vector
            def _(dve):
                for n, (_, hi, lo) in enumerate(jobs):
                    dve.wait_ge(loaded[n % 2], 16 * (n // 2 + 1))
                    dve.wait_ge(hi_done, n + 1)
                    nc.vector.tensor_tensor(lo, staged(n), hi, ALU.subtract).then_inc(lo_done, 1)


def routing(nc, k, name, wr, gate, rb, scale, finish, W):
    with ExitStack() as stack:
        s = Scope(nc, stack)
        ps = s.banks(name + "_ps", 2)
        L = s.sb(name + "_L", [P, TT, E], F32)
        pm = s.sb(name + "_pm", [P, TT, E], F32)
        mask2 = s.sb(name + "_mask2", [P, TT, E], F32)
        best = s.sb(name + "_best", [P, TT, 8], F32)
        idx = s.sb(name + "_idx", [P, TT, 8], U32)
        idxf = s.sb(name + "_idxf", [P, TT, 8], F32)
        col = s.sb(name + "_col", [P, 4, TT], F32)
        gsb = s.sb(name + "_g", [B, 64], F32)
        wsb = s.sb(name + "_w", [E, 64], F32)
        gT = s.sb(name + "_gT", [64, B, P], F32)
        wT = s.sb(name + "_wT", [64, E], F32)
        rbr = s.sb(name + "_rb", [1, E], F32)
        ones32 = s.sb(name + "_ones", [1, P], F32)
        loaded = s.sem(name + "_loaded")
        turned = s.sem(name + "_turned")
        ready = s.sem(name + "_rows_ready")
        logits = s.sem(name + "_logits")
        centred = s.sem(name + "_centred")
        exps = s.sem(name + "_exps")
        steps = s.sem(name + "_steps")
        with nc.Block() as block:
            @block.sync
            def _(sp):
                if gate:
                    sp.dma_start(gsb[:], gate[0]).then_inc(loaded, 16)
                    sp.dma_start(wsb[:], gate[1]).then_inc(loaded, 16)
                else:
                    sp.dma_start(rbr[:], rb.rearrange("(a e) -> a e", a=1)).then_inc(loaded, 16)
                    sp.wait_ge(loaded, 16)

            @block.tensor
            def _(pe):
                if gate:
                    pe.wait_ge(loaded, 32)
                    nc.tensor.transpose(ps[0:64, 1, 0:B], gsb[:], k.ident32[0:B, 0:B])
                    nc.tensor.transpose(ps[0:64, 1, 16:16 + E], wsb[:], k.ident32[0:E, 0:E]).then_inc(turned, 1)
                else:
                    pe.wait_ge(loaded, 16)
                pe.wait_ge(ready, 1)
                for tt in range(TT):
                    out = ps[:, 0, tt * E:(tt + 1) * E]
                    n = 0
                    for a, b in PRODUCTS:
                        for kc in range(KC):
                            nc.tensor.matmul(out, k.zT[:, a, kc, tt * P:(tt + 1) * P], wr[:, b, kc, :],
                                             start=(n == 0), stop=False)
                            n += 1
                    if gate:
                        last = nc.tensor.matmul(out, gT[:, tt * P // S, :], wT[:], start=False, stop=True)
                    else:
                        last = nc.tensor.matmul(out, ones32[:], rbr[:], start=False, stop=True)
                last.then_inc(logits, 1)

            @block.scalar
            def _(act):
                act.wait_ge(centred, 1)
                nc.scalar.activation(L[:], L[:], ACT.Exp).then_inc(exps, 1)

            @block.vector
            def _(dve):
                link = Chain(dve, steps)
                if gate:
                    dve.wait_ge(turned, 1)
                    link(nc.vector.tensor_copy(gT[:], ps[0:64, 1, 0:B].unsqueeze(2).broadcast_to([64, B, P])))
                    nc.vector.tensor_copy(wT[:], ps[0:64, 1, 16:16 + E]).then_inc(ready, 1)
                else:
                    nc.vector.memset(ones32[:], 1.0).then_inc(ready, 1)
                wide = lambda c: col[:, c, :].unsqueeze(2).broadcast_to([P, TT, E])
                dve.wait_ge(logits, 1)
                link(nc.vector.tensor_scalar(L[:], ps[:, 0, 0:TT * E].rearrange("p (t e) -> p t e", e=E),
                                             scale, None, ALU.mult))
                link(nc.vector.tensor_reduce(col[:, 0, :], L[:], X, ALU.max))
                nc.vector.tensor_tensor(L[:], L[:], wide(0), ALU.subtract).then_inc(centred, 1)
                dve.wait_ge(exps, 1)
                link(nc.vector.tensor_reduce(col[:, 1, :], L[:], X, ALU.add))
                link(nc.vector.reciprocal(col[:, 2, :], col[:, 1, :]))
                link(nc.vector.tensor_tensor(L[:], L[:], wide(2), ALU.mult))
                for tt in range(TT):
                    nc.vector.max(best[:, tt, :], L[:, tt, :]).then_inc(steps, 1)
                link.n += TT
                dve.wait_ge(steps, link.n)
                for tt in range(TT):
                    nc.vector.max_index(idx[:, tt, :], best[:, tt, :], L[:, tt, :]).then_inc(steps, 1)
                link.n += TT
                dve.wait_ge(steps, link.n)
                link(nc.vector.tensor_copy(idxf[:], idx[:]))
                lane = k.iota[:].unsqueeze(1).broadcast_to([P, TT, E])
                link(nc.vector.tensor_tensor(pm[:], lane, idxf[:, :, 0:1].broadcast_to([P, TT, E]), ALU.is_equal))
                link(nc.vector.tensor_tensor(mask2[:], lane, idxf[:, :, 1:2].broadcast_to([P, TT, E]), ALU.is_equal))
                link(nc.vector.tensor_tensor(pm[:], pm[:], mask2[:], ALU.add))
                link(nc.vector.tensor_tensor(pm[:], pm[:], L[:], ALU.mult))
                link(nc.vector.tensor_reduce(col[:, 3, :], pm[:], X, ALU.add))
                link(nc.vector.tensor_scalar(col[:, 3, :], col[:, 3, :], finish[0], None, finish[1]))
                link(nc.vector.reciprocal(col[:, 2, :], col[:, 3, :]))
                link(nc.vector.tensor_tensor(W[:, 0:E, :].rearrange("p e t -> p t e"), pm[:], wide(2), ALU.mult))


def block_col(w, e, width):
    if isinstance(e, int):
        return w[:, e, :]
    return w.rearrange("p e n -> p (e n)")[:, bass.ds(e * width, width)]


def expert_weight(W, e, t):
    if isinstance(e, int):
        return W[:, e, t:t + 1]
    return W[:].rearrange("p e t -> p (e t)")[:, bass.ds(e * TT + t, 1)]


def load_rows(nc, src, rows, name, jobs=(), arrived=None):
    with ExitStack() as stack:
        s = Scope(nc, stack, name + "_")
        loaded = s.sem("loaded") if arrived is None else arrived
        weights = WeightJobs(nc, s, jobs, 4)
        with nc.Block() as block:
            @block.sync
            def _(sp):
                sp.dma_start(rows[:], src.rearrange("b (t p) h -> p (b t) h", p=P)).then_inc(loaded, 16)
                weights.load(sp)
                if arrived is None:
                    sp.wait_ge(loaded, 16)

            @block.scalar
            def _(act):
                weights.hi(act)

            @block.gpsimd
            def _(pool):
                weights.lo_even(pool)

            @block.vector
            def _(dve):
                weights.lo_odd(dve)


def store_rows(nc, rows, out):
    with ExitStack() as stack:
        stored = Scope(nc, stack).sem("rows_stored")
        with nc.Block() as block:
            @block.sync
            def _(sp):
                sp.dma_start(out.rearrange("b (t p) h -> p (b t) h", p=P), rows[:]).then_inc(stored, 16)
                sp.wait_ge(stored, 16)


def gated_router_weights(nc, k, wt, wr, W):
    with ExitStack() as stack:
        s = Scope(nc, stack)
        ps = s.banks("wt_ps", 1)
        rows = s.sb("wt_rows", [E, H], F32)
        loaded = s.sem("wt_loaded")
        turned = s.sem("wt_turned")
        hi_done = s.sem("wt_hi_done")
        with nc.Block() as block:
            @block.sync
            def _(sp):
                sp.dma_start(rows[:], wt).then_inc(loaded, 16)

            @block.tensor
            def _(pe):
                pe.wait_ge(loaded, 16)
                for kc in range(KC):
                    last = nc.tensor.transpose(ps[:, 0, kc * E:(kc + 1) * E], rows[:, kc * P:(kc + 1) * P],
                                               k.ident32[0:E, 0:E])
                last.then_inc(turned, 1)

            @block.vector
            def _(dve):
                nc.vector.memset(W[:, E:GE, :], 1.0)
                turned_w = ps[:, 0, 0:KC * E].rearrange("p (c e) -> p c e", c=KC)
                dve.wait_ge(turned, 1)
                nc.vector.tensor_copy(wr[:, HI, :, :], turned_w).then_inc(hi_done, 1)
                dve.wait_ge(hi_done, 1)
                nc.vector.tensor_tensor(wr[:, LO, :, :], turned_w, wr[:, HI, :, :], ALU.subtract)


def gated_experts(nc, k, wg, wu, wd, W, acc):
    with ExitStack() as stack:
        s = Scope(nc, stack)
        pg = s.banks("gate_ps", 2)
        pu = s.banks("up_ps", 2)
        py = s.banks("down_ps", 4)
        small = s.sb("gate_small", [P, 2, 512], F32)
        leaky = s.sb("gate_leaky", [P, 2, 512], F32)
        prod = s.sb("gate_prod", [P, 2, 512], F32)
        parts = s.sb("gate_parts", [P, 2, 2, 512], F16)
        hid_ready = s.sem("hid_ready")
        small_ready = s.sem("small_ready")
        leaky_ready = s.sem("leaky_ready")
        prod_ready = s.sem("prod_ready")
        hi_ready = s.sem("prod_hi_ready")
        lo_ready = s.sem("prod_lo_ready")
        down_ready = s.sem("down_ready")
        down_free = s.sem("down_banks_free")
        cleared = s.sem("acc_cleared")
        with nc.Block() as block:
            @block.tensor
            def _(pe):
                pe.sem_inc(down_ready, 8)

                def hidden(e, c):
                    n = TC * e + c
                    pe.wait_ge(prod_ready, n + 1)
                    for bank, w in ((pg, wg), (pu, wu)):
                        i = 0
                        for a, b in PRODUCTS:
                            for kc in range(KC):
                                last = nc.tensor.matmul(bank[:, c % 2, :], block_col(w[:, a, kc], e, M),
                                                        k.zT[:, b, kc, c * 512:(c + 1) * 512],
                                                        start=(i == 0), stop=(i == 5))
                                i += 1
                    last.then_inc(hid_ready, 1)

                def down(e, c):
                    n = TC * e + c
                    pe.wait_ge(hi_ready, n + 1)
                    pe.wait_ge(lo_ready, n + 3)
                    for j in range(4):
                        pe.wait_ge(down_free, 4 * n + j + 1)
                        for i, (a, b) in enumerate(PRODUCTS):
                            last = nc.tensor.matmul(py[:, j, 0:H], parts[:, c % 2, a, j * P:(j + 1) * P],
                                                    block_col(wd[:, b], e, H), start=(i == 0), stop=(i == 2))
                        last.then_inc(down_ready, 1)

                def block_of(e, following):
                    for c in range(TC):
                        if c + 1 < TC:
                            hidden(e, c + 1)
                        elif following is not None:
                            hidden(following, 0)
                        down(e, c)

                hidden(0, 0)
                with pe.Fori(0, GE - 1) as e:
                    block_of(e, e + 1)
                block_of(GE - 1, None)

            @block.scalar
            def _(act):
                with act.Fori(0, GE) as e:
                    for c in range(TC):
                        n = TC * e + c
                        act.wait_ge(hid_ready, n + 1)
                        act.wait_ge(prod_ready, n + 1)
                        nc.scalar.mul(small[:, c % 2, :], pg[:, c % 2, :], 0.01).then_inc(small_ready, 1)
                        act.wait_ge(prod_ready, n + 3)
                        act.wait_ge(down_ready, 4 * n + 4)
                        nc.scalar.copy(parts[:, c % 2, HI, :], prod[:, c % 2, :]).then_inc(hi_ready, 1)

            @block.gpsimd
            def _(pool):
                pool.sem_inc(lo_ready, 2)
                with pool.Fori(0, GE) as e:
                    for c in range(TC):
                        n = TC * e + c
                        pool.wait_ge(hi_ready, n + 1)
                        nc.gpsimd.tensor_tensor(parts[:, c % 2, LO, :], prod[:, c % 2, :],
                                                parts[:, c % 2, HI, :], ALU.subtract).then_inc(lo_ready, 1)

            @block.vector
            def _(dve):
                dve.sem_inc(prod_ready, 2)
                dve.sem_inc(down_free, 4)
                nc.vector.memset(acc[:], 0.0).then_inc(cleared, 1)
                dve.wait_ge(cleared, 1)

                def product(e, c):
                    n = TC * e + c
                    dve.wait_ge(small_ready, n + 1)
                    nc.vector.tensor_tensor(leaky[:, c % 2, :], pg[:, c % 2, :], small[:, c % 2, :],
                                            ALU.max).then_inc(leaky_ready, 1)
                    dve.wait_ge(leaky_ready, n + 1)
                    dve.wait_ge(lo_ready, n + 1)
                    nc.vector.tensor_tensor(prod[:, c % 2, :], pu[:, c % 2, :], leaky[:, c % 2, :],
                                            ALU.mult).then_inc(prod_ready, 1)

                def weigh(e, c):
                    n = TC * e + c
                    for j in range(4):
                        t = 4 * c + j
                        dve.wait_ge(down_ready, 8 + 4 * n + j + 1)
                        nc.vector.scalar_tensor_tensor(out=acc[:, t, :], in0=py[:, j, 0:H],
                                                       scalar=expert_weight(W, e, t), in1=acc[:, t, :],
                                                       op0=ALU.mult, op1=ALU.add).then_inc(down_free, 1)

                def block_of(e, following):
                    for c in range(TC):
                        if c + 1 < TC:
                            product(e, c + 1)
                        elif following is not None:
                            product(following, 0)
                        weigh(e, c)

                product(0, 0)
                with dve.Fori(0, GE - 1) as e:
                    block_of(e, e + 1)
                block_of(GE - 1, None)


NH = 16
D = H // NH
RT = S // P
LB = 32
QT = P // LB
REL = 1023
RK = 2 * 3 * D
AHEAD = 3
LP = S + AHEAD * LB
WIN = S + LB - 2
RW = 2 * S + AHEAD * LB
QPARTS = (HI, HI, LO)
FOUR = (0, 1, 3, 4)
KPARTS = (HI, LO, HI)


def turned_weights(nc, k, jobs, name):
    with ExitStack() as stack:
        s = Scope(nc, stack)
        ps = s.banks(name + "_wturn_ps", len(jobs))
        rows = s.sb(name + "_wturn_rows", [P, len(jobs), KC, H], F32)
        loaded = s.sem(name + "_wturn_loaded")
        turned = s.sem(name + "_wturn_turned")
        hi_done = s.sem(name + "_wturn_hi_done")
        with nc.Block() as block:
            @block.sync
            def _(sp):
                for n, (src, _) in enumerate(jobs):
                    sp.dma_start(rows[:, n], src.rearrange("(c p) d -> p c d", p=P)).then_inc(loaded, 16)

            @block.tensor
            def _(pe):
                pe.wait_ge(loaded, 16 * len(jobs))
                for n in range(len(jobs)):
                    for dc in range(KC):
                        for ec in range(KC):
                            last = nc.tensor.transpose(ps[:, n, dc * H + ec * P:dc * H + (ec + 1) * P],
                                                       rows[:, n, ec, dc * P:(dc + 1) * P], k.ident32[:])
                    last.then_inc(turned, 1)

            @block.scalar
            def _(act):
                for n, (_, w) in enumerate(jobs):
                    act.wait_ge(turned, n + 1)
                    nc.scalar.copy(w[:, HI], ps[:, n, :].rearrange("p (c e) -> p c e", c=KC)).then_inc(hi_done, 1)

            @block.vector
            def _(dve):
                for n, (_, w) in enumerate(jobs):
                    dve.wait_ge(hi_done, n + 1)
                    nc.vector.tensor_tensor(w[:, LO], ps[:, n, :].rearrange("p (c e) -> p c e", c=KC),
                                            w[:, HI], ALU.subtract)


def queries_keys(nc, k, jobs):
    with ExitStack() as stack:
        s = Scope(nc, stack)
        ps = s.banks("proj_ps", 4)
        bias = s.sb("proj_bias", [P, 2, KC], F32)
        full = s.sb("proj_full", [P, 4, 512], F32)
        parts = s.sb("proj_parts", [P, 2, 2, KC, T], F16)
        loaded = s.sem("proj_loaded")
        scaled = s.sem("proj_bias_scaled")
        ready = s.sem("proj_ready")
        full_ready = s.sem("proj_full_ready")
        hi_done = s.sem("proj_hi_done")
        lo_done = s.sem("proj_lo_done")
        stored = s.sem("proj_stored")
        steps = [(j, ec, c) for j in range(2) for ec in range(KC) for c in range(TC)]
        with nc.Block() as block:
            @block.sync
            def _(sp):
                for j, (_, b, _, _) in enumerate(jobs):
                    sp.dma_start(bias[:, j, :], b.rearrange("(c p) -> p c", p=P),
                                 allow_slow_non_contiguous=True).then_inc(loaded, 16)
                for j, (_, _, _, dst) in enumerate(jobs):
                    sp.wait_ge(lo_done, 8 * (j + 1))
                    sp.wait_ge(hi_done, 8 * (j + 1))
                    for hl in range(2):
                        sp.dma_start(dst[hl].rearrange("(c p) t -> p c t", p=P), parts[:, j, hl]).then_inc(stored, 16)
                sp.wait_ge(stored, 64)

            @block.tensor
            def _(pe):
                for n, (j, ec, c) in enumerate(steps):
                    if n >= 4:
                        pe.wait_ge(full_ready, n - 3)
                    i = 0
                    for a, b in PRODUCTS:
                        for kc in range(KC):
                            last = nc.tensor.matmul(ps[:, n % 4, :], jobs[j][0][:, a, kc, ec * P:(ec + 1) * P],
                                                    k.zT[:, b, kc, c * 512:(c + 1) * 512],
                                                    start=(i == 0), stop=(i == 5))
                            i += 1
                    last.then_inc(ready, 1)

            @block.scalar
            def _(act):
                act.wait_ge(scaled, 2)
                for n, (j, ec, c) in enumerate(steps):
                    act.wait_ge(ready, n + 1)
                    if n >= 4:
                        act.wait_ge(lo_done, n - 3)
                    nc.scalar.activation(full[:, n % 4, :], ps[:, n % 4, :], ACT.Identity,
                                         bias=bias[:, j, ec:ec + 1], scale=jobs[j][2]).then_inc(full_ready, 1)

            @block.vector
            def _(dve):
                dve.wait_ge(loaded, 32)
                for j in range(2):
                    nc.vector.tensor_scalar(bias[:, j, :], bias[:, j, :], jobs[j][2], None, ALU.mult).then_inc(scaled, 1)
                for n, (j, ec, c) in enumerate(steps):
                    dve.wait_ge(full_ready, n + 1)
                    cols = slice(c * 512, (c + 1) * 512)
                    nc.vector.tensor_copy(parts[:, j, HI, ec, cols], full[:, n % 4, :]).then_inc(hi_done, 1)
                    dve.wait_ge(hi_done, n + 1)
                    nc.vector.tensor_tensor(parts[:, j, LO, ec, cols], full[:, n % 4, :],
                                            parts[:, j, HI, ec, cols], ALU.subtract).then_inc(lo_done, 1)


def values(nc, k, wv, bv, V):
    with ExitStack() as stack:
        s = Scope(nc, stack)
        ps = s.banks("v_ps", 4)
        bias = s.sb("v_bias", [P, H], F32)
        full = s.sb("v_full", [P, 4, H], F32)
        loaded = s.sem("v_loaded")
        ready = s.sem("v_ready")
        full_ready = s.sem("v_full_ready")
        hi_done = s.sem("v_hi_done")
        lo_done = s.sem("v_lo_done")
        heads = lambda t: t.rearrange("p (h d) -> p h d", d=D)
        with nc.Block() as block:
            @block.sync
            def _(sp):
                sp.dma_start(bias[:], bv.rearrange("(a d) -> a d", a=1).broadcast_to([P, H])).then_inc(loaded, 16)

            @block.gpsimd
            def _(pool):
                pool.memset(V[:, :, :, 2 * D:2 * D + 1], 1.0)

            @block.tensor
            def _(pe):
                for t in range(TT):
                    if t >= 4:
                        pe.wait_ge(full_ready, t - 3)
                    i = 0
                    for a, b in PRODUCTS:
                        for kc in range(KC):
                            last = nc.tensor.matmul(ps[:, t % 4, 0:H], k.zT[:, a, kc, t * P:(t + 1) * P],
                                                    wv[:, b, kc, :], start=(i == 0), stop=(i == 5))
                            i += 1
                    last.then_inc(ready, 1)

            @block.scalar
            def _(act):
                for t in range(TT):
                    act.wait_ge(full_ready, t + 1)
                    nc.scalar.copy(V[:, t, :, 0:D], heads(full[:, t % 4, :])).then_inc(hi_done, 1)

            @block.vector
            def _(dve):
                dve.wait_ge(loaded, 16)
                for t in range(TT + 2):
                    if t < TT:
                        dve.wait_ge(ready, t + 1)
                        if t >= 4:
                            dve.wait_ge(lo_done, t - 3)
                        nc.vector.tensor_tensor(full[:, t % 4, :], ps[:, t % 4, 0:H], bias[:], ALU.add)\
                            .then_inc(full_ready, 1)
                    if t >= 2:
                        dve.wait_ge(hi_done, t - 1)
                        nc.vector.tensor_tensor(V[:, t - 2, :, D:2 * D], heads(full[:, (t - 2) % 4, :]),
                                                V[:, t - 2, :, 0:D], ALU.subtract).then_inc(lo_done, 1)


def relative_rows(nc, k, rel, RS, half, quarter):
    with ExitStack() as stack:
        s = Scope(nc, stack)
        ps = s.banks("rel_ps", 2)
        rows = s.sb("rel_rows", [P, 8, D], F32)
        full = s.sb("rel_full", [D, 2048], F32)
        parts = s.sb("rel_parts", [D, 2, 2048], F16)
        loaded = s.sem("rel_loaded")
        turned = s.sem("rel_turned")
        cleared = s.sem("rel_cleared")
        steps = s.sem("rel_steps")
        placed = s.sem("rel_placed")
        masks = s.sem("rel_masks")
        WRAP = 512
        with nc.Block() as block:
            @block.sync
            def _(sp):
                sp.dma_start(rows[:, 0:7, :], rel[0:7 * P, :].rearrange("(c p) d -> p c d", p=P)).then_inc(loaded, 16)
                sp.dma_start(rows[0:P - 1, 7, :], rel[7 * P:REL, :]).then_inc(loaded, 16)
                sp.wait_ge(steps, 5)
                sp.wait_ge(cleared, 2)
                for l in range(2):
                    for i, hl in enumerate(KPARTS):
                        r = (3 * l + i) * D
                        x = AHEAD * LB + 1 + l
                        sp.dma_start(RS[r:r + D, 0, x:RW], parts[:, hl, 0:2 * S - 1 - l]).then_inc(placed, 16)
                for l, group in enumerate(FOUR):
                    r = group * D
                    x = AHEAD * LB + 1 + l
                    sp.dma_start(RS[r:r + D, 1, x:RW], parts[:, HI, 0:2 * S - 1 - l]).then_inc(placed, 16)
                sp.wait_ge(placed, 10 * 16)

            @block.gpsimd
            def _(pool):
                pool.memset(RS[:], 0.0).then_inc(cleared, 1)
                pool.wait_ge(cleared, 1)
                pool.memset(RS[RK:RK + 1, 0, :], 1.0).then_inc(cleared, 1)
                pool.memset(quarter[:], 1.0).then_inc(masks, 1)
                pool.wait_ge(masks, 1)
                for l, group in enumerate(FOUR):
                    rows = quarter[:, l:l + 1]
                    pool.affine_select(out=rows, in_=rows, compare_op=ALU.is_ge, fill=0.0,
                                       base=-group * D, pattern=[[0, 1]], channel_multiplier=1).then_inc(masks, 1)
                    pool.wait_ge(masks, 2 * l + 2)
                    pool.affine_select(out=rows, in_=rows, compare_op=ALU.is_ge, fill=0.0,
                                       base=group * D + D - 1, pattern=[[0, 1]], channel_multiplier=-1).then_inc(masks, 1)
                    pool.wait_ge(masks, 2 * l + 3)
                pool.memset(half[:], 1.0).then_inc(masks, 1)
                pool.wait_ge(masks, 10)
                pool.affine_select(out=half[:, 0:1], in_=half[:, 0:1], compare_op=ALU.is_ge, fill=0.0,
                                   base=3 * D - 1, pattern=[[0, 1]], channel_multiplier=-1).then_inc(masks, 1)
                pool.affine_select(out=half[:, 1:2], in_=half[:, 1:2], compare_op=ALU.is_ge, fill=0.0,
                                   base=-3 * D, pattern=[[0, 1]], channel_multiplier=1).then_inc(masks, 1)

            @block.tensor
            def _(pe):
                pe.wait_ge(loaded, 32)
                for c in range(8):
                    n = P if c < 7 else P - 1
                    last = nc.tensor.transpose(ps[0:D, c // 4, (c % 4) * P:(c % 4) * P + n], rows[0:n, c, :],
                                               k.ident32[0:n, 0:n])
                last.then_inc(turned, 1)

            @block.vector
            def _(dve):
                link = Chain(dve, steps)
                dve.wait_ge(turned, 1)
                turned_rows = ps[0:D].rearrange("p a b -> p (a b)")
                end = WRAP + REL
                nc.vector.tensor_copy(full[:, 0:WRAP], turned_rows[:, REL - WRAP:REL]).then_inc(steps, 1)
                nc.vector.tensor_copy(full[:, WRAP:end], turned_rows[:, 0:REL]).then_inc(steps, 1)
                nc.vector.tensor_copy(full[:, end:], turned_rows[:, REL - 1:REL].broadcast_to([D, 2048 - end])).then_inc(steps, 1)
                link.n = 3
                dve.wait_ge(steps, 3)
                link(nc.vector.tensor_copy(parts[:, HI, :], full[:]))
                link(nc.vector.tensor_tensor(parts[:, LO, :], full[:], parts[:, HI, :], ALU.subtract))


def relative_operands(nc, b, qd, kd, Q, KT):
    with ExitStack() as stack:
        s = Scope(nc, stack, f"b{b}_")
        loaded = s.sem("ops_loaded")
        cleared = s.sem("ops_cleared")
        tok = slice(b * S, (b + 1) * S)
        with nc.Block() as block:
            @block.sync
            def _(sp):
                for half in range(2):
                    for i in range(3):
                        r = (3 * half + i) * D
                        sp.dma_start(Q[r:r + D, :, 0:S], qd[QPARTS[i], :, tok].rearrange("(h d) t -> d h t", d=D))\
                            .then_inc(loaded, 16)
                        sp.dma_start(KT[r:r + D, :, :], kd[KPARTS[i], :, tok].rearrange(
                            "(g two d) t -> two d g t", two=2, d=D)[half]).then_inc(loaded, 16)
                sp.wait_ge(loaded, 12 * 16)

            @block.gpsimd
            def _(pool):
                pool.memset(Q[:, :, S:LP], 0.0).then_inc(cleared, 1)
                pool.wait_ge(cleared, 1)


def relative_attention(nc, k, b, Q, KT, RS, half, quarter, V, o):
    with ExitStack() as stack:
        s = Scope(nc, stack, f"b{b}_")
        pm = s.banks("max_ps", 2)
        pz = s.banks("score_ps", 2)
        pv = s.banks("pv_ps", 2)
        pt = s.banks("turn_ps", 1)
        top = s.sb("top", [P, 2, 512], F32)
        peak = s.sb("peak", [P, QT], F32)
        negpeak = s.sb("negpeak", [P, QT], F16)
        full = s.sb("prob_full", [P, 4, 512], F32)
        probs = s.sb("probs", [P, 2, RT, NH, P], F16)
        inv = s.sb("inv", [P, 2, 8], F32)
        low = s.sb("low", [P, 2, 8, D], F32)
        mid = s.sb("mid", [P, 2, 8, D], F32)
        win = s.sb("table_windows", [RK + 1, QT, 2, WIN + 2], F16)
        qr = s.sb("step_q_rel", [RK + 1, QT, NH, LB], F16)
        q4 = s.sb("step_q_rel4", [RK, QT, NH, LB], F16)
        qk = s.sb("step_q_key", [RK, QT, NH, LB], F16)
        laid = s.sem("step_laid")
        win_loaded = [s.sem(f"window_loaded{u}") for u in range(QT)]
        raw_ready = s.sem("raw_ready")
        raw_free = s.sem("raw_taken")
        turned = s.sem("top_turned")
        peak_done = s.sem("peak_done")
        neg_ready = s.sem("negpeak_ready")
        row_made = s.sem("row_made")
        row_ready = s.sem("row_ready")
        score_ready = s.sem("score_ready")
        full_ready = s.sem("full_ready")
        cast_ready = s.sem("hi_cast_ready")
        lo_ready = s.sem("prob_lo_ready")
        pv_ready = s.sem("pv_ready")
        out_done = s.sem("out_done")
        nsteps = s.sem("norm_steps")
        CAST = (3,)

        with nc.Block() as block:
            def windows(engine, n, u):
                x = (S + 2 + (AHEAD - 1) * LB) - LB * n
                engine.dma_start(win[:, u, :, 0:WIN], RS[:, :, bass.ds(x, WIN)]).then_inc(win_loaded[u], 16)

            @block.sync
            def _(sp):
                for u in range(QT):
                    sp.wait_ge(win_loaded[u], 16 * (RT + (u < AHEAD)))

            @block.tensor
            def _(pe):
                def keys(bank, u, rt):
                    for g in range(NH // 2):
                        nc.tensor.matmul(bank[:, 2 * g * LB:2 * (g + 1) * LB], KT[0:RK, g, rt * P:(rt + 1) * P],
                                         qk[0:RK, u, 2 * g:2 * g + 2, :], start=(g == 0), stop=False)

                def table(bank, u, rt, form, moving, rows, together):
                    cols = bank.rearrange("p (h l) -> p h l", l=LB)
                    for j in range(0, LB, together):
                        x = rt * P + LB - 2 - j
                        last = nc.tensor.matmul(cols[:, :, j:j + together], win[0:rows, u, form, x:x + P],
                                                moving[0:rows, u, :, j:j + together],
                                                start=False, stop=(j == LB - together))
                    return last

                def raw(t, n, u, rt):
                    if rt == 0:
                        pe.wait_ge(laid, n + 1)
                        pe.wait_ge(win_loaded[u], 16 * t + 16)
                    pe.wait_ge(raw_free, RT * n + rt + 1)
                    keys(pm[:, rt % 2, :], u, rt)
                    table(pm[:, rt % 2, :], u, rt, 1, q4, RK, 4).then_inc(raw_ready, 1)

                def score(n, u, rt):
                    if rt == 0:
                        pe.wait_ge(row_ready, n + 2)
                    pe.wait_ge(full_ready, RT * n + rt + 1)
                    keys(pz[:, rt % 2, :], u, rt)
                    table(pz[:, rt % 2, :], u, rt, 0, qr, RK + 1, 2).then_inc(score_ready, 1)

                def turn(n, u):
                    pe.wait_ge(raw_free, RT * n + RT + 2)
                    pe.wait_ge(row_ready, n + 1)
                    for c in range(QT):
                        last = nc.tensor.transpose(pt[:, 0, c * P:(c + 1) * P], top[:, u % 2, c * P:(c + 1) * P],
                                                   k.ident32[:])
                    last.then_inc(turned, 1)

                def row(n):
                    pe.wait_ge(neg_ready, n + 1)
                    for c in range(QT):
                        last = nc.tensor.matmul(pt[RK:RK + 1, 0, c * P:(c + 1) * P], negpeak[:, c:c + 1],
                                                k.ident16[:], start=True, stop=True)
                    last.then_inc(row_made, 1)

                def ahead(t, n, u, i):
                    m = 1 if i < 4 else 2
                    raw(t + (u + m) // QT, n + m, (u + m) % QT, (i + 4) % RT)

                def pv_tile(t, n, rt):
                    if rt == 0:
                        pe.wait_ge(out_done, t + 1)
                    if rt in CAST:
                        pe.wait_ge(cast_ready, len(CAST) * n + CAST.index(rt) + 1)
                    else:
                        pe.wait_ge(full_ready, 2 + RT * n + rt + 1)
                    for hl in range(2):
                        if hl == LO:
                            pe.wait_ge(lo_ready, 4 + RT * n + rt + 1)
                        for h in range(NH):
                            last = nc.tensor.matmul(pv[:, h // 8, (h % 8) * 33:(h % 8 + 1) * 33],
                                                    probs[:, hl, rt, h, :], V[:, b * RT + rt, h, :],
                                                    start=(rt == 0 and hl == HI and h % 8 == 0),
                                                    stop=(rt == RT - 1 and hl == LO and h % 8 == 7))
                    last.then_inc(pv_ready, 1)

                def step(t, u):
                    n = QT * t + u
                    for i in range(4):
                        ahead(t, n, u, i)
                        score(n, u, i)
                    if u < QT - 1:
                        order = ("a4", "s4", "a5", "s5", "turn", "a6", "s6", "row", "a7", "s7")
                    else:
                        order = ("p0", "a4", "s4", "p1", "a5", "s5", "turn", "p2", "a6", "s6", "row", "p3", "a7", "s7",
                                 "p4", "p5", "p6", "p7")
                    for what in order:
                        if what == "turn":
                            turn(n + 1, (u + 1) % QT)
                        elif what == "row":
                            row(n + 1)
                        elif what[0] == "a":
                            ahead(t, n, u, int(what[1]))
                        elif what[0] == "p":
                            pv_tile(t, n, int(what[1]))
                        else:
                            score(n, u, int(what[1]))

                pe.sem_inc(pv_ready, RT)
                pe.sem_inc(score_ready, QT * RT)
                for rt in range(RT):
                    raw(0, 0, 0, rt)
                raw(0, 1, 1, 0)
                raw(0, 1, 1, 1)
                turn(0, 0)
                raw(0, 1, 1, 2)
                row(0)
                raw(0, 1, 1, 3)
                with pe.Fori(0, RT) as t:
                    for u in range(QT):
                        step(t, u)

            @block.scalar
            def _(act):
                def copy_row(n, u):
                    act.wait_ge(row_made, n + 1)
                    nc.scalar.copy(qr[RK:RK + 1, u, :, :],
                                   pt[RK:RK + 1, 0, :].rearrange("p (h l) -> p h l", l=LB)).then_inc(row_ready, 1)

                act.sem_inc(full_ready, 2)
                act.sem_inc(row_ready, 1)
                for n in range(AHEAD):
                    windows(act, n, n)
                copy_row(0, 0)
                with act.Fori(0, RT) as t:
                    for q in range(QT):
                        n = QT * t + q
                        for rt in range(RT):
                            act.wait_ge(score_ready, QT * RT + RT * n + rt + 1)
                            if q == 0:
                                act.wait_ge(pv_ready, RT * t + rt + 1)
                            if rt not in CAST:
                                nc.scalar.activation(probs[:, HI, rt, :, q * LB:(q + 1) * LB],
                                                     pz[:, rt % 2, :].rearrange("p (h l) -> p h l", l=LB), ACT.Exp)
                            act.wait_ge(lo_ready, RT * n + rt + 1)
                            nc.scalar.activation(full[:, rt % 4, :], pz[:, rt % 2, :], ACT.Exp).then_inc(full_ready, 1)
                            if rt == 2:
                                windows(act, n + AHEAD, (q + AHEAD) % QT)
                            if rt == 6:
                                copy_row(n + 1, (q + 1) % QT)

            @block.gpsimd
            def _(pool):
                pool.sem_inc(lo_ready, 4)
                with pool.Fori(0, RT) as t:
                    for q in range(QT):
                        n = QT * t + q
                        for rt in range(RT):
                            if rt in CAST:
                                pool.wait_ge(cast_ready, len(CAST) * n + CAST.index(rt) + 1)
                            else:
                                pool.wait_ge(full_ready, 2 + RT * n + rt + 1)
                            nc.gpsimd.tensor_tensor(probs[:, LO, rt, :, q * LB:(q + 1) * LB],
                                                    full[:, rt % 4, :].rearrange("p (h l) -> p h l", l=LB),
                                                    probs[:, HI, rt, :, q * LB:(q + 1) * LB],
                                                    ALU.subtract).then_inc(lo_ready, 1)

            @block.vector
            def _(dve):
                dve.sem_inc(raw_free, 2)
                dve.sem_inc(out_done, 1)

                def lay(n, u, i):
                    if i == 0:
                        dve.wait_ge(score_ready, RT * n + RT)
                    q_in = Q[:, :, bass.ds(LB * n, LB)]
                    if i == 0:
                        pairs = lambda x: x.rearrange("p (g two) l -> p g two l", two=2)
                        nc.vector.tensor_tensor(pairs(qk[:, u]), pairs(q_in),
                                                half[:].unsqueeze(1).unsqueeze(3).broadcast_to([RK, NH // 2, 2, LB]),
                                                ALU.mult)
                        return
                    dst, mask, m = ((qr[0:RK, u], half, 2), (q4[:, u], quarter, 4))[i - 1]
                    groups = lambda x: x.rearrange("p h (l m) -> p h l m", m=m)
                    last = nc.vector.tensor_tensor(
                        groups(dst), groups(q_in),
                        mask[:].unsqueeze(1).unsqueeze(2).broadcast_to([RK, NH, LB // m, m]), ALU.mult)
                    if i == 2:
                        last.then_inc(laid, 1)

                def take(n, u, rt):
                    dve.wait_ge(raw_ready, RT * n + rt + 1)
                    if rt == 0:
                        nc.vector.tensor_copy(top[:, u % 2, :], pm[:, 0, :]).then_inc(raw_free, 1)
                    else:
                        dve.wait_ge(raw_free, RT * n + rt + 2)
                        nc.vector.tensor_tensor(top[:, u % 2, :], pm[:, rt % 2, :], top[:, u % 2, :],
                                                ALU.max).then_inc(raw_free, 1)

                def peaks(n):
                    dve.wait_ge(turned, n + 1)
                    nc.vector.tensor_reduce(peak[:], pt[:, 0, :].rearrange("p (c r) -> p c r", r=P), X, ALU.max)\
                        .then_inc(peak_done, 1)
                    dve.wait_ge(peak_done, n + 1)
                    nc.vector.tensor_scalar(negpeak[:], peak[:], -1.0, None, ALU.mult).then_inc(neg_ready, 1)

                def cast(n, q, rt):
                    dve.wait_ge(full_ready, 2 + RT * n + rt + 1)
                    nc.vector.tensor_copy(probs[:, HI, rt, :, q * LB:(q + 1) * LB],
                                          full[:, rt % 4, :].rearrange("p (h l) -> p h l", l=LB)).then_inc(cast_ready, 1)

                def norm(t, chain):
                    link = Chain(dve, nsteps)
                    link.base = chain
                    heads = pv[:, :, 0:8 * 33].rearrange("p a (h c) -> p a h c", c=33)
                    dve.wait_ge(pv_ready, RT * (t + 2))
                    nc.vector.reciprocal(inv[:], heads[:, :, :, 32]).then_inc(nsteps, 1)
                    link.n = 1
                    link(nc.vector.tensor_copy(low[:], heads[:, :, :, D:2 * D]))
                    link(nc.vector.tensor_tensor(mid[:], heads[:, :, :, 0:D], low[:], ALU.add))
                    place = slice((b * RT + t) * H, (b * RT + t + 1) * H) if isinstance(t, int) else \
                        bass.ds((b * RT + t) * H, H)
                    nc.vector.tensor_tensor(o[:, place].rearrange("p (a h d) -> p a h d", a=2, d=D),
                                            mid[:], inv[:].unsqueeze(3).broadcast_to([P, 2, 8, D]),
                                            ALU.mult).then_inc(out_done, 1)

                def step(t, u, before=None):
                    n = QT * t + u
                    for i in range(RT):
                        m = 1 if i < 4 else 2
                        take(n + m, (u + m) % QT, (i + 4) % RT)
                        if i < 3:
                            lay(n + 2, (u + 2) % QT, i)
                        if i == 3 and before is not None:
                            norm(before, 3 * before)
                        if i - 1 in CAST:
                            cast(n, u, i - 1)
                        if i == 5:
                            peaks(n + 1)

                for n in range(2):
                    for i in range(3):
                        lay(n, n, i)
                for rt in range(RT):
                    take(0, 0, rt)
                take(1, 1, 0)
                take(1, 1, 1)
                peaks(0)
                take(1, 1, 2)
                take(1, 1, 3)
                for u in range(QT):
                    step(0, u)
                with dve.Fori(1, RT) as t:
                    for u in range(QT):
                        step(t, u, t - 1 if u == 0 else None)
                norm(RT - 1, 3 * (RT - 1))


def output_rows(nc, k, w, bias, dst, name, tiles=TT, add=True, arrived=None):
    with ExitStack() as stack:
        s = Scope(nc, stack)
        ps = s.banks(name + "_ps", 4)
        row = s.sb(name + "_bias", [P, H], F32)
        loaded = s.sem(name + "_loaded")
        ready = s.sem(name + "_ready")
        biased = s.sem(name + "_biased")
        added = s.sem(name + "_added")
        with nc.Block() as block:
            @block.sync
            def _(sp):
                sp.dma_start(row[:], bias.rearrange("(a d) -> a d", a=1).broadcast_to([P, H])).then_inc(loaded, 16)

            @block.tensor
            def _(pe):
                for t in range(tiles):
                    if t >= 4:
                        pe.wait_ge(added, t - 3)
                    i = 0
                    for a, b in PRODUCTS:
                        for kc in range(KC):
                            last = nc.tensor.matmul(ps[:, t % 4, 0:H], k.zT[:, a, kc, t * P:(t + 1) * P],
                                                    w[:, b, kc, :], start=(i == 0), stop=(i == 5))
                            i += 1
                    last.then_inc(ready, 1)

            @block.vector
            def _(dve):
                dve.wait_ge(loaded, 16)
                if arrived is not None:
                    dve.wait_ge(arrived, 16)
                if add:
                    for t in range(tiles):
                        nc.vector.tensor_tensor(dst[:, t, :], dst[:, t, :], row[:], ALU.add).then_inc(biased, 1)
                for t in range(tiles):
                    dve.wait_ge(ready, t + 1)
                    if add:
                        dve.wait_ge(biased, t + 1)
                    nc.vector.tensor_tensor(dst[:, t, :], ps[:, t % 4, 0:H], dst[:, t, :] if add else row[:],
                                            ALU.add).then_inc(added, 1)


QH, QD = 16, 64
QI = QH * QD
RAISE = 10.5
FAR = -1e30
PAD = P
TL = PAD + S
VW = 2 * QD + 1


def row_of(v):
    return v.rearrange("(a d) -> a d", a=1)


def layer_norm(nc, src, dst, n, gain, shift, name, silu=False, jobs=(), gain_rows=None):
    with ExitStack() as stack:
        s = Scope(nc, stack, name + "_")
        rows = s.sb("rows", [P, 2, H], F32) if gain_rows is None else gain_rows
        stats = s.sb("stats", [P, n, 6], F32)
        mv = s.sb("mean_var", [P, n, 2], F32)
        std = s.sb("std", [P, n], F32)
        inv = s.sb("inv", [P, n], F32)
        off = s.sb("off", [P, n], F32)
        loaded = s.sem("loaded")
        steps = s.sem("steps")
        with_eps = s.sem("with_eps")
        rooted = s.sem("rooted")
        factors = s.sem("factors")
        normed = s.sem("normed")
        gained = s.sem("gained")
        scaled = s.sem("scaled")
        acted = s.sem("acted")
        params = [x for x in (gain, shift) if x is not None and gain_rows is None]
        weights = WeightJobs(nc, s, jobs, 4)
        G = n // 4
        of = lambda g: slice(4 * g, 4 * g + 4)
        wide = lambda i: rows[:, i, :].unsqueeze(1).broadcast_to([P, 4, H])
        with nc.Block() as block:
            @block.sync
            def _(sp):
                for i, x in enumerate(params):
                    sp.dma_start(rows[:, i, :], row_of(x).broadcast_to([P, H])).then_inc(loaded, 16)
                weights.load(sp)

            @block.gpsimd
            def _(pool):
                weights.lo_even(pool)

            @block.scalar
            def _(act):
                for i in range(G + 2):
                    if i < G:
                        act.wait_ge(with_eps, i + 1)
                        nc.scalar.activation(std[:, of(i)], std[:, of(i)], ACT.Sqrt).then_inc(rooted, 1)
                    if 1 <= i <= G:
                        act.wait_ge(factors, 2 * i)
                        for t in range(4 * i - 4, 4 * i):
                            nc.scalar.activation(dst[:, t, :], src[:, t, :], ACT.Identity, bias=off[:, t:t + 1],
                                                 scale=inv[:, t:t + 1]).then_inc(normed, 1)
                    if i >= 2 and silu:
                        act.wait_ge(scaled, i - 1)
                        nc.scalar.activation(dst[:, of(i - 2), :], dst[:, of(i - 2), :], ACT.Silu).then_inc(acted, 1)
                    if i >= 2:
                        weights.hi(act, i - 2)
                weights.hi(act)

            @block.vector
            def _(dve):
                for i in range(G + 2):
                    if i < G:
                        for t in range(4 * i, 4 * i + 4):
                            nc.vector.bn_stats(stats[:, t, :], src[:, t, :]).then_inc(steps, 1)
                        for t in range(4 * i, 4 * i + 4):
                            dve.wait_ge(steps, 4 * i + t + 1)
                            nc.vector.bn_aggr(mv[:, t, :], stats[:, t, :]).then_inc(steps, 1)
                        dve.wait_ge(steps, 8 * (i + 1))
                        nc.vector.tensor_scalar(std[:, of(i)], mv[:, of(i), 1], 1e-5, None, ALU.add).then_inc(with_eps, 1)
                    if 1 <= i <= G:
                        dve.wait_ge(rooted, i)
                        nc.vector.reciprocal(inv[:, of(i - 1)], std[:, of(i - 1)]).then_inc(factors, 1)
                        dve.wait_ge(factors, 2 * i - 1)
                        nc.vector.scalar_tensor_tensor(out=off[:, of(i - 1)], in0=mv[:, of(i - 1), 0], scalar=-1.0,
                                                       in1=inv[:, of(i - 1)], op0=ALU.mult, op1=ALU.mult)\
                            .then_inc(factors, 1)
                    if i >= 2:
                        if i == 2 and params:
                            dve.wait_ge(loaded, 16 * len(params))
                        rows4 = dst[:, of(i - 2), :]
                        dve.wait_ge(normed, 4 * (i - 1))
                        nc.vector.tensor_tensor(rows4, rows4, wide(0), ALU.mult)\
                            .then_inc(scaled if shift is None else gained, 1)
                        if shift is not None:
                            dve.wait_ge(gained, i - 1)
                            nc.vector.tensor_tensor(rows4, rows4, wide(1), ALU.add).then_inc(scaled, 1)
                weights.lo_odd(dve)


def position_rows(nc, w0, b0, dst):
    with ExitStack() as stack:
        s = Scope(nc, stack, "pos_")
        rows = s.sb("rows", [P, 2, H], F32)
        pos = s.sb("distance", [P, RT], F32)
        loaded = s.sem("loaded")
        counted = s.sem("counted")
        with nc.Block() as block:
            @block.sync
            def _(sp):
                sp.dma_start(rows[:, 0, :], w0.broadcast_to([P, H])).then_inc(loaded, 16)
                sp.dma_start(rows[:, 1, :], row_of(b0).broadcast_to([P, H])).then_inc(loaded, 16)

            @block.gpsimd
            def _(pool):
                pool.iota(pos[:], [[P, RT]], 0, 1, True).then_inc(counted, 1)

            @block.vector
            def _(dve):
                dve.wait_ge(loaded, 32)
                dve.wait_ge(counted, 1)
                for c in range(RT):
                    nc.vector.scalar_tensor_tensor(out=dst[:, c, :], in0=rows[:, 0, :], scalar=pos[:, c:c + 1],
                                                   in1=rows[:, 1, :], op0=ALU.mult, op1=ALU.add)


def bias_table(nc, k, w2, b2, q_scale, k_scale, null_bias, table, null_d, table_d, copied, early, nb):
    with ExitStack() as stack:
        s = Scope(nc, stack, "table_")
        ps = s.banks("ps", 2)
        col = s.sb("col", [QH, 8], F32)
        scales = s.sb("scales", [QH, 2, QD], F32)
        loaded = s.sem("loaded")
        rooted = s.sem("rooted")
        ready = s.sem("ready")
        steps = s.sem("steps")
        stored = s.sem("stored")
        early_loaded = s.sem("early_loaded")
        with nc.Block() as block:
            @block.sync
            def _(sp):
                sp.dma_start(scales[:, 0, :], row_of(q_scale).broadcast_to([QH, QD])).then_inc(loaded, 16)
                sp.dma_start(scales[:, 1, :], row_of(k_scale).broadcast_to([QH, QD])).then_inc(loaded, 16)
                sp.dma_start(col[:, 0:1], b2.rearrange("(h a) -> h a", a=1)).then_inc(loaded, 16)
                sp.dma_start(col[:, 1:2], null_bias.rearrange("(h a) -> h a", a=1)).then_inc(loaded, 16)
                for dst, src in early:
                    sp.dma_start(dst, src).then_inc(early_loaded, 16)
                sp.wait_ge(steps, 9)
                sp.dma_start(null_d, col[:, 5:6]).then_inc(stored, 16)
                sp.wait_ge(stored, 16)
                sp.dma_start(nb[:], null_d.rearrange("h a -> a h").broadcast_to([P, QH]),
                             allow_slow_non_contiguous=True).then_inc(early_loaded, 16)

            @block.tensor
            def _(pe):
                for c in range(2):
                    i = 0
                    for a, b in PRODUCTS:
                        for kc in range(KC):
                            last = nc.tensor.matmul(ps[0:QH, c, :], w2[:, a, kc, :], k.zT[:, b, kc, c * 512:(c + 1) * 512],
                                                    start=(i == 0), stop=(i == 5))
                            i += 1
                last.then_inc(ready, 1)

            @block.vector
            def _(dve):
                link = Chain(dve, steps)
                dve.wait_ge(loaded, 64)
                link(nc.vector.tensor_tensor(scales[:, 0, :], scales[:, 0, :], scales[:, 1, :], ALU.mult))
                link(nc.vector.tensor_tensor(scales[:, 0, :], scales[:, 0, :], scales[:, 0, :], ALU.mult))
                link(nc.vector.tensor_reduce(col[:, 2:3], scales[:, 0, :], X, ALU.max))
                dve.wait_ge(ready, 1)
                link(nc.vector.tensor_scalar(table[:, PAD:TL], ps[0:QH].rearrange("p a b -> p (a b)"), col[:, 0:1],
                                             None, ALU.add))
                link(nc.vector.tensor_reduce(col[:, 3:4], table[:, PAD:TL], X, ALU.max))
                link(nc.vector.tensor_tensor(col[:, 3:4], col[:, 3:4], col[:, 1:2], ALU.max))
                dve.wait_ge(rooted, 1)
                link(nc.vector.scalar_tensor_tensor(out=col[:, 4:5], in0=col[:, 4:5], scalar=-RAISE, in1=col[:, 3:4],
                                                    op0=ALU.add, op1=ALU.add))
                link(nc.vector.tensor_scalar(table[:, PAD:TL], table[:, PAD:TL], col[:, 4:5], None, ALU.subtract))
                link(nc.vector.tensor_tensor(col[:, 5:6], col[:, 1:2], col[:, 4:5], ALU.subtract))
                link(nc.vector.memset(table[:, 0:PAD], FAR))

            @block.scalar
            def _(act):
                act.wait_ge(steps, 3)
                nc.scalar.activation(col[:, 4:5], col[:, 2:3], ACT.Sqrt, scale=64.0).then_inc(rooted, 1)
                act.wait_ge(steps, 10)
                act.wait_ge(early_loaded, 16 * (len(early) + 1))
                for h in range(QH):
                    act.dma_start(table_d[h:h + 1], table[h:h + 1, :].unsqueeze(1).broadcast_to([1, P, TL])).then_inc(copied, 16)


def causal_operands(nc, k, wq, wkv, srow, nk, nb, m8, q_d, KT, V, side, null, copied):
    with ExitStack() as stack:
        s = Scope(nc, stack, "causal_")
        pq = s.banks("q_ps", 4)
        ptq = s.banks("turn_ps", 2, F16)
        kv_bank = s.banks("kv_ps", 1)
        pkv = kv_bank[:, 0, 0:2 * QD]
        small = s.banks("small_ps", 1)
        pn = small[:, 0, 0:TT * QH]
        ptk = small[:, 0, TT * QH:TT * QH + 2 * P]
        pmask = ptk[:, 2:2 + TT]
        sq = s.sb("sq", [P, QI], F32)
        norm = s.sb("norm", [P, 3, QH + 1], F32)
        unit = s.sb("unit", [P, 2, QI], F32)
        qn = s.sb("qn", [P, 2, QH, 2, QD], F16)
        QT = s.sb("QT", [P, 3, QH, P], F16)
        kv = s.sb("kv", [P, 2, 2 * QD], F32)
        kwork = s.sb("kwork", [P, QD], F32)
        kn = s.sb("kn", [P, 2, 2, 2, QD], F16)
        nkn = s.sb("nkn", [1, 2, 2, QD], F16)
        nkc = s.sb("nkc", [1, 4], F32)
        NK = s.sb("NK", [P, 2], F16)
        m32 = s.sb("mask32", [TT, P], F32)
        nsteps = s.sem("null_steps")
        null_sq = s.sem("null_squares")
        null_root = s.sem("null_root")
        null_turned = s.sem("null_turned")
        null_ready = s.sem("null_ready")
        null_scored = s.sem("null_scored")
        null_biased = s.sem("null_biased")
        mask_cast = s.sem("mask_cast")
        mask_turned = s.sem("mask_turned")
        q_ready = s.sem("q_ready")
        squared = s.sem("squared")
        added = s.sem("added")
        summed = s.sem("summed")
        rooted = s.sem("rooted")
        steps = s.sem("steps")
        unit_ready = s.sem("unit_ready")
        hi_done = s.sem("hi_done")
        lo_done = s.sem("lo_done")
        kv_taken = s.sem("kv_taken")
        k_done = s.sem("k_done")
        zeroed = s.sem("zeroed")
        turned = s.sem("turned")
        q_moved = s.sem("q_moved")
        k_moved = s.sem("k_moved")
        stored = [s.sem(f"stored{i}") for i in range(3)]
        with nc.Block() as block:
            @block.sync
            def _(sp):
                for t in range(TT):
                    sp.wait_ge(q_moved, 2 * (t + 1))
                    sp.dma_start(q_d[:, :, t * P:(t + 1) * P].rearrange("h p t -> p h t"), QT[:, t % 3]).then_inc(stored[t % 3], 16)
                for i in range(3):
                    sp.wait_ge(stored[i], 16 * len(range(i, TT, 3)))
                sp.wait_ge(copied, 16 * QH)

            @block.gpsimd
            def _(pool):
                pool.memset(kn[:], 0.0).then_inc(zeroed, 1)
                pool.memset(V[:, :, 2 * QD:VW], 1.0)
                for t in range(TT):
                    pool.wait_ge(hi_done, t + 1)
                    nc.gpsimd.tensor_tensor(qn[:, t % 2, :, LO, :], unit[:, t % 2].rearrange("p (h d) -> p h d", d=QD),
                                            qn[:, t % 2, :, HI, :], ALU.subtract).then_inc(lo_done, 1)

            @block.tensor
            def _(pe):
                def project(t):
                    if t >= 2:
                        pe.wait_ge(unit_ready, t - 1)
                    for c in range(2):
                        i = 0
                        for x, y in PRODUCTS:
                            for kc in range(KC):
                                nc.tensor.matmul(pq[:, 2 * (t % 2) + c, :], k.zT[:, x, kc, t * P:(t + 1) * P],
                                                 wq[:, y, kc, c * 512:(c + 1) * 512], start=(i == 0), stop=(i == 5))
                                i += 1
                    if t >= 1:
                        pe.wait_ge(kv_taken, t)
                    i = 0
                    for x, y in PRODUCTS:
                        for kc in range(KC):
                            last = nc.tensor.matmul(pkv, k.zT[:, x, kc, t * P:(t + 1) * P],
                                                    wkv[:, y, kc, :], start=(i == 0), stop=(i == 5))
                            i += 1
                    last.then_inc(q_ready, 1)

                def turn(t):
                    pe.wait_ge(lo_done, t + 1)
                    pe.wait_ge(k_done, t + 1)
                    for c in range(2):
                        if t >= 1:
                            pe.wait_ge(q_moved, 2 * (t - 1) + c + 1)
                        for h in range(8):
                            last = nc.tensor.transpose(ptq[:, c, h * P:(h + 1) * P],
                                                       qn[:, t % 2, 8 * c + h].rearrange("p a d -> p (a d)"), k.ident16[:])
                        last.then_inc(turned, 1)
                    if t >= 1:
                        pe.wait_ge(k_moved, t)
                        null_scores(t - 1)
                    for c in range(2):
                        last = nc.tensor.matmul(ptk[:, c * P:(c + 1) * P],
                                                kn[:, t % 2, c].rearrange("p a d -> p (a d)"), k.ident16[:],
                                                start=True, stop=True)
                    last.then_inc(turned, 1)

                def null_scores(t):
                    pe.wait_ge(q_moved, 2 * (t + 1))
                    for h in range(QH):
                        for c in range(2):
                            last = nc.tensor.matmul(pn[:, t * QH + h:t * QH + h + 1], QT[:, t % 3, h, :],
                                                    NK[:, c:c + 1], start=(c == 0), stop=(c == 1))
                    last.then_inc(null_scored, 1)

                project(0)
                pe.wait_ge(mask_cast, 1)
                nc.tensor.transpose(pmask, m32[:], k.ident32[0:TT, 0:TT]).then_inc(mask_turned, 1)
                pe.wait_ge(nsteps, 6)
                for c in range(2):
                    last = nc.tensor.matmul(ptk[:, c:c + 1], nkn[:, c].rearrange("p a d -> p (a d)"), k.ident16[0:1, 0:1],
                                            start=True, stop=True)
                last.then_inc(null_turned, 1)
                project(1)
                pe.wait_ge(null_ready, 1)
                for t in range(TT):
                    if t + 2 < TT:
                        project(t + 2)
                    turn(t)
                pe.wait_ge(k_moved, TT)
                null_scores(TT - 1)

            @block.scalar
            def _(act):
                act.wait_ge(null_sq, 1)
                nc.scalar.activation(nkc[:, 1:2], nkc[:, 0:1], ACT.Sqrt).then_inc(null_root, 1)

                def squares(t):
                    act.wait_ge(q_ready, t + 1)
                    nc.scalar.activation(sq[:], pq[:, 2 * (t % 2):2 * (t % 2) + 2, :].rearrange("p a b -> p (a b)"),
                                         ACT.Square).then_inc(squared, 1)

                def hi_part(t):
                    act.wait_ge(unit_ready, t + 1)
                    if t >= 2:
                        act.wait_ge(turned, 3 * (t - 2) + 2)
                    nc.scalar.copy(qn[:, t % 2, :, HI, :], unit[:, t % 2].rearrange("p (h d) -> p h d", d=QD))\
                        .then_inc(hi_done, 1)

                def move(t):
                    if t >= 3:
                        act.wait_ge(stored[t % 3], 16 * (t // 3))
                        act.wait_ge(null_scored, t - 2)
                    for c in range(2):
                        act.wait_ge(turned, 3 * t + c + 1)
                        nc.scalar.copy(QT[:, t % 3, 8 * c:8 * c + 8, :],
                                       ptq[:, c, :].rearrange("p (h t) -> p h t", t=P)).then_inc(q_moved, 1)

                squares(0)
                for t in range(TT):
                    act.wait_ge(summed, t + 1)
                    nc.scalar.activation(norm[:, 1, :], norm[:, 0, :], ACT.Sqrt).then_inc(rooted, 1)
                    if t + 1 < TT:
                        squares(t + 1)
                    hi_part(t)
                    if t >= 1:
                        move(t - 1)
                move(TT - 1)
                act.wait_ge(null_biased, 1)
                nc.scalar.activation(null[:], null[:], ACT.Exp).then_inc(null_biased, 1)

            @block.vector
            def _(dve):
                link = Chain(dve, nsteps)
                link(nc.vector.tensor_tensor(srow[:, 2, :], srow[:, 0, :], srow[:, 1, :], ALU.mult))
                link(nc.vector.tensor_scalar(srow[:, 2, :], srow[:, 2, :], 8.0, None, ALU.mult))
                nc.vector.tensor_copy(m32[:], m8[:]).then_inc(mask_cast, 1)
                link(nc.vector.tensor_tensor(nk[:, 1, :], nk[:, 0, :], nk[:, 0, :], ALU.mult))
                nc.vector.tensor_reduce(nkc[:, 0:1], nk[:, 1, :], X, ALU.add).then_inc(null_sq, 1)
                dve.wait_ge(null_root, 1)
                nc.vector.tensor_scalar(nkc[:, 2:3], nkc[:, 1:2], 1e-12, None, ALU.max).then_inc(null_sq, 1)
                dve.wait_ge(null_sq, 2)
                nc.vector.reciprocal(nkc[:, 3:4], nkc[:, 2:3]).then_inc(null_sq, 1)
                dve.wait_ge(null_sq, 3)
                link(nc.vector.scalar_tensor_tensor(out=nk[:, 2, :], in0=nk[:, 0, :], scalar=nkc[:, 3:4],
                                                    in1=srow[0:1, 2, :], op0=ALU.mult, op1=ALU.mult))
                nc.vector.memset(nkn[:, 1, 1, :], 0.0)
                nc.vector.tensor_copy(nkn[:, 0, 1, :], nk[:, 2, :])
                link(nc.vector.tensor_copy(nkn[:, 0, 0, :], nk[:, 2, :]))
                link(nc.vector.tensor_tensor(nkn[:, 1, 0, :], nk[:, 2, :], nkn[:, 0, 0, :], ALU.subtract))
                dve.wait_ge(mask_turned, 1)
                dve.wait_ge(null_turned, 1)
                nc.vector.tensor_scalar(side[:], pmask, 1.0, -FAR, ALU.subtract, ALU.mult)
                nc.vector.tensor_copy(NK[:], ptk[:, 0:2]).then_inc(null_ready, 1)
                dve.wait_ge(zeroed, 1)
                chain = Chain(dve, steps)

                def sums(t):
                    dve.wait_ge(squared, t + 1)
                    nc.vector.tensor_copy(kv[:, t % 2, :], pkv).then_inc(kv_taken, 1)
                    nc.vector.tensor_reduce(norm[:, 0, 0:QH], sq[:].rearrange("p (h d) -> p h d", d=QD), X,
                                            ALU.add).then_inc(added, 1)
                    dve.wait_ge(kv_taken, t + 1)
                    chain(nc.vector.tensor_tensor(kwork[:], kv[:, t % 2, 0:QD], kv[:, t % 2, 0:QD], ALU.mult))
                    dve.wait_ge(added, t + 1)
                    nc.vector.tensor_reduce(norm[:, 0, QH:QH + 1], kwork[:], X, ALU.add).then_inc(summed, 1)

                def move_keys(t):
                    dve.wait_ge(turned, 3 * t + 3)
                    nc.vector.tensor_copy(KT[:, :, t * P:(t + 1) * P],
                                          ptk.rearrange("p (a t) -> p a t", a=2)).then_inc(k_moved, 1)

                def finish(t):
                    dve.wait_ge(rooted, t + 1)
                    chain(nc.vector.tensor_scalar(norm[:, 2, :], norm[:, 1, :], 1e-12, None, ALU.max))
                    chain(nc.vector.reciprocal(norm[:, 2, :], norm[:, 2, :]))
                    if t >= 2:
                        dve.wait_ge(lo_done, t - 1)
                    nc.vector.tensor_tensor(unit[:, t % 2].rearrange("p (h d) -> p h d", d=QD),
                                            pq[:, 2 * (t % 2):2 * (t % 2) + 2, :].rearrange("p a (h d) -> p (a h) d", d=QD),
                                            norm[:, 2, 0:QH].unsqueeze(2).broadcast_to([P, QH, QD]),
                                            ALU.mult).then_inc(unit_ready, 1)
                    chain(nc.vector.scalar_tensor_tensor(out=kwork[:], in0=kv[:, t % 2, 0:QD], scalar=norm[:, 2, QH:QH + 1],
                                                         in1=srow[:, 2, :], op0=ALU.mult, op1=ALU.mult))
                    if t >= 2:
                        dve.wait_ge(turned, 3 * (t - 1))
                    nc.vector.tensor_copy(kn[:, t % 2, 0, 1, :], kwork[:])
                    nc.vector.tensor_copy(V[:, t, 0:QD], kv[:, t % 2, QD:2 * QD])
                    chain(nc.vector.tensor_copy(kn[:, t % 2, 0, 0, :], kwork[:]))
                    nc.vector.tensor_tensor(V[:, t, QD:2 * QD], kv[:, t % 2, QD:2 * QD], V[:, t, 0:QD], ALU.subtract)
                    nc.vector.tensor_tensor(kn[:, t % 2, 1, 0, :], kwork[:], kn[:, t % 2, 0, 0, :],
                                            ALU.subtract).then_inc(k_done, 1)

                sums(0)
                for t in range(TT):
                    finish(t)
                    if t >= 1:
                        move_keys(t - 1)
                    if t + 1 < TT:
                        sums(t + 1)
                move_keys(TT - 1)
                dve.wait_ge(null_scored, TT)
                nc.vector.tensor_tensor(null[:], pn.rearrange("p (t h) -> p t h", h=QH),
                                        nb[:].unsqueeze(1).broadcast_to([P, TT, QH]), ALU.add).then_inc(null_biased, 1)


def causal_pieces():
    out, at = [], 0
    for c in range(2):
        for j in range(4 * (c + 1)):
            first = max(512 * c, P * j)
            out.append((j, first, 512 * (c + 1) - first, at))
            at += 512 * (c + 1) - first
    return out, at


PIECES, PCOLS = causal_pieces()
NP = len(PIECES)


def causal_attention(nc, k, table_d, q_d, KT, V, side, null, nv, o):
    with ExitStack() as stack:
        s = Scope(nc, stack, "heads_")
        pz = s.banks("ps", 4)
        pv = s.banks("pv", 4)
        tile = s.sb("toeplitz", [P, 2, S], F32)
        q = s.sb("q", [P, 4, S], F16)
        sums = s.sb("biased", [P, 4, 512], F32)
        full = s.sb("prob_full", [P, 4, 512], F32)
        probs = s.sb("probs", [P, 2, 2, PCOLS], F16)
        nvrow = s.sb("null_value", [P, QD], F32)
        low = s.sb("low", [P, RT, QD], F32)
        mid = s.sb("mid", [P, RT, QD], F32)
        nulls = s.sb("nulls", [P, RT, QD], F32)
        inv = s.sb("inv", [P, 2, RT], F32)
        nv_loaded = s.sem("nv_loaded")
        tile_loaded = [s.sem(f"tile_loaded{i}") for i in range(2)]
        q_loaded = [s.sem(f"q_loaded{i}") for i in range(4)]
        score_ready = s.sem("score_ready")
        sum_ready = s.sem("sum_ready")
        full_ready = s.sem("full_ready")
        cast_ready = s.sem("hi_cast_ready")
        lo_ready = s.sem("lo_ready")
        pv_ready = s.sem("pv_ready")
        pv_free = s.sem("pv_free")
        steps = s.sem("steps")
        HP = QH // 2
        SUMS = 4 + 2 * NP
        AFTER = {3: (0, 1), 4: (2,), 5: (3,), 6: (4,), 8: (5,), 10: (6,), 11: (7,)}
        CAST = range(0, NP - 2, 2)
        with nc.Block() as block:
            @block.sync
            def _(sp):
                sp.dma_start(nvrow[:], nv.broadcast_to([P, QD])).then_inc(nv_loaded, 16)
                sp.wait_ge(nv_loaded, 16)
                with sp.Fori(0, HP) as g:
                    for u in range(2):
                        n0 = 4 * g + 2 * u
                        sp.wait_ge(sum_ready, SUMS + NP * (n0 - 2))
                        src = bass.AP(tensor=table_d.tensor, offset=(2 * g + u) * (P * TL) + PAD,
                                      ap=[[TL - 1, P], [1, S]])
                        sp.dma_start(tile[:, u, :], src).then_inc(tile_loaded[u], 16)
                        for b in range(B):
                            sp.dma_start(q[:, 2 * u + b, :], q_rows(q_d, 2 * g + u, b)).then_inc(q_loaded[2 * u + b], 16)

            @block.tensor
            def _(pe):
                def score(n, g, v, i):
                    j, first, w, _ = PIECES[i]
                    if i == 0:
                        pe.wait_ge(q_loaded[v], 16 * g + 16)
                    pe.wait_ge(sum_ready, SUMS - 4 + NP * n + i + 1)
                    at = v % 2 * S + j * P
                    nc.tensor.matmul(pz[:, i % 4, 0:w], KT[:, 0, at:at + P], q[:, v, first:first + w],
                                     start=True, stop=False)
                    nc.tensor.matmul(pz[:, i % 4, 0:w], KT[:, 1, at:at + P], q[:, v, first:first + w],
                                     start=False, stop=True).then_inc(score_ready, 1)

                def mix(n, v, t):
                    b = v % 2
                    if t == 0:
                        pe.wait_ge(pv_free, n + 1)
                    mine = [(i, j, at + t * P - first) for i, (j, first, w, at) in enumerate(PIECES)
                            if first <= t * P < first + w and j <= t]
                    pe.wait_ge(lo_ready, 4 + NP * n + mine[-1][0] + 1)
                    for i, j, at in mine:
                        for hl in range(2):
                            last = nc.tensor.matmul(pv[:, t // 2, (t % 2) * VW:(t % 2 + 1) * VW],
                                                    probs[:, n_par(v), hl, at:at + P], V[:, b * RT + j, :],
                                                    start=(j == 0 and hl == 0), stop=(j == t and hl == 1))
                    if t == RT - 1:
                        last.then_inc(pv_ready, 1)

                def step(n, g, v):
                    for i in range(NP):
                        score(n + 1, g + (v + 1) // 4, (v + 1) % 4, i)
                        for t in AFTER.get(i, ()):
                            mix(n, v, t)

                pe.sem_inc(pv_ready, 2)
                for i in range(NP):
                    score(0, 0, 0, i)
                with pe.Fori(0, HP - 1) as g:
                    for v in range(4):
                        step(4 * g + v, g, v)
                g = HP - 1
                for v in range(3):
                    step(4 * g + v, g, v)
                for t in range(RT):
                    mix(4 * g + 3, 3, t)

            @block.scalar
            def _(act):
                act.sem_inc(full_ready, 4)
                with act.Fori(0, HP) as g:
                    for v in range(4):
                        n = 4 * g + v
                        act.wait_ge(pv_ready, n + 1)
                        for i, (j, first, w, at) in enumerate(PIECES):
                            key = v % 2 * RT + j
                            act.wait_ge(sum_ready, SUMS + NP * n + i + 1)
                            if i not in CAST:
                                nc.scalar.activation(probs[:, n_par(v), HI, at:at + w], sums[:, i % 4, 0:w], ACT.Exp,
                                                     bias=side[:, key:key + 1])
                            act.wait_ge(lo_ready, NP * n + i + 1)
                            nc.scalar.activation(full[:, i % 4, 0:w], sums[:, i % 4, 0:w], ACT.Exp,
                                                 bias=side[:, key:key + 1]).then_inc(full_ready, 1)

            @block.gpsimd
            def _(pool):
                pool.sem_inc(lo_ready, 4)
                with pool.Fori(0, HP) as g:
                    for v in range(4):
                        n = 4 * g + v
                        for i, (j, first, w, at) in enumerate(PIECES):
                            if i in CAST:
                                pool.wait_ge(cast_ready, len(CAST) * n + CAST.index(i) + 1)
                            else:
                                pool.wait_ge(full_ready, 4 + NP * n + i + 1)
                            nc.gpsimd.tensor_tensor(probs[:, n_par(v), LO, at:at + w], full[:, i % 4, 0:w],
                                                    probs[:, n_par(v), HI, at:at + w], ALU.subtract).then_inc(lo_ready, 1)

            @block.vector
            def _(dve):
                dve.sem_inc(sum_ready, SUMS)
                dve.sem_inc(pv_free, 1)

                def bias(n, g, v, i):
                    j, first, w, _ = PIECES[i]
                    if i == 0:
                        dve.wait_ge(tile_loaded[v // 2], 16 * g + 16)
                    dve.wait_ge(score_ready, NP * n + i + 1)
                    dve.wait_ge(full_ready, NP * n + i + 1)
                    nc.vector.tensor_tensor(sums[:, i % 4, 0:w], pz[:, i % 4, 0:w],
                                            tile[:, v // 2, first - j * P:first - j * P + w],
                                            ALU.add).then_inc(sum_ready, 1)
                    if i - 2 in CAST:
                        _, _, w, at = PIECES[i - 2]
                        dve.wait_ge(full_ready, 4 + NP * n + i - 1)
                        nc.vector.tensor_copy(probs[:, n_par(v), HI, at:at + w],
                                              full[:, (i - 2) % 4, 0:w]).then_inc(cast_ready, 1)

                def norm(n, g, v, i):
                    b = v % 2
                    head = 2 * g + v // 2
                    pn = null_of(null, b, head)
                    acc = pv[:, :, 0:2 * VW].rearrange("p a (t c) -> p a t c", c=VW)
                    pair = lambda x: x.rearrange("p (a t) d -> p a t d", t=2)
                    if i == 0:
                        nc.vector.tensor_tensor(nulls[:], pn.unsqueeze(2).broadcast_to([P, RT, QD]),
                                                nvrow[:].unsqueeze(1).broadcast_to([P, RT, QD]),
                                                ALU.mult).then_inc(steps, 1)
                    elif i == 1:
                        dve.wait_ge(pv_ready, n + 3)
                        nc.vector.tensor_tensor(inv[:, 0, :].rearrange("p (a t) -> p a t", t=2), acc[:, :, :, 2 * QD],
                                                pn.rearrange("p (a t) -> p a t", t=2), ALU.add).then_inc(steps, 1)
                        dve.wait_ge(steps, 5 * n + 1)
                        nc.vector.tensor_tensor(pair(low[:]), acc[:, :, :, QD:2 * QD], pair(nulls[:]),
                                                ALU.add).then_inc(steps, 1)
                    elif i == 2:
                        dve.wait_ge(steps, 5 * n + 3)
                        nc.vector.tensor_tensor(pair(mid[:]), acc[:, :, :, 0:QD], pair(low[:]), ALU.add).then_inc(pv_free, 1)
                    elif i == 3:
                        nc.vector.reciprocal(inv[:, 1, :], inv[:, 0, :]).then_inc(steps, 1)
                    else:
                        dve.wait_ge(steps, 5 * n + 4)
                        dve.wait_ge(pv_free, n + 2)
                        nc.vector.tensor_tensor(out_of(o, b, head), mid[:],
                                                inv[:, 1, :].unsqueeze(2).broadcast_to([P, RT, QD]),
                                                ALU.mult).then_inc(steps, 1)

                def step(g, v):
                    n = 4 * g + v
                    for i in range(NP):
                        bias(n, g, v, i)
                        if i < 5 and not (isinstance(g, int) and n < 2):
                            norm(n - 2, g - (1 if v < 2 else 0), (v + 2) % 4, i)

                for v in range(4):
                    step(0, v)
                with dve.Fori(1, HP) as g:
                    for v in range(4):
                        step(g, v)
                for v in (2, 3):
                    for i in range(5):
                        norm(4 * (HP - 1) + v, HP - 1, v, i)


def n_par(v):
    return v % 2


def q_rows(q_d, head, b):
    return bass.AP(tensor=q_d.tensor, offset=head * (P * T) + b * S, ap=[[T, P], [1, S]])


def null_of(null, b, head):
    return null[:].rearrange("p h t -> p (h t)")[:, bass.ds(head * TT + b * RT, RT)]


def out_of(o, b, head):
    return o[:, b * RT:(b + 1) * RT, bass.ds(head * QD, QD)]


def causal_output(nc, k, o, w, dst):
    with ExitStack() as stack:
        s = Scope(nc, stack, "causal_out_")
        pt = s.banks("turn_ps", 4)
        ps = s.banks("ps", 2)
        oT = s.sb("oT", [P, 2, 2, 8, P], F16)
        turned = s.sem("turned")
        hi_done = s.sem("hi_done")
        lo_done = s.sem("lo_done")
        ready = s.sem("ready")
        copied = s.sem("copied")
        with nc.Block() as block:
            @block.tensor
            def _(pe):
                def turn(t):
                    for c in range(2):
                        n = 2 * t + c
                        if n >= 4:
                            pe.wait_ge(lo_done, n - 3)
                        for i in range(4):
                            x = (4 * c + i) * P
                            last = nc.tensor.transpose(pt[:, n % 4, i * P:(i + 1) * P], o[:, t, x:x + P], k.ident32[:])
                        last.then_inc(turned, 1)

                turn(0)
                for t in range(TT):
                    if t + 1 < TT:
                        turn(t + 1)
                    pe.wait_ge(lo_done, 2 * (t + 1))
                    if t >= 2:
                        pe.wait_ge(copied, t - 1)
                    i = 0
                    for x, y in PRODUCTS:
                        for c in range(8):
                            last = nc.tensor.matmul(ps[:, t % 2, 0:H], oT[:, t % 2, x, c, :], w[:, y, c, :],
                                                    start=(i == 0), stop=(i == 23))
                            i += 1
                    last.then_inc(ready, 1)

            @block.scalar
            def _(act):
                for n in range(2 * TT):
                    t, c = n // 2, n % 2
                    act.wait_ge(turned, n + 1)
                    if t >= 2:
                        act.wait_ge(ready, t - 1)
                    nc.scalar.copy(oT[:, t % 2, HI, 4 * c:4 * c + 4, :],
                                   pt[:, n % 4, :].rearrange("p (c t) -> p c t", t=P)).then_inc(hi_done, 1)

            @block.vector
            def _(dve):
                for t in range(TT):
                    for c in range(2):
                        n = 2 * t + c
                        dve.wait_ge(hi_done, n + 1)
                        nc.vector.tensor_tensor(oT[:, t % 2, LO, 4 * c:4 * c + 4, :],
                                                pt[:, n % 4, :].rearrange("p (c t) -> p c t", t=P),
                                                oT[:, t % 2, HI, 4 * c:4 * c + 4, :], ALU.subtract).then_inc(lo_done, 1)
                    if t >= 1:
                        dve.wait_ge(ready, t)
                        nc.vector.tensor_copy(dst[:, t - 1, :], ps[:, (t - 1) % 2, 0:H]).then_inc(copied, 1)
                dve.wait_ge(ready, TT)
                nc.vector.tensor_copy(dst[:, TT - 1, :], ps[:, (TT - 1) % 2, 0:H]).then_inc(copied, 1)


def gelu_weight_jobs(a, w1, w2):
    jobs = []
    for kc in range(KC):
        for h in range(2):
            es = slice(4 * h, 4 * h + 4)
            jobs.append((a["L0_ffn_W1"][es, kc * P:(kc + 1) * P, :].rearrange("e p f -> p e f"),
                         w1[:, HI, kc, es, :], w1[:, LO, kc, es, :]))
    for h in range(4):
        es = slice(8 * h, 8 * h + 8)
        jobs.append((a["L0_ffn_W2"].rearrange("e (c p) h -> p (e c) h", p=P)[:, es, :],
                     w2[:, HI, es, :], w2[:, LO, es, :]))
    return jobs


def gelu_operands(nc, k, b1, b2, W, b1T, x):
    with ExitStack() as stack:
        s = Scope(nc, stack, "gelu_pre_")
        pt = s.banks("ps", 4)
        pb = s.banks("bias_ps", 4)
        rows = s.sb("b1_rows", [E * FC, P], F32)
        b2r = s.sb("b2_rows", [E, H], F32)
        b2s = s.sb("b2_parts", [E, 2, H], F16)
        WT = s.sb("WT", [E, 2, T], F16)
        loaded = s.sem("loaded")
        b1_turned = s.sem("b1_turned")
        b1_done = s.sem("b1_done")
        w_turned = s.sem("w_turned")
        w_hi = s.sem("w_hi")
        w_done = s.sem("w_done")
        b2_hi = s.sem("b2_hi")
        b2_done = s.sem("b2_done")
        ready = s.sem("ready")
        added = s.sem("added")
        with nc.Block() as block:
            @block.sync
            def _(sp):
                sp.dma_start(rows[:], b1.rearrange("e (c p) -> (e c) p", p=P)).then_inc(loaded, 16)
                sp.dma_start(b2r[:], b2).then_inc(loaded, 16)

            @block.tensor
            def _(pe):
                for t in range(TT):
                    last = nc.tensor.transpose(pt[0:E, t // 4, (t % 4) * P:(t % 4 + 1) * P], W[:, 0:E, t], k.ident32[:])
                last.then_inc(w_turned, 1)
                pe.wait_ge(loaded, 32)
                nc.tensor.transpose(pb[:, 0, 0:E * FC], rows[:], k.ident32[0:E * FC, 0:E * FC]).then_inc(b1_turned, 1)
                pe.wait_ge(w_done, 1)
                pe.wait_ge(b2_done, 1)
                pe.wait_ge(b1_done, 1)
                for n in range(TT // 2):
                    if n >= 4:
                        pe.wait_ge(added, n - 3)
                    for t in (2 * n, 2 * n + 1):
                        for i, (x, y) in enumerate(PRODUCTS):
                            last = nc.tensor.matmul(pb[:, n % 4, (t % 2) * H:(t % 2 + 1) * H], WT[:, x, t * P:(t + 1) * P],
                                                    b2s[:, y, :], start=(i == 0), stop=(i == 2))
                    last.then_inc(ready, 1)

            @block.scalar
            def _(act):
                act.wait_ge(loaded, 32)
                nc.scalar.copy(b2s[:, HI, :], b2r[:]).then_inc(b2_hi, 1)
                act.wait_ge(w_turned, 1)
                nc.scalar.copy(WT[:, HI, :], pt[0:E].rearrange("p a b -> p (a b)")).then_inc(w_hi, 1)

            @block.vector
            def _(dve):
                dve.wait_ge(b2_hi, 1)
                nc.vector.tensor_tensor(b2s[:, LO, :], b2r[:], b2s[:, HI, :], ALU.subtract).then_inc(b2_done, 1)
                dve.wait_ge(w_hi, 1)
                nc.vector.tensor_tensor(WT[:, LO, :], pt[0:E].rearrange("p a b -> p (a b)"), WT[:, HI, :],
                                        ALU.subtract).then_inc(w_done, 1)
                dve.wait_ge(b1_turned, 1)
                nc.vector.tensor_copy(b1T[:], pb[:, 0, 0:E * FC]).then_inc(b1_done, 1)
                for n in range(TT // 2):
                    dve.wait_ge(ready, n + 1)
                    pair = x[:, 2 * n:2 * n + 2, :]
                    nc.vector.tensor_tensor(pair, pb[:, n % 4, :].rearrange("p (t h) -> p t h", h=H), pair,
                                            ALU.add).then_inc(added, 1)


def gelu_experts(nc, k, w1, w2, b1T, W, acc):
    with ExitStack() as stack:
        s = Scope(nc, stack, "gelu_")
        ph = s.banks("hid_ps", FC)
        py = s.banks("down_ps", 4)
        full = s.sb("full", [P, 2, FC, 512], F32)
        parts = s.sb("parts", [P, 2, 2, FC, 512], F16)
        hid_ready = s.sem("hid_ready")
        full_ready = s.sem("full_ready")
        hi_ready = s.sem("hi_ready")
        lo_ready = s.sem("lo_ready")
        down_ready = s.sem("down_ready")
        down_free = s.sem("down_free")
        b1 = s.sb("b1_of_expert", [P, FC], F32)
        b1_ready = s.sem("b1_ready")
        with nc.Block() as block:
            @block.tensor
            def _(pe):
                pe.sem_inc(down_ready, 8)

                def hidden(e, c):
                    n = TC * e + c
                    for f in range(FC):
                        pe.wait_ge(full_ready, FC * n + f + 1)
                        i = 0
                        for a, b in PRODUCTS:
                            for kc in range(KC):
                                last = nc.tensor.matmul(ph[:, f, :], part_of(w1[:, a, kc], e, F, f * P, P),
                                                        k.zT[:, b, kc, c * 512:(c + 1) * 512],
                                                        start=(i == 0), stop=(i == 5))
                                i += 1
                        last.then_inc(hid_ready, 1)

                def down(e, c):
                    n = TC * e + c
                    pe.wait_ge(hi_ready, FC * (n + 1))
                    pe.wait_ge(lo_ready, 8 + FC * (n + 1))
                    for j in range(4):
                        pe.wait_ge(down_free, 4 * n + j + 1)
                        i = 0
                        for f in range(FC):
                            for a, b in PRODUCTS:
                                last = nc.tensor.matmul(py[:, j, 0:H], parts[:, c % 2, a, f, j * P:(j + 1) * P],
                                                        part_of(w2[:, b].rearrange("p (e f) h -> p e (f h)", f=FC),
                                                                e, FC * H, f * H, H),
                                                        start=(i == 0), stop=(i == 3 * FC - 1))
                                i += 1
                        last.then_inc(down_ready, 1)

                def expert(e, following):
                    for c in range(TC):
                        if c + 1 < TC:
                            hidden(e, c + 1)
                        elif following is not None:
                            hidden(following, 0)
                        down(e, c)

                hidden(0, 0)
                with pe.Fori(0, E - 1) as e:
                    expert(e, e + 1)
                expert(E - 1, None)

            @block.scalar
            def _(act):
                act.sem_inc(full_ready, 4)
                with act.Fori(0, E) as e:
                    act.wait_ge(b1_ready, e + 1)
                    for c in range(TC):
                        for f in range(FC):
                            m = FC * (TC * e + c) + f
                            act.wait_ge(hid_ready, m + 1)
                            act.wait_ge(lo_ready, m + 1)
                            nc.scalar.activation(full[:, c % 2, f, :], ph[:, f, :], ACT.Gelu,
                                                 bias=b1[:, f:f + 1]).then_inc(full_ready, 1)

            @block.gpsimd
            def _(pool):
                pool.sem_inc(lo_ready, 8)
                with pool.Fori(0, E) as e:
                    for c in range(TC):
                        for f in range(FC):
                            m = FC * (TC * e + c) + f
                            pool.wait_ge(hi_ready, m + 1)
                            nc.gpsimd.tensor_tensor(parts[:, c % 2, LO, f, :], full[:, c % 2, f, :],
                                                    parts[:, c % 2, HI, f, :], ALU.subtract).then_inc(lo_ready, 1)

            @block.vector
            def _(dve):
                dve.sem_inc(down_free, 4)

                def bias(e):
                    cols = slice(0, FC) if isinstance(e, int) and e == 0 else bass.ds(FC * e, FC)
                    nc.vector.tensor_copy(b1[:], b1T[:, cols]).then_inc(b1_ready, 1)

                def halves(e, c):
                    n = TC * e + c
                    dve.wait_ge(down_ready, 4 * n + 4)
                    for f in range(FC):
                        dve.wait_ge(full_ready, 4 + FC * n + f + 1)
                        nc.vector.tensor_copy(parts[:, c % 2, HI, f, :], full[:, c % 2, f, :]).then_inc(hi_ready, 1)

                def weigh(e, c):
                    n = TC * e + c
                    for j in range(4):
                        t = 4 * c + j
                        dve.wait_ge(down_ready, 8 + 4 * n + j + 1)
                        nc.vector.scalar_tensor_tensor(out=acc[:, t, :], in0=py[:, j, 0:H],
                                                       scalar=expert_weight(W, e, t), in1=acc[:, t, :],
                                                       op0=ALU.mult, op1=ALU.add).then_inc(down_free, 1)

                def expert(e, following):
                    for c in range(TC):
                        if c + 1 < TC:
                            halves(e, c + 1)
                            if c + 2 == TC and following is not None:
                                bias(following)
                        elif following is not None:
                            halves(following, 0)
                        weigh(e, c)

                bias(0)
                halves(0, 0)
                with dve.Fori(0, E - 1) as e:
                    expert(e, e + 1)
                expert(E - 1, None)


def part_of(w, e, stride, at, width):
    if isinstance(e, int):
        return w[:, e, at:at + width]
    return w.rearrange("p e n -> p (e n)")[:, bass.ds(e * stride + at, width)]


def add_rows(nc, src, dst):
    with nc.Block() as block:
        @block.vector
        def _(dve):
            for t in range(TT):
                nc.vector.tensor_tensor(dst[:, t, :], dst[:, t, :], src[:, t, :], ALU.add)


def build(nc, a, out):
    with ExitStack() as stack:
        s = Scope(nc, stack)

        SEMAPHORES.clear()

        class Kept:
            ident32 = s.sb("ident32", [P, P], F32)
            ident16 = s.sb("ident16", [P, P], F16)
            ones = s.sb("ones", [P, P], F16)
            iota = s.sb("iota", [P, E], F32)
            acc = s.sb("acc_rows", [P, TT, H], F32)

        k = Kept
        constants(nc, k)
        with ExitStack() as inner:
            g = Scope(nc, inner)
            k.zT = g.sb("xT", [P, 2, KC, T], F16)
            wg = g.sb("wg", [P, 2, KC, GE, M], F16)
            wu = g.sb("wu", [P, 2, KC, GE, M], F16)
            wd = g.sb("wd", [P, 2, GE, H], F16)
            wr = g.sb("wr", [P, 2, KC, E], F16)
            W = g.sb("W", [P, GE, TT], F32)
            jobs = []
            for w, name, shared in ((wg, "L0_cond_w_gate", "L0_cond_sw_gate"), (wu, "L0_cond_w_up", "L0_cond_sw_up")):
                for kc in range(KC):
                    jobs.append((a[name][:, kc * P:(kc + 1) * P, :].rearrange("e p m -> p e m"),
                                 w[:, HI, kc, 0:E, :], w[:, LO, kc, 0:E, :]))
                    jobs.append((a[shared][kc * P:(kc + 1) * P, :].rearrange("p (e m) -> p e m", e=NS),
                                 w[:, HI, kc, E:GE, :], w[:, LO, kc, E:GE, :]))
            jobs.append((a["L0_cond_w_down"].rearrange("e m h -> m e h"), wd[:, HI, 0:E, :], wd[:, LO, 0:E, :]))
            jobs.append((a["L0_cond_sw_down"].rearrange("(e m) h -> m e h", e=NS), wd[:, HI, E:GE, :], wd[:, LO, E:GE, :]))
            with ExitStack() as first:
                x = Scope(nc, first).sb("x_rows", [P, TT, H], F32)
                load_rows(nc, a["x"], x, "x", jobs)
                transpose_split(nc, k, x, "x")
            gated_router_weights(nc, k, a["L0_cond_wt"], wr, W)
            routing(nc, k, "gated_router", wr, (a["cond_64"], a["L0_cond_wg"]), None, 0.5, (1e-20, ALU.add), W)
            gated_experts(nc, k, wg, wu, wd, W, k.acc)
        end_of_part(nc)
        with ExitStack() as inner:
            g = Scope(nc, inner)
            qd = nc.dram_tensor("query_parts", (2, H, T), F16, kind="Internal").ap()
            kd = nc.dram_tensor("key_parts", (2, H, T), F16, kind="Internal").ap()
            V = g.sb("V", [P, TT, NH, 2 * D + 1], F16)
            with ExitStack() as first:
                f = Scope(nc, first)
                k.zT = f.sb("yT", [P, 2, KC, T], F16)
                transpose_split(nc, k, k.acc, "y")
                wq, wk, wv = (f.sb(n, [P, 2, KC, H], F16) for n in ("wq", "wk", "wv"))
                turned_weights(nc, k, [(a["L0_attn_Wq"], wq), (a["L0_attn_Wk"], wk), (a["L0_attn_Wv"], wv)], "qkv")
                queries_keys(nc, k, [(wq, a["L0_attn_bq"], 1.0, qd), (wk, a["L0_attn_bk"], D ** -0.5, kd)])
                values(nc, k, wv, a["L0_attn_bv"], V)
            with ExitStack() as main:
                f = Scope(nc, main)
                RS = f.sb("RS", [RK + 1, 2, RW], F16)
                quarter = f.sb("quarter", [RK, 4], F16)
                half = f.sb("half", [RK, 2], F16)
                Q = f.sb("Q", [RK, NH, LP], F16)
                KT = f.sb("KT", [RK, NH // 2, S], F16)
                relative_rows(nc, k, a["L0_attn_rel_emb"], RS, half, quarter)
                for b in range(B):
                    relative_operands(nc, b, qd, kd, Q, KT)
                    relative_attention(nc, k, b, Q, KT, RS, half, quarter, V, k.acc[:].rearrange("p t h -> p (t h)"))
        k.x = s.sb("x_rows_again", [P, TT, H], F32)
        arrived = s.sem("x_arrived")
        load_rows(nc, a["x"], k.x, "x_again", arrived=arrived)
        with ExitStack() as inner:
            g = Scope(nc, inner)
            wo = g.sb("wo", [P, 2, KC, H], F16)
            k.zT = g.sb("oT", [P, 2, KC, T], F16)
            turned_weights(nc, k, [(a["L0_attn_Wo"], wo)], "wo")
            transpose_split(nc, k, k.acc, "o")
            output_rows(nc, k, wo, a["L0_attn_bo"], k.x, "attn_out", arrived=arrived)
        end_of_part(nc)
        with ExitStack() as inner:
            g = Scope(nc, inner)
            q_d = nc.dram_tensor("unit_queries", (QH, P, T), F16, kind="Internal").ap()
            table_d = nc.dram_tensor("bias_tables", (QH, P, TL), F32, kind="Internal").ap()
            null_d = nc.dram_tensor("null_bias_less_bound", (QH, 1), F32, kind="Internal").ap()
            KT = g.sb("causal_KT", [P, 2, T], F16)
            V = g.sb("causal_V", [P, TT, VW], F16)
            side = g.sb("key_mask", [P, TT], F32)
            null = g.sb("null_probs", [P, QH, TT], F32)
            wout = g.sb("wout", [P, 2, 8, H], F16)
            with ExitStack() as first:
                f = Scope(nc, first)
                wq = f.sb("c_wq", [P, 2, KC, QI], F16)
                wkv = f.sb("c_wkv", [P, 2, KC, 2 * QD], F16)
                w1 = f.sb("c_w1", [P, 2, KC, H], F16)
                w2 = f.sb("c_w2", [P, 2, KC, QH], F16)
                table = f.sb("bias_table", [QH, TL], F32)
                copied = f.sem("table_copied")
                srow = f.sb("both_scales", [P, 3, QD], F32)
                nk = f.sb("null_key", [1, 4, QD], F32)
                nb = f.sb("null_bias", [P, QH], F32)
                m8 = f.sb("mask8", [TT, P], U8)
                gain = f.sb("ln_in_gain", [P, 1, H], F32)
                early = [(srow[:, 0, :], row_of(a["L0_cond2_q_scale"]).broadcast_to([P, QD])),
                         (srow[:, 1, :], row_of(a["L0_cond2_k_scale"]).broadcast_to([P, QD])),
                         (nk[:, 0, :], a["cond_64"][0:1, :]),
                         (m8[:], a["mask_BxS_bf1"].rearrange("b (t p) -> (b t) p", p=P)),
                         (gain[:, 0, :], row_of(a["L0_cond2_g_norm"]).broadcast_to([P, H]))]
                hp = f.sb("pos_hidden", [P, RT, H], F32)
                k.zT = f.sb("c_zT", [P, 2, KC, T], F16)
                chunked = lambda name: a[name].rearrange("(c p) n -> p c n", p=P)
                jobs = [(chunked(n), w[:, HI], w[:, LO]) for n, w in (
                    ("L0_cond2_w1", w1), ("L0_cond2_w2", w2), ("L0_cond2_Wkv", wkv), ("L0_cond2_Wq", wq),
                    ("L0_cond2_Wout", wout))]
                position_rows(nc, a["L0_cond2_w0"], a["L0_cond2_b0"], hp)
                layer_norm(nc, hp, hp, RT, a["L0_cond2_g0"], None, "pos_ln0", silu=True, jobs=jobs)
                transpose_split(nc, k, hp, "pos0", RT)
                output_rows(nc, k, w1, a["L0_cond2_b1"], hp, "pos1", RT, add=False)
                layer_norm(nc, hp, hp, RT, a["L0_cond2_g1"], None, "pos_ln1", silu=True)
                transpose_split(nc, k, hp, "pos2", RT)
                bias_table(nc, k, w2, a["L0_cond2_b2"], a["L0_cond2_q_scale"], a["L0_cond2_k_scale"],
                           a["L0_cond2_null_attn_bias"], table, null_d, table_d, copied, early, nb)
                layer_norm(nc, k.x, k.acc, TT, None, None, "ln_in", gain_rows=gain)
                transpose_split(nc, k, k.acc, "xn")
                causal_operands(nc, k, wq, wkv, srow, nk, nb, m8, q_d, KT, V, side,
                                null[:].rearrange("p h t -> p t h"), copied)
            with ExitStack() as main:
                f = Scope(nc, main)
                o = f.sb("causal_o", [P, TT, QI], F32)
                causal_attention(nc, k, table_d, q_d, KT, V, side, null, a["cond_64"][1:2, :], o)
                causal_output(nc, k, o, wout, k.acc)
        end_of_part(nc)
        with ExitStack() as inner:
            g = Scope(nc, inner)
            w1 = g.sb("f_w1", [P, 2, KC, E, F], F16)
            w2 = g.sb("f_w2", [P, 2, E * FC, H], F16)
            wr = g.sb("f_wr", [P, 2, KC, E], F16)
            b1T = g.sb("f_b1T", [P, E * FC], F32)
            W = g.sb("f_W", [P, E, TT], F32)
            k.zT = g.sb("f_zT", [P, 2, KC, T], F16)
            jobs = []
            for kc in range(KC):
                for h in range(2):
                    es = slice(4 * h, 4 * h + 4)
                    jobs.append((a["L0_ffn_W1"][es, kc * P:(kc + 1) * P, :].rearrange("e p f -> p e f"),
                                 w1[:, HI, kc, es, :], w1[:, LO, kc, es, :]))
            for h in range(4):
                es = slice(8 * h, 8 * h + 8)
                jobs.append((a["L0_ffn_W2"].rearrange("e (c p) h -> p (e c) h", p=P)[:, es, :],
                             w2[:, HI, es, :], w2[:, LO, es, :]))
            jobs.append((a["L0_ffn_rW"].rearrange("(c p) e -> p c e", p=P), wr[:, HI], wr[:, LO]))
            layer_norm(nc, k.acc, k.acc, TT, a["L0_cond2_g_out"], None, "ln_out", jobs=jobs[0:4])
            add_rows(nc, k.acc, k.x)
            layer_norm(nc, k.acc, k.acc, TT, a["L0_ffn_ln_g"], a["L0_ffn_ln_b"], "ln_ffn", jobs=jobs[4:])
            transpose_split(nc, k, k.acc, "z")
            routing(nc, k, "gelu_router", wr, None, a["L0_ffn_rb"], 1.0, (1e-8, ALU.max), W)
            gelu_operands(nc, k, a["L0_ffn_b1"], a["L0_ffn_b2"], W, b1T, k.x)
            gelu_experts(nc, k, w1, w2, b1T, W, k.x)
        store_rows(nc, k.x, out)


def kernel(**inputs):
    import numpy as _np
    import concourse.bacc as _bacc
    from concourse import mybir as _mybir
    from concourse.bass_utils import run_bass_kernel_spmd as _run

    nc = _bacc.Bacc("TRN2", target_bir_lowering=False, num_devices=1)
    arrays, args = {}, {}
    for name, value in inputs.items():
        v = _np.ascontiguousarray(value)
        if v.dtype == _np.bool_:
            v = v.view(_np.uint8)
        arrays["in_" + name] = v
        args[name] = nc.dram_tensor("in_" + name, v.shape, _mybir.dt.from_np(v.dtype), kind="ExternalInput").ap()
    out = nc.dram_tensor("out", (B, S, H), F32, kind="ExternalOutput").ap()
    build(nc, args, out)
    r = _run(nc, [arrays], core_ids=[0])
    return r.results[0]["out"]
```
